# Optimizing a Trainium2 kernel written in Bass

```python
import numpy as np
import jax
import jax.numpy as jnp

def _softmax(x, axis=-1):
    return jax.nn.softmax(x, axis=axis)

def _gelu(x):
    return jax.nn.gelu(x, approximate=True)

def _silu(x):
    return jax.nn.silu(x)

def _sigmoid(x):
    return jax.nn.sigmoid(x)

def _layernorm(x, axis=-1, eps=1e-05):
    m = jnp.mean(x, axis=axis, keepdims=True)
    v = jnp.var(x, axis=axis, keepdims=True)
    return (x - m) / jnp.sqrt(v + eps)

def _scatter_add(tgt, idx, src, axis=0):
    return tgt.at[idx].add(src)

def _segment_sum(src, seg, n):
    return jax.ops.segment_sum(src, seg, n)
kernel_name = 'mk_gnn_preln_d2_gnn_r8_0325d6'

def setup_inputs(seed: int=0):
    np.random.seed(seed)
    _w = jnp.asarray

    def _rec_inputs():
        import jax
        import jax.numpy as jnp
        _gk = jax.random.key(seed)
        x = -0.0006008 + 1.001 * jax.random.normal(jax.random.fold_in(_gk, 1), (6250, 256), jnp.float32)
        src = jax.random.randint(jax.random.fold_in(_gk, 2), (100000,), 0, 6250, jnp.int32)
        dst = jnp.minimum((6250 * jax.random.uniform(jax.random.fold_in(_gk, 3), (100000,)) ** 2.0).astype(jnp.int32), 49999)
        _o = jnp.argsort(dst, stable=True)
        src = src[_o]
        dst = dst[_o]
        edge_type_2 = jax.random.randint(jax.random.fold_in(_gk, 12), (100000,), 0, 2, jnp.int32)
        edge_weight = jax.random.uniform(jax.random.fold_in(_gk, 13), (100000,), jnp.float32, 0.0, 0.999999)
        return (x, src, dst, edge_type_2, edge_weight)
    x, src, dst, edge_type_2, edge_weight = _rec_inputs()

    def _L0_gnn_setup():
        import jax, jax.numpy as jnp
        import numpy as np
        N = 1250
        E = 40000
        IN = 256
        H = 4
        C1 = 64
        C2 = 256

        def _segment_softmax(logits, seg, n):
            m = jax.lax.stop_gradient(jax.ops.segment_max(logits, seg, num_segments=n))
            e = jnp.exp(logits - m[seg])
            s = jax.ops.segment_sum(e, seg, num_segments=n)
            return e / (s[seg] + 1e-16)

        def _prelu(x, a):
            return jnp.where(x > 0, x, a * x)
        key = jax.random.key(seed)
        ks = jax.random.split(key, 12)
        g = lambda k, shp: jax.random.normal(k, shp, jnp.float32) * 0.05
        return {'x': jax.random.normal(ks[0], (N, IN), jnp.float32), 'edge_index': jax.random.randint(ks[1], (2, E), 0, N), 'gat_W': g(ks[2], (IN, H * C1)), 'att_src': g(ks[3], (H, C1)), 'att_dst': g(ks[4], (H, C1)), 'gat_bias': jnp.zeros((H * C1,), jnp.float32), 'prelu1_a': jnp.full((H * C1,), 0.25, jnp.float32), 'Wq': g(ks[5], (H * C1, C2)), 'bq': jnp.zeros((C2,), jnp.float32), 'Wk': g(ks[6], (H * C1, C2)), 'bk': jnp.zeros((C2,), jnp.float32), 'Wv': g(ks[7], (H * C1, C2)), 'bv': jnp.zeros((C2,), jnp.float32), 'Wskip': g(ks[8], (H * C1, C2)), 'bskip': jnp.zeros((C2,), jnp.float32), 'prelu2_a': jnp.full((C2,), 0.25, jnp.float32)}
    _L0_gnn_all = _L0_gnn_setup()
    _L0_gnn_in = {k: v for k, v in _L0_gnn_all.items() if k in ('gat_W', 'att_src', 'att_dst', 'gat_bias', 'prelu1_a', 'Wq', 'bq', 'Wk', 'bk', 'Wv', 'bv', 'Wskip', 'bskip', 'prelu2_a')}
    del _L0_gnn_all

    def _L1_gnn_setup():
        import jax, jax.numpy as jnp
        import numpy as np
        N, E = (6250, 100000)
        IN_CH, H, C = (256, 8, 32)
        HID = H * C
        T = 2
        FFN = 4 * HID
        EPS = 1e-05

        def _layernorm(h, g, b):
            mu = jnp.mean(h, axis=-1, keepdims=True)
            var = jnp.mean(jnp.square(h - mu), axis=-1, keepdims=True)
            return (h - mu) * jax.lax.rsqrt(var + EPS) * g + b

        def _gat_forward(x, edge_index, edge_type, edge_weight, W_src, W_dst, att_src, att_dst, bias, ln1_g, ln1_b, ln2_g, ln2_b, ffn_W1, ffn_b1, ffn_W2, ffn_b2):
            n = x.shape[0]
            loop = jnp.arange(n, dtype=edge_index.dtype)
            src = jnp.concatenate([edge_index[0], loop])
            dst = jnp.concatenate([edge_index[1], loop])
            etype = jnp.concatenate([edge_type, jnp.zeros((n,), edge_type.dtype)])
            ew = jnp.concatenate([edge_weight, jnp.ones((n,), edge_weight.dtype)])
            x_src = (x @ W_src.T).reshape(n, H, C)
            x_dst = (x @ W_dst.T).reshape(n, H, C)
            xs_j = x_src[src]
            xd_i = x_dst[dst]
            a_s = att_src[etype]
            a_d = att_dst[etype]
            alpha = jnp.sum(xs_j * a_s, axis=-1) + jnp.sum(xd_i * a_d, axis=-1)
            alpha = jnp.where(alpha >= 0, alpha, 0.2 * alpha)
            m = jax.lax.stop_gradient(jax.ops.segment_max(alpha, dst, num_segments=n))
            a = jnp.exp(alpha - m[dst])
            denom = jax.ops.segment_sum(a, dst, num_segments=n)
            a = a / denom[dst]
            a = a * ew[:, None]
            msg = xs_j * a[:, :, None]
            out = jax.ops.segment_sum(msg, dst, num_segments=n)
            out = out.reshape(n, H * C) + bias
            h = _layernorm(out + x, ln1_g, ln1_b)
            ff = jax.nn.gelu(h @ ffn_W1.T + ffn_b1, approximate=False) @ ffn_W2.T + ffn_b2
            return _layernorm(h + ff, ln2_g, ln2_b)
        key = jax.random.key(seed)
        ks = jax.random.split(key, 16)
        s_in = 1.0 / np.sqrt(IN_CH)
        s_h = 1.0 / np.sqrt(HID)
        return {'x': jax.random.normal(ks[0], (N, IN_CH), jnp.float32), 'edge_index': jax.random.randint(ks[1], (2, E), 0, N, jnp.int32), 'edge_type': jax.random.randint(ks[2], (E,), 0, T, jnp.int32), 'edge_weight': jax.random.uniform(ks[3], (E,), jnp.float32), 'W_src': jax.random.normal(ks[4], (H * C, IN_CH), jnp.float32) * s_in, 'W_dst': jax.random.normal(ks[5], (H * C, IN_CH), jnp.float32) * s_in, 'att_src': jax.random.normal(ks[6], (T, H, C), jnp.float32) * (1.0 / np.sqrt(C)), 'att_dst': jax.random.normal(ks[7], (T, H, C), jnp.float32) * (1.0 / np.sqrt(C)), 'bias': jnp.zeros((HID,), jnp.float32), 'ln1_g': jnp.ones((HID,), jnp.float32), 'ln1_b': jnp.zeros((HID,), jnp.float32), 'ln2_g': jnp.ones((HID,), jnp.float32), 'ln2_b': jnp.zeros((HID,), jnp.float32), 'ffn_W1': jax.random.normal(ks[8], (FFN, HID), jnp.float32) * s_h, 'ffn_b1': jnp.zeros((FFN,), jnp.float32), 'ffn_W2': jax.random.normal(ks[9], (HID, FFN), jnp.float32) * (1.0 / np.sqrt(FFN)), 'ffn_b2': jnp.zeros((HID,), jnp.float32)}
    _L1_gnn_all = _L1_gnn_setup()
    _L1_gnn_in = {k: v for k, v in _L1_gnn_all.items() if k in ('W_src', 'W_dst', 'att_src', 'att_dst', 'bias', 'ln1_g', 'ln1_b', 'ln2_g', 'ln2_b', 'ffn_W1', 'ffn_b1', 'ffn_W2', 'ffn_b2')}
    del _L1_gnn_all
    return {'x': x, 'src': src, 'dst': dst, 'edge_type_2': edge_type_2, 'edge_weight': edge_weight, 'L0_gnn_gat_W': _L0_gnn_in['gat_W'], 'L0_gnn_att_src': _L0_gnn_in['att_src'], 'L0_gnn_att_dst': _L0_gnn_in['att_dst'], 'L0_gnn_gat_bias': _L0_gnn_in['gat_bias'], 'L0_gnn_prelu1_a': _L0_gnn_in['prelu1_a'], 'L0_gnn_Wq': _L0_gnn_in['Wq'], 'L0_gnn_bq': _L0_gnn_in['bq'], 'L0_gnn_Wk': _L0_gnn_in['Wk'], 'L0_gnn_bk': _L0_gnn_in['bk'], 'L0_gnn_Wv': _L0_gnn_in['Wv'], 'L0_gnn_bv': _L0_gnn_in['bv'], 'L0_gnn_Wskip': _L0_gnn_in['Wskip'], 'L0_gnn_bskip': _L0_gnn_in['bskip'], 'L0_gnn_prelu2_a': _L0_gnn_in['prelu2_a'], 'L1_gnn_W_src': _L1_gnn_in['W_src'], 'L1_gnn_W_dst': _L1_gnn_in['W_dst'], 'L1_gnn_att_src': _L1_gnn_in['att_src'], 'L1_gnn_att_dst': _L1_gnn_in['att_dst'], 'L1_gnn_bias': _L1_gnn_in['bias'], 'L1_gnn_ln1_g': _L1_gnn_in['ln1_g'], 'L1_gnn_ln1_b': _L1_gnn_in['ln1_b'], 'L1_gnn_ln2_g': _L1_gnn_in['ln2_g'], 'L1_gnn_ln2_b': _L1_gnn_in['ln2_b'], 'L1_gnn_ffn_W1': _L1_gnn_in['ffn_W1'], 'L1_gnn_ffn_b1': _L1_gnn_in['ffn_b1'], 'L1_gnn_ffn_W2': _L1_gnn_in['ffn_W2'], 'L1_gnn_ffn_b2': _L1_gnn_in['ffn_b2']}

def reference(x, src, dst, edge_type_2, edge_weight, L0_gnn_gat_W, L0_gnn_att_src, L0_gnn_att_dst, L0_gnn_gat_bias, L0_gnn_prelu1_a, L0_gnn_Wq, L0_gnn_bq, L0_gnn_Wk, L0_gnn_bk, L0_gnn_Wv, L0_gnn_bv, L0_gnn_Wskip, L0_gnn_bskip, L0_gnn_prelu2_a, L1_gnn_W_src, L1_gnn_W_dst, L1_gnn_att_src, L1_gnn_att_dst, L1_gnn_bias, L1_gnn_ln1_g, L1_gnn_ln1_b, L1_gnn_ln2_g, L1_gnn_ln2_b, L1_gnn_ffn_W1, L1_gnn_ffn_b1, L1_gnn_ffn_W2, L1_gnn_ffn_b2):
    import jax
    import jax.numpy as jnp

    def _L0_gnn_ref(x, edge_index, gat_W, att_src, att_dst, gat_bias, prelu1_a, Wq, bq, Wk, bk, Wv, bv, Wskip, bskip, prelu2_a):
        import jax, jax.numpy as jnp
        import numpy as np
        N = 1250
        E = 40000
        IN = 256
        H = 4
        C1 = 64
        C2 = 256

        def _segment_softmax(logits, seg, n):
            m = jax.lax.stop_gradient(jax.ops.segment_max(logits, seg, num_segments=n))
            e = jnp.exp(logits - m[seg])
            s = jax.ops.segment_sum(e, seg, num_segments=n)
            return e / (s[seg] + 1e-16)

        def _prelu(x, a):
            return jnp.where(x > 0, x, a * x)
        n = x.shape[0]
        loops = jnp.arange(n)
        src = jnp.concatenate([edge_index[0], loops])
        dst = jnp.concatenate([edge_index[1], loops])
        h = (x @ gat_W).reshape(n, H, C1)
        a_src = jnp.einsum('nhc,hc->nh', h, att_src)
        a_dst = jnp.einsum('nhc,hc->nh', h, att_dst)
        logits = jax.nn.leaky_relu(a_src[src] + a_dst[dst], negative_slope=0.2)
        alpha = _segment_softmax(logits, dst, n)
        msg = h[src] * alpha[:, :, None]
        x1 = jax.ops.segment_sum(msg, dst, num_segments=n).reshape(n, H * C1) + gat_bias
        x1 = _prelu(x1, prelu1_a)
        q = x1 @ Wq + bq
        k = x1 @ Wk + bk
        v = x1 @ Wv + bv
        s2, d2 = (edge_index[0], edge_index[1])
        scale = 1.0 / jnp.sqrt(jnp.float32(C2))
        logits2 = jnp.einsum('ec,ec->e', q[d2], k[s2]) * scale
        alpha2 = _segment_softmax(logits2, d2, n)
        out = jax.ops.segment_sum(v[s2] * alpha2[:, None], d2, num_segments=n)
        out = out + x1 @ Wskip + bskip
        return _prelu(out, prelu2_a)

    def _L1_gnn_ref(x, edge_index, edge_type, edge_weight, W_src, W_dst, att_src, att_dst, bias, ln1_g, ln1_b, ln2_g, ln2_b, ffn_W1, ffn_b1, ffn_W2, ffn_b2):
        import jax, jax.numpy as jnp
        import numpy as np
        N, E = (6250, 100000)
        IN_CH, H, C = (256, 8, 32)
        HID = H * C
        T = 2
        FFN = 4 * HID
        EPS = 1e-05

        def _layernorm(h, g, b):
            mu = jnp.mean(h, axis=-1, keepdims=True)
            var = jnp.mean(jnp.square(h - mu), axis=-1, keepdims=True)
            return (h - mu) * jax.lax.rsqrt(var + EPS) * g + b

        def _gat_forward(x, edge_index, edge_type, edge_weight, W_src, W_dst, att_src, att_dst, bias, ln1_g, ln1_b, ln2_g, ln2_b, ffn_W1, ffn_b1, ffn_W2, ffn_b2):
            n = x.shape[0]
            loop = jnp.arange(n, dtype=edge_index.dtype)
            src = jnp.concatenate([edge_index[0], loop])
            dst = jnp.concatenate([edge_index[1], loop])
            etype = jnp.concatenate([edge_type, jnp.zeros((n,), edge_type.dtype)])
            ew = jnp.concatenate([edge_weight, jnp.ones((n,), edge_weight.dtype)])
            x_src = (x @ W_src.T).reshape(n, H, C)
            x_dst = (x @ W_dst.T).reshape(n, H, C)
            xs_j = x_src[src]
            xd_i = x_dst[dst]
            a_s = att_src[etype]
            a_d = att_dst[etype]
            alpha = jnp.sum(xs_j * a_s, axis=-1) + jnp.sum(xd_i * a_d, axis=-1)
            alpha = jnp.where(alpha >= 0, alpha, 0.2 * alpha)
            m = jax.lax.stop_gradient(jax.ops.segment_max(alpha, dst, num_segments=n))
            a = jnp.exp(alpha - m[dst])
            denom = jax.ops.segment_sum(a, dst, num_segments=n)
            a = a / denom[dst]
            a = a * ew[:, None]
            msg = xs_j * a[:, :, None]
            out = jax.ops.segment_sum(msg, dst, num_segments=n)
            out = out.reshape(n, H * C) + bias
            h = _layernorm(out + x, ln1_g, ln1_b)
            ff = jax.nn.gelu(h @ ffn_W1.T + ffn_b1, approximate=False) @ ffn_W2.T + ffn_b2
            return _layernorm(h + ff, ln2_g, ln2_b)
        return _gat_forward(x, edge_index, edge_type, edge_weight, W_src, W_dst, att_src, att_dst, bias, ln1_g, ln1_b, ln2_g, ln2_b, ffn_W1, ffn_b1, ffn_W2, ffn_b2)
    edge_index = jnp.stack([src, dst])
    h = jnp.maximum(_layernorm(x, axis=-1), 0.0)
    x = x + _L0_gnn_ref(h, edge_index, L0_gnn_gat_W, L0_gnn_att_src, L0_gnn_att_dst, L0_gnn_gat_bias, L0_gnn_prelu1_a, L0_gnn_Wq, L0_gnn_bq, L0_gnn_Wk, L0_gnn_bk, L0_gnn_Wv, L0_gnn_bv, L0_gnn_Wskip, L0_gnn_bskip, L0_gnn_prelu2_a)
    h = jnp.maximum(_layernorm(x, axis=-1), 0.0)
    x = x + _L1_gnn_ref(h, edge_index, edge_type_2, edge_weight, L1_gnn_W_src, L1_gnn_W_dst, L1_gnn_att_src, L1_gnn_att_dst, L1_gnn_bias, L1_gnn_ln1_g, L1_gnn_ln1_b, L1_gnn_ln2_g, L1_gnn_ln2_b, L1_gnn_ffn_W1, L1_gnn_ffn_b1, L1_gnn_ffn_W2, L1_gnn_ffn_b2)
    return x

_drawn_inputs = setup_inputs


def setup_inputs(seed=0):
    import zlib

    import numpy as np

    out = dict(_drawn_inputs(seed))
    spreads = {'L0_gnn_gat_bias': (0.0, 0.1),
     'L0_gnn_prelu1_a': (0.25, 0.6),
     'L0_gnn_bq': (0.0, 2.0),
     'L0_gnn_bk': (0.0, 2.0),
     'L0_gnn_bv': (0.0, 0.1),
     'L0_gnn_bskip': (0.0, 0.1),
     'L0_gnn_prelu2_a': (0.25, 0.6),
     'L1_gnn_bias': (0.0, 0.1),
     'L1_gnn_ln1_g': (1.0, 0.2),
     'L1_gnn_ln1_b': (0.0, 0.1),
     'L1_gnn_ln2_g': (1.0, 0.2),
     'L1_gnn_ln2_b': (0.0, 0.1),
     'L1_gnn_ffn_b1': (0.0, 0.271),
     'L1_gnn_ffn_b2': (0.0, 0.1)}
    factors = {'L0_gnn_att_src': 6.506, 'L0_gnn_att_dst': 8.0, 'L0_gnn_Wq': 8.0, 'L0_gnn_Wk': 8.0}
    for name, (base, spread) in spreads.items():
        noise = np.random.default_rng([zlib.crc32(name.encode()), seed]).standard_normal(out[name].shape)
        drawn = base * np.exp(spread * noise) if base else spread * noise
        out[name] = jnp.asarray(drawn.astype(out[name].dtype))
    for name, factor in factors.items():
        out[name] = (out[name] * factor).astype(out[name].dtype)
    return out
```

```python
import concourse.bass as bass
from concourse import mybir
from contextlib import ExitStack

F32 = mybir.dt.float32
I32 = mybir.dt.int32
BF16 = mybir.dt.bfloat16
ALU = mybir.AluOpType
ACT = mybir.ActivationFunctionType
DVE_ENGINE = mybir.EngineType.DVE
PE_ENGINE = mybir.EngineType.PE

P = 128
N = 6250
E = 100000
D = 256
NB = (N + P - 1) // P
NP = NB * P
NT = (E + P - 1) // P
PAD_NODE = NP - 1
G = 16
VISITS = NT + NB - 1
NBATCH = (VISITS + G - 1) // G
assert NBATCH % 2 == 0
VC = (NBATCH * G + P - 1) // P
NV = VC * P
HB = 8
BIG = 1e30
DST_SCALE = 1e30
FAR = 1000.0
H0, H2, FFN = 4, 8, 1024
W0 = D + 2 * H0
W1 = D + 4
W2 = D + 4 * H2
WA = D + 2 * H2
WQ = D + 2
EPS = 1e-5


class Sems:

    def __init__(self, nc, ctx, prefix):
        self.nc, self.prefix, self.made = nc, prefix, {}
        ctx.callback(self.clear)

    def __getitem__(self, name):
        if name not in self.made:
            self.made[name] = self.nc.alloc_semaphore(f"{self.prefix}_{name}")
        return self.made[name]

    def clear(self):
        self.nc.clear_and_free_semaphores(list(self.made.values()))
        self.nc.all_engine_barrier()


class Chain:

    def __init__(self, eng, sem):
        self.eng, self.sem, self.n = eng, sem, 0

    def step(self, ins):
        self.n += 1
        ins.then_inc(self.sem, 1)
        self.eng.wait_ge(self.sem, self.n)


def wait_apart(eng, sem, value, reg):
    if isinstance(value, int):
        eng.wait_ge(sem, value)
    else:
        eng.reg_mov(reg, value)
        eng.wait_ge(sem, 1)
        eng.wait_ge(sem, reg)


def spread(ap, n):
    return ap.unsqueeze(2).to_broadcast([ap.shape[0], ap.shape[1], n])


def constants(nc, m):
    with ExitStack() as ctx:
        S = Sems(nc, ctx, "const")
        block = ctx.enter_context(nc.Block())

        @block.gpsimd
        def _(pool):
            nc.gpsimd.iota(m.iota[:, :], [[1, P]], base=0, channel_multiplier=0,
                           allow_small_or_imprecise_dtypes=True).then_inc(S["iota"], 1)
            nc.gpsimd.iota(m.pcol[:, :], [[0, 1]], base=0, channel_multiplier=1,
                           allow_small_or_imprecise_dtypes=True).then_inc(S["iota"], 1)
            nc.gpsimd.iota(m.ints[:, 0:G], [[-1, G]], base=0, channel_multiplier=1).then_inc(S["iota"], 1)
            nc.gpsimd.iota(m.ints[:, G:G + HB], [[-G, HB]], base=0, channel_multiplier=1).then_inc(S["iota"], 1)
            nc.gpsimd.iota(m.ints_t[:, :], [[1, P]], base=0, channel_multiplier=-G).then_inc(S["iota"], 1)

        @block.vector
        def _(dve):
            c = Chain(dve, S["dve"])
            dve.wait_ge(S["iota"], 5)
            nc.vector.memset(m.half[:, :], -0.5)
            nc.vector.memset(m.ones[:, :], 1.0)
            nc.vector.memset(m.seg_bias[:, :, 0:1], -BIG)
            nc.vector.memset(m.seg_bias[:, :, P:P + 1], -BIG)
            nc.vector.memset(m.back_max[:, :, G:G + 1], -BIG)
            nc.vector.tensor_scalar(m.ident[:, :], m.iota[:, :], m.pcol[:, 0:1], None, ALU.is_equal)
            nc.vector.tensor_scalar(m.ints2[:, 0:G], m.ints[:, 0:G], G - 1, None, ALU.bitwise_and)
            nc.vector.tensor_scalar(m.ints2[:, G:G + HB], m.ints[:, G:G + HB], 4, None, ALU.arith_shift_right)
            c.step(nc.vector.tensor_scalar(m.ints_t2[:, :], m.ints_t[:, :], 4, None, ALU.arith_shift_right))
            nc.vector.tensor_scalar(m.visit_col[:, :], m.ints2[:, 0:G], 0, None, ALU.is_equal)
            nc.vector.tensor_scalar(m.head_rows[:, :], m.ints2[:, G:G + HB], 0, None, ALU.is_equal)
            c.step(nc.vector.tensor_scalar(m.head_rows_t[:, :], m.ints_t2[:, :], 0, None, ALU.is_equal))


def visits(nc, m, dram):
    with ExitStack() as ctx:
        S = Sems(nc, ctx, "meta")
        rec = m.arena[:, 0:4 * P].bitcast(I32)
        wrec = m.arena[:, 512:512 + P]
        dst_f, src_f, next_f, rel, et_f, last_f = (m.arena[:, 640 + P * i:640 + P * (i + 1)] for i in range(6))
        in_block, tmp, dst_s = (m.arena[:, 1408 + P * i:1408 + P * (i + 1)] for i in range(3))
        rel16 = m.arena[:, 1792:1856].bitcast(BF16)
        scal = m.arena[:, 1856:1860]
        last_dst = m.arena[:, 1860:1860 + VC].bitcast(I32)
        last_blk = m.arena[:, 1868:1868 + VC].bitcast(I32)
        v_end = m.arena[:, 1876:1876 + VC]
        v_idx = m.arena[:, 1884:1884 + VC]
        t_idx = m.arena[:, 1892:1892 + VC]
        blk = m.arena[:, 1900:1900 + VC]
        blk128 = m.arena[:, 1908:1908 + VC]
        tile_i = m.arena[:, 1916:1916 + VC].bitcast(I32)
        before = m.arena[:, 2048:2048 + NV // 2].bitcast(BF16)
        v_row = m.arena[:, 3072:3072 + NV]
        one16 = m.arena[:, 4096:4097].bitcast(BF16)
        rows = m.acc[0:1, 0:4 * NV].rearrange("p (a v) -> p a v", a=4)
        outs = m.acc[0:1, 4 * NV:10 * NV].rearrange("p (a v) -> p a v", a=6)
        both = m.acc[0:1, 10 * NV:11 * NV]
        ps = m.psum
        tables = [m.src_t, m.rel_t, m.last_t, m.type_t, m.weight_t]
        block = ctx.enter_context(nc.Block())

        @block.sync
        def _(sp):
            sp.wait_ge(S["preset"], 1)
            for c in range(VC):
                k = min(P, NT - c * P)
                if k > 0:
                    sp.dma_start(last_dst[0:k, c:c + 1], dram.edges[c * P:c * P + k, 2 * P - 1:2 * P], allow_slow_non_contiguous=True).then_inc(S["last_dst"], 16)
            for c in range(VC):
                sp.wait_ge(S["chunk"], c + 1)
                sp.dma_start(dram.rel16[c * P * P:(c + 1) * P * P].rearrange("(v e) -> v e", e=P), rel16).then_inc(S["stored"], 16)
                sp.dma_start(dram.scal[:, c * P:(c + 1) * P].rearrange("a v -> v a"), scal, allow_slow_non_contiguous=True).then_inc(S["stored"], 16)
                for h in range(HB):
                    sp.dma_start(dram.dst_s[c * (P // G):(c + 1) * (P // G), h, :, :], dst_s).then_inc(S["stored"], 16)
            sp.wait_ge(S["kept"], 1)
            for i, t in enumerate((m.last_t, m.type_t, m.type0_t, m.weight_t)):
                sp.dma_start(dram.kept[:, i, :], t[:, :]).then_inc(S["kept_stored"], 16)
            sp.wait_ge(S["kept_stored"], 64)
            sp.wait_ge(S["stored"], VC * 16 * (2 + HB))
            sp.dma_start(rows, dram.scal.rearrange("(p a) v -> p a v", p=1)).then_inc(S["rows"], 16)
            sp.wait_ge(S["outs"], 1)
            for a in range(6):
                sp.dma_start(dram.rows[:, a, :].rearrange("(p k) g -> p k g", p=1),
                             outs[:, a, :].rearrange("p (k g) -> p k g", g=G)).then_inc(S["end"], 16)
            sp.wait_ge(S["end"], 96)

        @block.gpsimd
        def _(pool):
            nc.gpsimd.iota(v_idx, [[P, VC]], base=0, channel_multiplier=1,
                           allow_small_or_imprecise_dtypes=True).then_inc(S["iota"], 1)
            nc.gpsimd.iota(v_row, [[1, NV]], base=0, channel_multiplier=0,
                           allow_small_or_imprecise_dtypes=True).then_inc(S["iota"], 1)
            pool.wait_ge(S["tiles"], 1)
            for c in range(VC):
                if c:
                    pool.wait_ge(S["chunk"], c)
                    pool.wait_ge(S["turned"], c)
                pool.indirect_dma_start(rec, None, dram.edges, bass.IndirectOffsetOnAxis(ap=tile_i[:, c:c + 1], axis=0)).then_inc(S["rec"], 16)
                pool.indirect_dma_start(wrec, None, dram.weights, bass.IndirectOffsetOnAxis(ap=tile_i[:, c:c + 1], axis=0)).then_inc(S["wrec"], 16)
                pool.wait_ge(S["rec"], 16 * (c + 1))
                pool.wait_ge(S["wrec"], 16 * (c + 1))

        @block.tensor
        def _(pe):
            for c in range(VC):
                pe.wait_ge(S["before"], c + 1)
                for q in range(VC):
                    last = nc.tensor.matmul(ps[:, c, q:q + 1], before[:, q * P:(q + 1) * P], one16[:, 0:1], start=True, stop=True)
                last.then_inc(S["counted"], 1)
            for c in range(VC):
                pe.wait_ge(S["chunk"], c + 1)
                pe.wait_ge(S["wrec"], 16 * (c + 1))
                pe.wait_ge(S["summed"], 1)
                if c:
                    pe.wait_ge(S["tables"], c)
                for i, a in enumerate([src_f, rel, last_f, et_f, wrec]):
                    last = nc.tensor.transpose(ps[:, i, 0:P], a, m.ident[:, :])
                last.then_inc(S["turned"], 1)

        @block.vector
        def _(dve):
            c_ = Chain(dve, S["dve"])
            nc.vector.memset(one16[:, 0:1], 1.0)
            nc.vector.memset(last_dst, 1 << 20).then_inc(S["preset"], 1)
            dve.wait_ge(S["iota"], 2)
            dve.wait_ge(S["last_dst"], 16 * sum(c * P < NT for c in range(VC)))
            c_.step(nc.vector.tensor_scalar(last_blk, last_dst, 7, None, ALU.arith_shift_right))
            c_.step(nc.vector.tensor_tensor(v_end, last_blk, v_idx, ALU.add))
            for c in range(VC):
                if c:
                    dve.wait_ge(S["counted"], c)
                nc.vector.tensor_scalar(before, v_row, v_end[:, c:c + 1], None, ALU.is_gt).then_inc(S["before"], 1)
            dve.wait_ge(S["counted"], VC)
            c_.step(nc.vector.tensor_copy(t_idx, ps[:, 0, 0:VC]))
            for c in range(1, VC):
                c_.step(nc.vector.tensor_tensor(t_idx, t_idx, ps[:, c, 0:VC], ALU.add))
            nc.vector.tensor_copy(tile_i, t_idx).then_inc(S["tiles"], 1)
            nc.vector.tensor_copy(blk128, t_idx).then_inc(S["summed"], 1)
            c_.step(nc.vector.tensor_tensor(blk, v_idx, t_idx, ALU.subtract))
            c_.step(nc.vector.tensor_scalar(blk, blk, float(NB - 1), None, ALU.min))
            dve.wait_ge(S["summed"], 1)
            c_.step(nc.vector.tensor_scalar(blk128, blk, float(P), None, ALU.mult))
            for c in range(VC):
                dve.wait_ge(S["rec"], 16 * (c + 1))
                if c:
                    dve.wait_ge(S["stored"], c * 16 * (2 + HB))
                    dve.wait_ge(S["turned"], c)
                nc.vector.tensor_copy(src_f, rec[:, 0:P])
                nc.vector.tensor_copy(dst_f, rec[:, P:2 * P])
                nc.vector.tensor_copy(next_f, rec[:, 2 * P:3 * P])
                c_.step(nc.vector.tensor_copy(et_f, rec[:, 3 * P:4 * P]))
                nc.vector.tensor_scalar(dst_s, dst_f, DST_SCALE, None, ALU.mult)
                nc.vector.tensor_tensor(last_f, dst_f, next_f, ALU.not_equal)
                nc.vector.tensor_copy(scal[:, 0:1], dst_f[:, 0:1])
                nc.vector.tensor_copy(scal[:, 1:2], dst_f[:, P - 1:P])
                nc.vector.tensor_copy(scal[:, 3:4], blk[:, c:c + 1])
                c_.step(nc.vector.tensor_scalar(tmp, dst_f, blk128[:, c:c + 1], None, ALU.subtract))
                c_.step(nc.vector.tensor_scalar(in_block, tmp, 0.0, None, ALU.is_ge))
                c_.step(nc.vector.scalar_tensor_tensor(in_block, tmp, float(P - 1), in_block, ALU.is_le, ALU.mult))
                c_.step(nc.vector.tensor_scalar(rel, tmp, -FAR, None, ALU.add))
                c_.step(nc.vector.tensor_tensor(rel, rel, in_block, ALU.mult))
                c_.step(nc.vector.tensor_scalar(rel, rel, FAR, None, ALU.add))
                c_.step(nc.vector.tensor_copy(rel16, rel))
                nc.vector.tensor_copy(scal[:, 2:3], rel[:, 0:1]).then_inc(S["chunk"], 1)
                dve.wait_ge(S["turned"], c + 1)
                for i, t in enumerate(tables):
                    last = nc.vector.tensor_copy(t[:, c * P:(c + 1) * P], ps[:, i, 0:P])
                last.then_inc(S["tables"], 1)
            dve.wait_ge(S["tables"], VC)
            nc.vector.tensor_scalar(m.mask_t[:, :], m.rel_t[:, :], FAR / 2, -BIG, ALU.is_gt, ALU.mult)
            nc.vector.tensor_scalar(m.type0_t[:, :], m.type_t[:, :], 0.0, None, ALU.is_equal).then_inc(S["kept"], 1)
            dve.wait_ge(S["rows"], 16)
            first, lastd, rel0, blkr = (rows[:, a, :] for a in range(4))
            same, cont = both, outs[:, 4, :]
            nc.vector.tensor_copy(m.blocks[:, :], blkr)
            nc.vector.tensor_copy(outs[:, 5, :], rel0)
            nc.vector.memset(cont[:, 0:1], 0.0)
            nc.vector.memset(outs[:, 1, NV - 1:NV], -BIG)
            nc.vector.memset(outs[:, 3, NV - 1:NV], -BIG)
            nc.vector.tensor_tensor(same, first, lastd, ALU.is_equal)
            c_.step(nc.vector.tensor_tensor(cont[:, 1:NV], first[:, 1:NV], lastd[:, 0:NV - 1], ALU.is_equal))
            nc.vector.tensor_tensor(outs[:, 0, :], same, cont, ALU.mult)
            nc.vector.tensor_tensor(outs[:, 1, 0:NV - 1], same[:, 0:NV - 1], cont[:, 1:NV], ALU.mult)
            nc.vector.tensor_scalar(outs[:, 2, :], cont, -1.0, BIG, ALU.add, ALU.mult)
            c_.step(nc.vector.tensor_scalar(outs[:, 3, 0:NV - 1], cont[:, 1:NV], -1.0, BIG, ALU.add, ALU.mult))
            nc.vector.tensor_scalar(outs[:, 0, :], outs[:, 0, :], -1.0, BIG, ALU.add, ALU.mult)
            nc.vector.tensor_scalar(outs[:, 1, 0:NV - 1], outs[:, 1, 0:NV - 1], -1.0, BIG, ALU.add, ALU.mult).then_inc(S["outs"], 1)


class Phase:

    def __init__(self, m, name, heads, table, width, summed, keys, slots):
        self.name, self.H, self.R = name, heads, heads * G
        self.table, self.W, self.WS = table, width, summed
        self.keys = keys
        self.dot = name == "attn"
        self.typed = name == "typed"
        self.X = m.arena[:, 0:2 * G * width].rearrange("p (a g w) -> p a g w", a=2, g=G)
        self.tab = m.tabs[:, 0:NB * 3 * keys].rearrange("p (b s k) -> p b s k", b=NB, s=3)
        self.at_logits, self.at_scan, self.at_join, self.at_max, self.at_shift = slots


def edge_pass(nc, m, dram, ph):
    H, R, X, K = ph.H, ph.R, ph.X, ph.keys
    ps = m.psum
    sum_ps = ps[:, 0:2, :]
    exp_ps = ps[:, 2:4, :]
    exp_all = ps[:, 2, 0:G * K].rearrange("p (g k) -> p g k", g=G) if not ph.dot else None
    logit_ps = ps[0:R, 4, 0:P]
    max_ps = ps[:, 5, 0:R]
    edge_ps = ps[0:H, 6, 0:2 * G].rearrange("p (a g) -> p a g", a=2)
    join_ps = ps[0:R, 6, 64:64 + 2 * G].rearrange("p (a g) -> p a g", a=2)
    grow_ps = ps[:, 7, 0:H]
    logit, shifted = m.logit[:, 0:R], m.shifted[:, 0:R]

    def by_head(ap):
        return ap.rearrange("p (h g) -> p h g", h=H)

    def by_visit(ap):
        return ap.rearrange("p (h g) -> p g h", h=H)

    with ExitStack() as ctx:
        S = Sems(nc, ctx, ph.name)
        block = ctx.enter_context(nc.Block())


        def steps(eng, chain, step):
            chain(0, 0)
            step(0, 0, True)
            step(1, 1, True)
            with eng.Fori(1, NBATCH // 2 - 1) as j:
                step(j * 2, 0, True)
                step(j * 2 + 1, 1, True)
            step(NBATCH - 2, 0, True)
            step(NBATCH - 1, 1, False)

        @block.sync
        def _(sp):
            def load(k, p, half):
                if not (isinstance(k, int) and k < 2):
                    sp.wait_ge(S["onehot_t"], k - 1)
                sp.dma_start(m.rel_row[:, p, :], dram.rel16[bass.ds(k * (G * P), G * P)].rearrange("(a n) -> a n", a=1).to_broadcast([P, G * P])).then_inc(S[f"rel{p}"], 16)
                if not (isinstance(k, int) and k < 2):
                    sp.wait_ge(S["joined"], k - 1)
                sp.dma_start(m.rows[0:H, p, :], dram.rows[bass.ds(k, 1), :, :].rearrange("k a g -> k (a g)").to_broadcast([H, 6 * G])).then_inc(S[f"rows{p}"], 16)
                if not (isinstance(k, int) and k < 2):
                    sp.wait_ge(S["maxes"], k - 1)
                sp.dma_start(m.dst_s[0:R, p, :], dram.dst_s[bass.ds(k, 1), 0:H, :, :].rearrange("k h g e -> (k h g) e")).then_inc(S[f"dst{p}"], 16)

            load(0, 0, 0)
            load(1, 1, 0)
            with sp.Fori(1, NBATCH // 2) as j:
                load(j * 2, 0, j)
                load(j * 2 + 1, 1, j)

        @block.gpsimd
        def _(pool):
            idle = pool.alloc_register(f"{ph.name}_idle")
            pool.reg_mov(idle, 0)

            def gather(k, p, uses):
                first = isinstance(k, int)
                if not first:
                    pool.wait_ge(S[f"gathered{p}"], uses * (16 * G))
                nc.gpsimd.tensor_copy(m.idx[:, p, :], m.src_t[:, bass.ds(k * G, G)]).then_inc(S["indices"], 1)
                pool.wait_ge(S["indices"], k + 1)
                for g in range(G):
                    if not first:
                        wait_apart(pool, S["summed"], (k - 2) * G + (g + 1), idle)
                    pool.indirect_dma_start(X[:, p, g, :], None, ph.table,
                                            bass.IndirectOffsetOnAxis(ap=m.idx[:, p, g:g + 1], axis=0)).then_inc(S[f"gathered{p}"], 16)

            gather(0, 0, 0)
            gather(1, 1, 0)
            with pool.Fori(1, NBATCH // 2) as j:
                gather(j * 2, 0, j)
                gather(j * 2 + 1, 1, j)

        @block.scalar
        def _(act):
            def weigh(k, p):
                act.wait_ge(S["grown"], k + 1)
                nc.scalar.activation(m.shrink[:, 0:H], grow_ps, ACT.Exp).then_inc(S["shrink"], 1)
                act.wait_ge(S["shifted"], k + 1)
                if ph.dot:
                    nc.scalar.activation(m.weight[:, p, 0:G], shifted, ACT.Exp).then_inc(S["weights"], 1)
                    act.wait_ge(S["weights"], k + 1)
                    nc.scalar.activation(m.neg_weight[:, p, 0:G], m.weight[:, p, 0:G], ACT.Copy, scale=-1.0).then_inc(S["neg"], 1)
                    act.wait_ge(S["neg"], k + 1)
                else:
                    nc.scalar.activation(X[:, p, :, D:D + H], by_visit(shifted), ACT.Exp).then_inc(S["weights"], 1)

            def distance(k, p, g):
                if not (isinstance(k, int) and k * G + g < 4):
                    act.wait_ge(S["onehot"], k * G + (g - 3))
                nc.scalar.activation(m.dist[:, g % 4, :], m.iota[:, :], ACT.Abs, scale=-1.0,
                                     bias=m.rel_t[:, bass.ds(k * G + g, 1)]).then_inc(S["distance"], 1)

            def step(k, p, more):
                distance(k, p, 0)
                for g in range(G):
                    if g + 1 < G:
                        distance(k, p, g + 1)
                    act.wait_ge(S["distance"], k * G + (g + 1))
                    if not (isinstance(k, int) and k * G + g < 4):
                        act.wait_ge(S["summed"], k * G + (g - 3))
                    if ph.dot:
                        nc.scalar.activation(m.onehot[:, g % 4, :], m.dist[:, g % 4, :], ACT.Relu,
                                             scale=m.neg_weight[:, p, g:g + 1], bias=m.weight[:, p, g:g + 1]).then_inc(S["onehot"], 1)
                    else:
                        nc.scalar.activation(m.onehot[:, g % 4, :], m.dist[:, g % 4, :], ACT.Relu,
                                             scale=-1.0, bias=m.ones[:, 0:1]).then_inc(S["onehot"], 1)
                if more:
                    weigh(k + 1, 1 - p)

            steps(act, weigh, step)

        @block.tensor
        def _(pe):
            idle = pe.alloc_register(f"{ph.name}_idle_pe")
            pe.reg_mov(idle, 0)

            def blocks_of(k):
                return nc.values_load_multi_w_load_instructions(
                    m.blocks[0:1, bass.ds(k * G, G)], engines=[PE_ENGINE], min_val=0, max_val=NB - 1)[1]

            def expand(k, p, g, blk):
                out = exp_ps[:, g % 2, 0:K] if ph.dot else exp_all[:, g, :]
                if g == 0:
                    pe.wait_ge(S["onehot_t"], k + 1)
                if ph.dot and not (isinstance(k, int) and k == 0 and g < 2):
                    pe.wait_ge(S["dotted"], k * G + (g - 1))
                for s in range(3):
                    last = nc.tensor.matmul(out, m.onehot_t[:, g, :], ph.tab[:, bass.ds(blk, 1), s, :].rearrange("p a k -> p (a k)"),
                                            start=(s == 0), stop=(s == 2))
                if ph.dot or g == G - 1:
                    last.then_inc(S["expanded"], 1)

            def turn_logits(k):
                wait_apart(pe, S["logits"], k + 1, idle)
                nc.tensor.transpose(logit_ps, logit, m.ident[:, :]).then_inc(S["turned"], 1)

            def edge_values(k):
                wait_apart(pe, S["scanned"], k + 1, idle)
                nc.tensor.matmul(edge_ps, m.head_rows[0:R, 0:H], m.ends[0:R, :, :], start=True, stop=True).then_inc(S["ends"], 1)

            def spread_joined(k):
                wait_apart(pe, S["joined"], k + 1, idle)
                nc.tensor.matmul(join_ps, m.head_rows_t[0:H, 0:R], m.joined[0:H, :, :], start=True, stop=True).then_inc(S["spread"], 1)
                nc.tensor.matmul(grow_ps, m.first_hot[0:H, :], m.growth[0:H, 0:H], start=True, stop=True).then_inc(S["grown"], 1)

            def turn_max(k):
                wait_apart(pe, S["maxes"], k + 1, idle)
                nc.tensor.transpose(max_ps, m.seg_max[0:R, 2, :], m.ident[0:R, 0:R]).then_inc(S["max_turned"], 1)

            def chain(k, p):
                blks = blocks_of(k)
                for g in range(G):
                    expand(k, p, g, blks[g])
                turn_logits(k)
                edge_values(k)
                spread_joined(k)
                turn_max(k)

            def step(k, p, more):
                blks = blocks_of(k + 1) if more else None
                for g in range(G):
                    if more:
                        for i in (range(2 * g, 2 * g + 2) if ph.dot else range(4 * g - 4, 4 * g)):
                            if 0 <= i < G:
                                expand(k + 1, 1 - p, i, blks[i])
                    pe.wait_ge(S["onehot"], k * G + (g + 1))
                    if not ph.dot:
                        pe.wait_ge(S["scaled"], k * G + (g + 1))
                    if not (isinstance(k, int) and k * G + g < 2):
                        pe.wait_ge(S["added"], k * G + (g - 1))
                    nc.tensor.matmul(sum_ps[:, g % 2, 0:ph.WS], m.onehot[:, g % 4, :], X[:, p, g, 0:ph.WS],
                                     start=True, stop=True).then_inc(S["summed"], 1)
                    if more:
                        if g == ph.at_logits:
                            turn_logits(k + 1)
                        if g == ph.at_scan:
                            edge_values(k + 1)
                        if g == ph.at_join:
                            spread_joined(k + 1)
                        if g == ph.at_max:
                            turn_max(k + 1)

            steps(pe, chain, step)

        @block.vector
        def _(dve):
            own = S["dve"]
            PER_BATCH = {"gat": 16, "attn": 13, "typed": 19}[ph.name]
            count = {}

            def then(k, ins):
                count["n"] += 1
                ins.then_inc(own, 1)
                return count["n"]

            def wait(k, n):
                dve.wait_ge(own, k * PER_BATCH + n)

            def transposed_onehot(k, p, j):
                count["n"] = 0
                dve.wait_ge(S[f"rel{p}"], (j + 1) * 16)
                nc.vector.tensor_scalar(m.onehot_t[:, :, :].rearrange("p g e -> p (g e)"), m.rel_row[:, p, :],
                                        m.pcol[:, 0:1], None, ALU.is_equal).then_inc(S["onehot_t"], 1)
                if ph.dot:
                    dve.wait_ge(S[f"gathered{p}"], (j + 1) * (16 * G))

            def dot(k, p, g):
                dve.wait_ge(S["expanded"], k * G + (g + 1))
                nc.vector.tensor_tensor_reduce(out=m.junk[:, g % 2, 0:K], in0=exp_ps[:, g % 2, 0:K], in1=X[:, p, g, 0:K], scale=1.0,
                                               scalar=0.0, op0=ALU.mult, op1=ALU.add,
                                               accum_out=m.raw[:, g:g + 1]).then_inc(S["dotted"], 1)

            def logits(k, p, j):
                cols = bass.ds(k * G, G)
                mask = m.mask_t[:, cols].unsqueeze(1).to_broadcast([P, H, G])
                if ph.dot:
                    dve.wait_ge(S["dotted"], (k + 1) * G)
                    nc.vector.tensor_tensor(logit, m.raw[:, 0:G], m.mask_t[:, cols], ALU.add).then_inc(S["logits"], 1)
                    return
                dve.wait_ge(S["expanded"], k + 1)
                dve.wait_ge(S[f"gathered{p}"], (j + 1) * (16 * G))
                if ph.typed:
                    both = m.both
                    n = then(k, nc.vector.tensor_tensor(both[:, :, :], X[:, p, :, D:D + 2 * H], exp_all, ALU.add))
                    wait(k, n)
                    a = nc.vector.tensor_tensor(both[:, :, 0:H], both[:, :, 0:H], spread(m.type0_t[:, cols], H), ALU.mult)
                    then(k, a)
                    n = then(k, nc.vector.tensor_tensor(both[:, :, H:2 * H], both[:, :, H:2 * H], spread(m.type_t[:, cols], H), ALU.mult))
                    wait(k, n)
                    n = then(k, nc.vector.tensor_tensor(by_visit(m.raw[:, 0:R]), both[:, :, 0:H], both[:, :, H:2 * H], ALU.add))
                else:
                    n = then(k, nc.vector.tensor_tensor(by_visit(m.raw[:, 0:R]), X[:, p, :, D:D + H], exp_all, ALU.add))
                wait(k, n)
                n = then(k, nc.vector.scalar_tensor_tensor(m.raw[:, 0:R], m.raw[:, 0:R], 0.2, m.raw[:, 0:R], ALU.mult, ALU.max))
                wait(k, n)
                nc.vector.tensor_tensor(by_head(logit), by_head(m.raw[:, 0:R]), mask, ALU.add).then_inc(S["logits"], 1)

            def scan(k, p, j):
                dve.wait_ge(S[f"dst{p}"], (j + 1) * 16)
                dst, bias = m.dst_s[0:R, p, :], m.seg_bias[0:R, 0, :]
                ahead, local = m.seg_max[0:R, 0, :], m.seg_max[0:R, 1, :]
                n = then(k, nc.vector.tensor_tensor(bias[:, 1:P], dst[:, 0:P - 1], dst[:, 1:P], ALU.subtract))
                dve.wait_ge(S["turned"], k + 1)
                wait(k, n)
                n = then(k, nc.vector.tensor_tensor_scan(ahead, bias[:, 0:P], logit_ps, -BIG, ALU.add, ALU.max))
                wait(k, n)
                n = then(k, nc.vector.tensor_tensor_scan(local[:, ::-1], bias[:, 1:P + 1][:, ::-1], ahead[:, ::-1], -BIG, ALU.add, ALU.max))
                wait(k, n)
                nc.vector.tensor_scalar(m.ends[0:R, 0, :], m.visit_col[0:R, :], local[:, 0:1], None, ALU.mult).then_inc(S["scanned_a"], 1)
                nc.vector.tensor_scalar(m.ends[0:R, 1, :], m.visit_col[0:R, :], local[:, P - 1:P], None, ALU.mult).then_inc(S["scanned"], 1)

            def join(k, p, j):
                dve.wait_ge(S[f"rows{p}"], (j + 1) * 16)
                dve.wait_ge(S["ends"], k + 1)
                row = m.rows[0:H, p, :].rearrange("h (a g) -> h a g", a=6)
                fore, back, tot, t = m.fore_max[0:H, p, :], m.back_max[0:H, 0, :], m.joined[0:H, :, :], m.join_tmp[0:H, :, :]
                then(k, nc.vector.tensor_tensor_scan(fore[:, 1:G + 1], row[:, 0, :], edge_ps[:, 1, :], fore[:, 0:1], ALU.add, ALU.max))
                n = then(k, nc.vector.tensor_tensor_scan(back[:, 0:G][:, ::-1], row[:, 1, :][:, ::-1], edge_ps[:, 0, :][:, ::-1], -BIG, ALU.add, ALU.max))
                nc.vector.tensor_scalar(m.first_hot[0:H, :], m.iota[0:H, :], row[:, 5, 0:1], None, ALU.is_equal).then_inc(S["first_hot"], 1)
                wait(k, n)
                then(k, nc.vector.tensor_tensor(t[:, 0, :], fore[:, 0:G], row[:, 2, :], ALU.add))
                n = then(k, nc.vector.tensor_tensor(t[:, 1, :], back[:, 1:G + 1], row[:, 3, :], ALU.add))
                wait(k, n)
                then(k, nc.vector.tensor_tensor(tot[:, 0, :], t[:, 0, :], back[:, 0:G], ALU.max))
                n = then(k, nc.vector.tensor_tensor(tot[:, 1, :], t[:, 1, :], fore[:, 1:G + 1], ALU.max))
                wait(k, n)
                then(k, nc.vector.tensor_copy(m.fore_max[0:H, 1 - p, 0:1], tot[:, 1, G - 1:G]))
                n = then(k, nc.vector.tensor_tensor(m.join_tmp[0:H, 2, 0:1], fore[:, 0:1], tot[:, 0, 0:1], ALU.subtract))
                wait(k, n)
                nc.vector.tensor_scalar(m.growth[0:H, 0:H], m.ident[0:H, 0:H], m.join_tmp[0:H, 2, 0:1], row[:, 4, 0:1],
                                        ALU.mult, ALU.mult).then_inc(S["joined"], 1)

            def maxes(k, p, j):
                dve.wait_ge(S["spread"], k + 1)
                dst = m.dst_s[0:R, p, :]
                local = m.seg_max[0:R, 1, :]
                first_b, last_b, tmp = m.seg_tmp[0:R, 0, :], m.seg_tmp[0:R, 1, :], m.seg_tmp[0:R, 2, :]
                for i in range(2):
                    then(k, nc.vector.tensor_tensor_reduce(out=m.junk[0:R, i, 0:G], in0=join_ps[:, i, :], in1=m.visit_col[0:R, :], scale=1.0,
                                                           scalar=0.0, op0=ALU.mult, op1=ALU.add, accum_out=m.end_max[0:R, i:i + 1]))
                nc.vector.tensor_scalar(first_b, dst, -1.0, dst[:, 0:1], ALU.mult, ALU.add)
                nc.vector.tensor_scalar(last_b, dst, dst[:, P - 1:P], None, ALU.subtract).then_inc(S["end_bias"], 1)
                dve.wait_ge(S["end_bias"], k + 1)
                nc.vector.scalar_tensor_tensor(tmp, first_b, m.end_max[0:R, 0:1], local, ALU.add, ALU.max).then_inc(S["max_a"], 1)
                dve.wait_ge(S["max_a"], k + 1)
                nc.vector.scalar_tensor_tensor(m.seg_max[0:R, 2, :], last_b, m.end_max[0:R, 1:2], tmp, ALU.add, ALU.max).then_inc(S["maxes"], 1)

            def shift(k, p, j):
                dve.wait_ge(S["max_turned"], k + 1)
                if not ph.dot:
                    last = m.last_t[:, bass.ds(k * G, G)]
                    then(k, nc.vector.tensor_tensor(X[:, p, :, D + H:D + 2 * H], by_visit(max_ps), spread(last, H), ALU.mult))
                nc.vector.tensor_tensor(shifted, logit, max_ps, ALU.subtract).then_inc(S["shifted"], 1)

            def add(k, p, g, blk):
                dve.wait_ge(S["summed"], k * G + (g + 1))
                if not (isinstance(k, int) and k * G + g == 0):
                    dve.wait_ge(S["added"], k * G + g)
                if g == 0:
                    dve.wait_ge(S["rescaled"], (k + 1) * (2 if not ph.dot else 1))
                row = m.acc[:, bass.ds(blk * WA, ph.WS)]
                nc.vector.tensor_tensor(row, row, sum_ps[:, g % 2, 0:ph.WS], ALU.add).then_inc(S["added"], 1)

            def rescale(k, p, blk):
                dve.wait_ge(S["shrink"], k + 1)
                if not (isinstance(k, int) and k == 0):
                    dve.wait_ge(S["added"], k * G)
                if ph.dot:
                    row = m.acc[:, bass.ds(blk * WA, ph.WS)]
                    nc.vector.tensor_scalar(row, row, m.shrink[:, 0:1], None, ALU.mult).then_inc(S["rescaled"], 1)
                    return
                row = m.acc[:, bass.ds(blk * WA, D)].rearrange("p (h c) -> p h c", h=H)
                den = m.acc[:, bass.ds(blk * WA + D, H)]
                nc.vector.tensor_tensor(row, row, spread(m.shrink[:, 0:H], D // H), ALU.mult).then_inc(S["rescaled"], 1)
                nc.vector.tensor_tensor(den, den, m.shrink[:, 0:H], ALU.mult).then_inc(S["rescaled"], 1)

            def scale_rows(k, p, g):
                if g == 0:
                    dve.wait_ge(S["weights"], k + 1)
                    if ph.typed:
                        nc.vector.tensor_tensor(m.edge_scale[:, :, 0:H], X[:, p, :, D:D + H], spread(m.weight_t[:, bass.ds(k * G, G)], H),
                                                ALU.mult).then_inc(S["edge_scale"], 1)
                        dve.wait_ge(S["edge_scale"], k + 1)
                row = X[:, p, g, 0:D].rearrange("p (h c) -> p h c", h=H)
                w = m.edge_scale[:, g, 0:H] if ph.typed else X[:, p, g, D:D + H]
                nc.vector.tensor_tensor(row, row, spread(w, D // H), ALU.mult).then_inc(S["scaled"], 1)

            def chain(k, p):
                transposed_onehot(k, p, 0)
                if ph.dot:
                    for g in range(G):
                        dot(k, p, g)
                for part in (logits, scan, join, maxes, shift):
                    part(k, p, 0)
                assert count["n"] == PER_BATCH, count

            def step(k, p, more):
                blks = nc.values_load_multi_w_load_instructions(
                    m.blocks[0:1, bass.ds(k * G, G)], engines=[DVE_ENGINE], min_val=0, max_val=NB - 1)[1]
                j = (k + 1) // 2
                rescale(k, p, blks[0])
                for g in range(G):
                    if not ph.dot:
                        scale_rows(k, p, g)
                    if g:
                        add(k, p, g - 1, blks[g - 1])
                    if more:
                        if g == 0:
                            transposed_onehot(k + 1, 1 - p, j)
                        if ph.dot and g < G // 2:
                            dot(k + 1, 1 - p, 2 * g)
                            dot(k + 1, 1 - p, 2 * g + 1)
                        for at, part in ((ph.at_logits, logits), (ph.at_scan, scan), (ph.at_join, join),
                                         (ph.at_max, maxes), (ph.at_shift, shift)):
                            if g == at:
                                part(k + 1, 1 - p, j)
                if more:
                    assert count["n"] == PER_BATCH, count
                add(k, p, G - 1, blks[G - 1])

            nc.vector.memset(m.acc[:, :], 0.0).then_inc(S["cleared"], 1)
            nc.vector.memset(m.fore_max[:, 0, 0:1], -BIG).then_inc(S["cleared"], 1)
            dve.wait_ge(S["cleared"], 2)
            steps(dve, chain, step)


class Space:

    def __init__(self, tensor, at=0):
        self.tensor, self.at = tensor, at

    def take(self, *shape):
        n = 1
        for s in shape:
            n *= s
        ap = self.tensor[:, self.at:self.at + n]
        self.at += n
        assert self.at <= self.tensor.shape[1], self.at
        if len(shape) == 2:
            ap = ap.rearrange("p (a b) -> p a b", a=shape[0])
        if len(shape) == 3:
            ap = ap.rearrange("p (a b c) -> p a b c", a=shape[0], b=shape[1])
        return ap


def node_blocks(eng, *stages):
    lag = len(stages) - 1
    start = lag + 1 if lag % 2 == 0 else lag + 2
    assert (NB - start) % 2 == 0

    def turn(i, p):
        for s, stage in reversed(list(enumerate(stages))):
            b = i - s
            if stage is not None and (not isinstance(b, int) or 0 <= b < NB):
                stage(b, (p - s) % 2)

    for i in range(start):
        turn(i, i % 2)
    with eng.Fori(0, (NB - start) // 2) as j:
        turn(j * 2 + start, start % 2)
        turn(j * 2 + (start + 1), (start + 1) % 2)
    for i in range(NB, NB + lag):
        turn(i, i % 2)


def landed(eng, sem, b, p):
    eng.wait_ge(sem, (b - p) * 8 + 16)


def vacated(eng, sem, b, p):
    if not (isinstance(b, int) and b < 2):
        eng.wait_ge(sem, (b - p) * 8)


def use(eng, sem, b, ahead=0):
    if isinstance(b, int):
        if b - ahead >= 0:
            eng.wait_ge(sem, b - ahead + 1)
    else:
        eng.wait_ge(sem, b + (1 - ahead))


def as_row(v, n=P):
    return v.rearrange("(a n) -> a n", a=1).to_broadcast([n, v.shape[0]])


def rows_of(t, b, width=None):
    return t[bass.ds(b * P, P), 0:(width or t.shape[1])]


def head_mask_into(nc, m, chain, mask, C, heads):
    shift = {64: 6, 32: 5}[C]
    a = m.head_int[:, 0:2 * heads].rearrange("p (c h) -> p c h", c=2)
    chain.step(nc.vector.tensor_scalar(a, a, shift, None, ALU.arith_shift_right))
    chain.step(nc.vector.tensor_scalar(mask, a, 0, None, ALU.is_equal))


def split3(nc, dve, S, tab, value, rest, b, p, tag):
    nc.vector.tensor_copy(tab(0), value).then_inc(S[tag + "_hi"], 1)
    use(dve, S[tag + "_hi"], b)
    nc.vector.tensor_tensor(rest[:, 0], value, tab(0), ALU.subtract).then_inc(S[tag + "_r1"], 1)
    use(dve, S[tag + "_r1"], b)
    nc.vector.tensor_copy(tab(1), rest[:, 0]).then_inc(S[tag + "_mid"], 1)
    use(dve, S[tag + "_mid"], b)
    nc.vector.tensor_tensor(tab(2), rest[:, 0], tab(1), ALU.subtract).then_inc(S[tag + "_lo"], 1)


def prepare_gat(nc, m, args, sp_):
    w = sp_.take(2, W0)
    raw = sp_.take(2, D)
    turned = sp_.take(2, D)
    att = sp_.take(2, 2)
    mask = sp_.take(2, H0)
    att_m = sp_.take(2, 2 * H0)
    ps = m.psum
    with ExitStack() as ctx:
        S = Sems(nc, ctx, "pgat")
        block = ctx.enter_context(nc.Block())

        @block.sync
        def _(sp):
            sp.dma_start(raw, args.gat_W.rearrange("(c p) n -> p c n", p=P)).then_inc(S["load"], 16)
            for i, a in enumerate((args.att_src0, args.att_dst0)):
                sp.dma_start(att[:, :, i], a.rearrange("h k -> (h k)").rearrange("(c p) -> p c", p=P), allow_slow_non_contiguous=True).then_inc(S["load"], 16)
            sp.wait_ge(S["load"], 48)

        @block.gpsimd
        def _(pool):
            nc.gpsimd.iota(m.head_int[:, 0:2 * H0], [[P, 2], [-64, H0]], base=0, channel_multiplier=1).then_inc(S["iota"], 1)

        @block.tensor
        def _(pe):
            pe.wait_ge(S["load"], 48)
            for kc in range(2):
                for cc in range(2):
                    last = nc.tensor.transpose(ps[:, cc, kc * P:(kc + 1) * P], raw[:, kc, cc * P:(cc + 1) * P], m.ident[:, :])
            last.then_inc(S["turned"], 1)
            pe.wait_ge(S["masked"], 1)
            for kc in range(2):
                for cc in range(2):
                    last = nc.tensor.matmul(ps[:, 2, kc * 8:kc * 8 + 8], turned[:, cc, kc * P:(kc + 1) * P], att_m[:, cc, :], start=(cc == 0), stop=(cc == 1))
            last.then_inc(S["logit_w"], 1)

        @block.vector
        def _(dve):
            c = Chain(dve, S["dve"])
            dve.wait_ge(S["iota"], 1)
            head_mask_into(nc, m, c, mask, 64, H0)
            dve.wait_ge(S["load"], 48)
            dve.wait_ge(S["turned"], 1)
            nc.vector.tensor_copy(turned, ps[:, 0:2, 0:D])
            nc.vector.tensor_copy(w[:, :, 0:D], raw)
            for i in range(2):
                for cc in range(2):
                    last = nc.vector.tensor_scalar(att_m[:, cc, i * H0:(i + 1) * H0], mask[:, cc, :], att[:, cc, i:i + 1], None, ALU.mult)
            last.then_inc(S["masked"], 1)
            dve.wait_ge(S["logit_w"], 1)
            nc.vector.tensor_copy(w[:, :, D:W0], ps[:, 2, 0:16].rearrange("p (k j) -> p k j", k=2)).then_inc(S["done"], 1)
    return w


def layernorm_stats(nc, dve, S, x, st, b, idle, tag="ln"):
    nc.vector.bn_stats(st[:, 0:6], x).then_inc(S[tag + "_stats"], 1)
    wait_apart(dve, S[tag + "_stats"], b + 1, idle)
    nc.vector.bn_aggr(st[:, 6:8], st[:, 0:6]).then_inc(S[tag + "_aggr"], 1)
    use(dve, S[tag + "_aggr"], b)
    nc.vector.tensor_scalar(st[:, 8:9], st[:, 7:8], EPS, None, ALU.add).then_inc(S[tag + "_var"], 1)


def inverse_root(nc, pool, S, m, st, b, tag="ln"):
    use(pool, S[tag + "_var"], b)
    nc.gpsimd.tensor_tensor(st[:, 9:10], st[:, 8:9], m.half[:, :], ALU.pow).then_inc(S[tag + "_rstd"], 1)


def nodes_in(nc, m, args, dram, w, sp_):
    x, h, hT, row, st, rest = sp_.take(2, D), sp_.take(2, D), sp_.take(2, D), sp_.take(2, W0), sp_.take(2, 10), sp_.take(2, H0)
    tab = m.tabs[:, 0:NB * 3 * H0].rearrange("p (b s k) -> p b s k", b=NB, s=3)
    ps = m.psum
    with ExitStack() as ctx:
        S = Sems(nc, ctx, "in")
        block = ctx.enter_context(nc.Block())

        @block.sync
        def _(sp):
            def load(b, p):
                use(sp, S["hn"], b, 2)
                sp.dma_start(x[:, p, :], rows_of(args.x, b)).then_inc(S[f"x{p}"], 16)

            node_blocks(sp, load)

        @block.scalar
        def _(act):
            def first(b, p):
                use(act, S["hn"], b)
                use(act, S["turned"], b, 2)
                nc.scalar.activation(h[:, p, :], h[:, p, :], ACT.Relu).then_inc(S["h"], 1)

            def second(b, p):
                use(act, S["turned"], b)
                use(act, S["mm"], b, 2)
                nc.scalar.activation(hT[:, p, :], ps[:, p, 0:D], ACT.Copy).then_inc(S["hT"], 1)
                use(act, S["row"], b)
                act.dma_start(rows_of(dram.t0, b), row[:, p, :]).then_inc(S[f"stored{p}"], 16)

            node_blocks(act, first, second)
            act.wait_ge(S["stored0"], 16 * (NB - NB // 2))
            act.wait_ge(S["stored1"], 16 * (NB // 2))

        @block.gpsimd
        def _(pool):
            def rstd(b, p):
                inverse_root(nc, pool, S, m, st[:, p, :], b)

            node_blocks(pool, rstd)

        @block.tensor
        def _(pe):
            def turn(b, p):
                use(pe, S["h"], b)
                use(pe, S["hT"], b, 2)
                for c in range(2):
                    last = nc.tensor.transpose(ps[:, p, c * P:(c + 1) * P], h[:, p, c * P:(c + 1) * P], m.ident[:, :])
                last.then_inc(S["turned"], 1)

            def project(b, p):
                use(pe, S["hT"], b)
                use(pe, S["row"], b, 2)
                for c in range(2):
                    last = nc.tensor.matmul(ps[:, 2 + p, 0:W0], hT[:, p, c * P:(c + 1) * P], w[:, c, :], start=(c == 0), stop=(c == 1))
                last.then_inc(S["mm"], 1)

            node_blocks(pe, turn, project)

        @block.vector
        def _(dve):
            idle = dve.alloc_register("in_idle")
            dve.reg_mov(idle, 0)

            def normalize(b, p):
                landed(dve, S[f"x{p}"], b, p)
                layernorm_stats(nc, dve, S, x[:, p, :], st[:, p, :], b, idle)
                use(dve, S["ln_rstd"], b)
                use(dve, S["turned"], b, 2)
                nc.vector.tensor_scalar(h[:, p, :], x[:, p, :], st[:, p, 6:7], st[:, p, 9:10], ALU.subtract, ALU.mult).then_inc(S["hn"], 1)

            def finish(b, p):
                use(dve, S["mm"], b)
                vacated(dve, S[f"stored{p}"], b, p)
                nc.vector.tensor_copy(row[:, p, :], ps[:, 2 + p, 0:W0]).then_inc(S["row"], 1)
                use(dve, S["row"], b)
                a = row[:, p, D + H0:W0]
                nc.vector.tensor_copy(m.self_logit[:, bass.ds(b, 1), 0:2 * H0], row[:, p, D:W0].unsqueeze(1)).then_inc(S["self"], 1)
                split3(nc, dve, S, lambda s: tab[:, bass.ds(b, 1), s, :].rearrange("p a k -> p (a k)"), a, rest[:, p:p + 1, :], b, p, "ad")

            node_blocks(dve, normalize, finish)


def acc_rows(m, b, at, n):
    return m.acc[:, bass.ds(b * WA + at, n)]


def by_heads(ap, H):
    return ap.rearrange("p (h c) -> p h c", h=H)


def one(ap):
    return ap.rearrange("p a k -> p (a k)")


def head_factors(nc, m, dram, H, src_at, dst_at, eps, sp_, name):
    keep, own = sp_.take(NB, H), sp_.take(NB, H)
    t = [sp_.take(NB, H) for _ in range(5)]
    acc = m.acc[:, :].rearrange("p (b w) -> p b w", b=NB)
    den, top = acc[:, :, D:D + H], acc[:, :, D + H:D + 2 * H]
    src, dst = m.self_logit[:, :, src_at:src_at + H], m.self_logit[:, :, dst_at:dst_at + H]
    with ExitStack() as ctx:
        S = Sems(nc, ctx, name)
        block = ctx.enter_context(nc.Block())

        @block.scalar
        def _(act):
            act.wait_ge(S["shifted"], 2)
            nc.scalar.activation(t[3], t[1], ACT.Exp).then_inc(S["exp"], 1)
            nc.scalar.activation(t[4], t[2], ACT.Exp).then_inc(S["exp"], 1)

        @block.vector
        def _(dve):
            c = Chain(dve, S["dve"])
            c.step(nc.vector.tensor_tensor(t[0], src, dst, ALU.add))
            c.step(nc.vector.scalar_tensor_tensor(t[0], t[0], 0.2, t[0], ALU.mult, ALU.max))
            c.step(nc.vector.tensor_scalar(t[1], den, 0.5, None, ALU.is_lt))
            c.step(nc.vector.scalar_tensor_tensor(t[1], t[1], -BIG, top, ALU.mult, ALU.add))
            c.step(nc.vector.tensor_tensor(t[2], t[0], t[1], ALU.max))
            nc.vector.tensor_tensor(t[1], t[1], t[2], ALU.subtract).then_inc(S["shifted"], 1)
            dve.wait_ge(S["shifted"], 1)
            nc.vector.tensor_tensor(t[2], t[0], t[2], ALU.subtract).then_inc(S["shifted"], 1)
            dve.wait_ge(S["exp"], 2)
            c.step(nc.vector.tensor_tensor(t[0], den, t[3], ALU.mult))
            c.step(nc.vector.tensor_tensor(t[0], t[0], t[4], ALU.add))
            c.step(nc.vector.tensor_scalar(t[0], t[0], eps, None, ALU.add))
            c.step(nc.vector.reciprocal(t[0], t[0]))
            nc.vector.tensor_tensor(keep, t[3], t[0], ALU.mult)
            c.step(nc.vector.tensor_tensor(own, t[4], t[0], ALU.mult))
    return keep, own


def prepare_attn(nc, m, args, sp_):
    w, wskip = sp_.take(2, WQ), sp_.take(2, D)
    qrow, gat_b, slope, skip_b = sp_.take(WQ), sp_.take(D), sp_.take(D), sp_.take(D)
    at = sp_.at
    wq, wk, wq_t, wk_t = sp_.take(2, D), sp_.take(2, D), sp_.take(2, D), sp_.take(2, WQ)
    bq, bqs = sp_.take(2), sp_.take(2, P)
    ps = m.psum
    with ExitStack() as ctx:
        S = Sems(nc, ctx, "pattn")
        block = ctx.enter_context(nc.Block())

        @block.sync
        def _(sp):
            for t, a in ((wq, args.Wq), (wk, args.Wk), (wskip, args.Wskip)):
                sp.dma_start(t, a.rearrange("(c p) n -> p c n", p=P)).then_inc(S["load"], 16)
            sp.dma_start(bq, args.bq.rearrange("(c p) -> p c", p=P), allow_slow_non_contiguous=True).then_inc(S["load"], 16)
            sp.dma_start(wk_t[:, :, D], args.bk.rearrange("(c p) -> p c", p=P), allow_slow_non_contiguous=True).then_inc(S["load"], 16)
            for t, a in ((gat_b, args.gat_bias), (slope, args.prelu1), (skip_b, args.bskip)):
                sp.dma_start(t, as_row(a)).then_inc(S["load"], 16)
            sp.wait_ge(S["load"], 128)

        @block.tensor
        def _(pe):
            pe.wait_ge(S["load"], 128)
            for i, t in enumerate((wq, wk)):
                for r in range(2):
                    for c in range(2):
                        last = nc.tensor.transpose(ps[:, 2 * i + c, r * P:(r + 1) * P], t[:, r, c * P:(c + 1) * P], m.ident[:, :])
            last.then_inc(S["turned"], 1)
            pe.wait_ge(S["copied"], 1)
            for r in range(2):
                for c in range(2):
                    nc.tensor.matmul(ps[:, 4 + r, 0:WQ], wq_t[:, c, r * P:(r + 1) * P], wk_t[:, c, :], start=(c == 0), stop=(c == 1))
            for c in range(2):
                last = nc.tensor.matmul(ps[:, 6, 0:WQ], bqs[:, c, :], wk_t[:, c, :], start=(c == 0), stop=(c == 1))
            last.then_inc(S["product"], 1)

        @block.vector
        def _(dve):
            nc.vector.memset(wk_t[:, :, D + 1], 0.0)
            dve.wait_ge(S["load"], 128)
            dve.wait_ge(S["turned"], 1)
            nc.vector.tensor_copy(wq_t, ps[:, 0:2, 0:D])
            nc.vector.tensor_copy(wk_t[:, :, 0:D], ps[:, 2:4, 0:D])
            nc.vector.tensor_copy(bqs, spread(bq, P)).then_inc(S["copied"], 1)
            dve.wait_ge(S["product"], 1)
            nc.vector.tensor_scalar(w, ps[:, 4:6, 0:WQ], float(D) ** -0.5, None, ALU.mult)
            nc.vector.tensor_scalar(qrow, ps[:, 6, 0:WQ], float(D) ** -0.5, None, ALU.mult).then_inc(S["done"], 1)
    sp_.at = at
    return w, wskip, qrow, gat_b, slope, skip_b


def prelu(nc, dve, S, b, x, low, slope, out, tag):
    nc.vector.scalar_tensor_tensor(low, x, 0.0, slope, ALU.min, ALU.mult).then_inc(S[tag + "_low"], 1)
    use(dve, S[tag + "_low"], b)
    return nc.vector.scalar_tensor_tensor(out, x, 0.0, low, ALU.max, ALU.add)


def nodes_mid(nc, m, dram, weights, keep, own, sp_):
    w, wskip, qrow, gat_b, slope, skip_b = weights
    h, t1, t2, low = (sp_.take(2, D) for _ in range(4))
    x1 = sp_.take(2, W1)
    xT, q, rest, skip = sp_.take(2, D), sp_.take(2, WQ), sp_.take(2, WQ), sp_.take(2, D)
    tab = m.tabs[:, 0:NB * 3 * WQ].rearrange("p (b s k) -> p b s k", b=NB, s=3)
    ps = m.psum
    with ExitStack() as ctx:
        S = Sems(nc, ctx, "mid")
        block = ctx.enter_context(nc.Block())

        def part(b, s):
            return one(tab[:, bass.ds(b, 1), s, :])

        @block.sync
        def _(sp):
            def load(b, p):
                use(sp, S["own"], b, 2)
                sp.dma_start(h[:, p, :], rows_of(dram.t0, b, D)).then_inc(S[f"h{p}"], 16)

            def store(b, p):
                use(sp, S["skip"], b)
                sp.dma_start(rows_of(dram.skip, b), skip[:, p, :]).then_inc(S[f"skip_stored{p}"], 16)

            node_blocks(sp, load, store)
            sp.wait_ge(S["skip_stored0"], 16 * (NB - NB // 2))
            sp.wait_ge(S["skip_stored1"], 16 * (NB // 2))

        @block.gpsimd
        def _(pool):
            def own_rows(b, p):
                landed(pool, S[f"h{p}"], b, p)
                use(pool, S["joined"], b, 2)
                nc.gpsimd.tensor_tensor(by_heads(t2[:, p, :], H0), by_heads(h[:, p, :], H0), spread(one(own[:, bass.ds(b, 1), :]), D // H0), ALU.mult).then_inc(S["own"], 1)
                use(pool, S["own"], b)
                nc.gpsimd.tensor_tensor(t2[:, p, :], t2[:, p, :], gat_b, ALU.add).then_inc(S["own_bias"], 1)

            node_blocks(pool, own_rows)

        @block.scalar
        def _(act):
            def turned(b, p):
                use(act, S["x1"], b)
                act.dma_start(rows_of(dram.t1, b), x1[:, p, :]).then_inc(S[f"x1_stored{p}"], 16)
                use(act, S["turned"], b)
                use(act, S["projected"], b, 2)
                nc.scalar.activation(xT[:, p, :], ps[:, p, 0:D], ACT.Copy).then_inc(S["xT"], 1)

            def parts(b, p):
                use(act, S["q"], b)
                nc.scalar.activation(part(b, 0), q[:, p, :], ACT.Copy).then_inc(S["hi"], 1)
                use(act, S["rest"], b)
                nc.scalar.activation(part(b, 1), rest[:, p, :], ACT.Copy).then_inc(S["mid"], 1)

            node_blocks(act, turned, parts)
            act.wait_ge(S["x1_stored0"], 16 * (NB - NB // 2))
            act.wait_ge(S["x1_stored1"], 16 * (NB // 2))

        @block.tensor
        def _(pe):
            def turn(b, p):
                use(pe, S["x1"], b)
                use(pe, S["xT"], b, 2)
                for c in range(2):
                    last = nc.tensor.transpose(ps[:, p, c * P:(c + 1) * P], x1[:, p, c * P:(c + 1) * P], m.ident[:, :])
                last.then_inc(S["turned"], 1)

            def project(b, p):
                use(pe, S["xT"], b)
                use(pe, S["q"], b, 2)
                use(pe, S["skip"], b, 2)
                for at, width, ww in ((2, WQ, w), (4, D, wskip)):
                    for c in range(2):
                        last = nc.tensor.matmul(ps[:, at + p, 0:width], xT[:, p, c * P:(c + 1) * P], ww[:, c, :], start=(c == 0), stop=(c == 1))
                last.then_inc(S["projected"], 1)

            node_blocks(pe, turn, project)

        @block.vector
        def _(dve):
            def output(b, p):
                use(dve, S["joined"], b, 2)
                nc.vector.tensor_tensor(by_heads(t1[:, p, :], H0), by_heads(acc_rows(m, b, 0, D), H0), spread(one(keep[:, bass.ds(b, 1), :]), D // H0), ALU.mult).then_inc(S["kept"], 1)
                use(dve, S["kept"], b)
                use(dve, S["own_bias"], b)
                use(dve, S["x1"], b, 2)
                nc.vector.tensor_tensor(t1[:, p, :], t1[:, p, :], t2[:, p, :], ALU.add).then_inc(S["joined"], 1)
                use(dve, S["joined"], b)
                vacated(dve, S[f"x1_stored{p}"], b, p)
                use(dve, S["turned"], b, 2)
                prelu(nc, dve, S, b, t1[:, p, :], low[:, p, :], slope, x1[:, p, 0:D], "p1").then_inc(S["x1"], 1)

            def tables(b, p):
                use(dve, S["projected"], b)
                use(dve, S["lo"], b, 2)
                use(dve, S["mid"], b, 2)
                nc.vector.tensor_tensor(q[:, p, :], ps[:, 2 + p, 0:WQ], qrow, ALU.add).then_inc(S["q"], 1)
                vacated(dve, S[f"skip_stored{p}"], b, p)
                nc.vector.tensor_tensor(skip[:, p, :], ps[:, 4 + p, 0:D], skip_b, ALU.add).then_inc(S["skip"], 1)
                use(dve, S["hi"], b)
                nc.vector.tensor_tensor(rest[:, p, :], q[:, p, :], part(b, 0), ALU.subtract).then_inc(S["rest"], 1)
                use(dve, S["rest"], b)
                use(dve, S["mid"], b)
                nc.vector.tensor_tensor(part(b, 2), rest[:, p, :], part(b, 1), ALU.subtract).then_inc(S["lo"], 1)

            nc.vector.memset(x1[:, :, D:D + 1], 1.0)
            nc.vector.memset(x1[:, :, D + 1:W1], 0.0)
            node_blocks(dve, output, tables)


def prepare_typed(nc, m, args, dram, sp_):
    w, wv = sp_.take(2, W2), sp_.take(2, D)
    bv, slope = sp_.take(D), sp_.take(D)
    per_den, share = sp_.take(NB), sp_.take(NB)
    at = sp_.at
    ws, wd = sp_.take(2, D), sp_.take(2, D)
    att, mask, att_m = sp_.take(2, 4), sp_.take(2, H2), sp_.take(2, 4 * H2)
    acc = m.acc[:, :].rearrange("p (b w) -> p b w", b=NB)
    ps = m.psum
    with ExitStack() as ctx:
        S = Sems(nc, ctx, "ptyped")
        block = ctx.enter_context(nc.Block())

        @block.sync
        def _(sp):
            for t, a in ((ws, args.W_src), (wd, args.W_dst), (wv, args.Wv)):
                sp.dma_start(t, a.rearrange("(c p) n -> p c n", p=P)).then_inc(S["load"], 16)
            for i, a in enumerate((args.att_src1, args.att_dst1)):
                for ty in range(2):
                    sp.dma_start(att[:, :, 2 * i + ty], a[ty, :, :].rearrange("h k -> (h k)").rearrange("(c p) -> p c", p=P),
                                 allow_slow_non_contiguous=True).then_inc(S["load"], 16)
            for t, a in ((bv, args.bv), (slope, args.prelu2)):
                sp.dma_start(t, as_row(a)).then_inc(S["load"], 16)
            for i, t in enumerate((m.last_t, m.type_t, m.type0_t, m.weight_t)):
                sp.dma_start(t[:, :], dram.kept[:, i, :]).then_inc(S["load"], 16)
            sp.wait_ge(S["load"], 208)

        @block.gpsimd
        def _(pool):
            nc.gpsimd.iota(m.head_int[:, 0:2 * H2], [[P, 2], [-32, H2]], base=0, channel_multiplier=1).then_inc(S["iota"], 1)

        @block.tensor
        def _(pe):
            pe.wait_ge(S["load"], 208)
            for r in range(2):
                for c in range(2):
                    nc.tensor.transpose(ps[:, c, r * P:(r + 1) * P], ws[:, r, c * P:(c + 1) * P], m.ident[:, :])
            pe.wait_ge(S["masked"], 1)
            for r in range(2):
                for i, t in enumerate((ws, wd)):
                    for c in range(2):
                        last = nc.tensor.matmul(ps[:, 2 + r, 16 * i:16 * i + 16], t[:, c, r * P:(r + 1) * P], att_m[:, c, 16 * i:16 * i + 16],
                                                start=(c == 0), stop=(c == 1))
            last.then_inc(S["product"], 1)

        @block.vector
        def _(dve):
            c_ = Chain(dve, S["dve"])
            c_.step(nc.vector.tensor_scalar(share, acc[:, :, D], 1e-16, None, ALU.add))
            c_.step(nc.vector.reciprocal(per_den, share))
            c_.step(nc.vector.tensor_tensor(share, per_den, acc[:, :, D], ALU.mult))
            dve.wait_ge(S["iota"], 1)
            head_mask_into(nc, m, c_, mask, 32, H2)
            dve.wait_ge(S["load"], 208)
            for i in range(4):
                for c in range(2):
                    last = nc.vector.tensor_scalar(att_m[:, c, i * H2:(i + 1) * H2], mask[:, c, :], att[:, c, i:i + 1], None, ALU.mult)
            last.then_inc(S["masked"], 1)
            dve.wait_ge(S["product"], 1)
            nc.vector.tensor_copy(w[:, :, 0:D], ps[:, 0:2, 0:D])
            nc.vector.tensor_copy(w[:, :, D:W2], ps[:, 2:4, 0:4 * H2]).then_inc(S["done"], 1)
    sp_.at = at
    return w, wv, bv, slope, per_den, share


def nodes_between(nc, m, args, dram, weights, sp_):
    w, wv, bv, slope, per_den, share = weights
    agg, aggT, y, low, x, x2, h, hT = (sp_.take(2, D) for _ in range(8))
    row, st, rest = sp_.take(2, W2), sp_.take(2, 10), sp_.take(2, 2 * H2)
    tab = m.tabs[:, 0:NB * 3 * 2 * H2].rearrange("p (b s k) -> p b s k", b=NB, s=3)
    ps = m.psum
    with ExitStack() as ctx:
        S = Sems(nc, ctx, "between")
        block = ctx.enter_context(nc.Block())

        @block.sync
        def _(sp):
            def load(b, p):
                use(sp, S["y"], b, 2)
                sp.dma_start(y[:, p, :], rows_of(dram.skip, b)).then_inc(S[f"skip{p}"], 16)
                use(sp, S["x2"], b, 2)
                sp.dma_start(x[:, p, :], rows_of(args.x, b)).then_inc(S[f"x{p}"], 16)

            def store_x(b, p):
                use(sp, S["x2"], b)
                sp.dma_start(rows_of(dram.x2, b), x2[:, p, :]).then_inc(S[f"x2_stored{p}"], 16)
                use(sp, S["h"], b)
                sp.dma_start(rows_of(dram.h1, b), h[:, p, :]).then_inc(S[f"h_stored{p}"], 16)

            def store_row(b, p):
                use(sp, S["row"], b)
                sp.dma_start(rows_of(dram.t2, b), row[:, p, :]).then_inc(S[f"row_stored{p}"], 16)

            node_blocks(sp, load, store_x, store_row)
            for name in ("x2_stored", "h_stored", "row_stored"):
                sp.wait_ge(S[name + "0"], 16 * (NB - NB // 2))
                sp.wait_ge(S[name + "1"], 16 * (NB // 2))

        @block.gpsimd
        def _(pool):
            node_blocks(pool, lambda b, p: inverse_root(nc, pool, S, m, st[:, p, :], b))

        @block.scalar
        def _(act):
            def turned_sum(b, p):
                use(act, S["agg_turned"], b)
                use(act, S["valued"], b, 2)
                nc.scalar.activation(aggT[:, p, :], ps[:, p, 0:D], ACT.Copy).then_inc(S["aggT"], 1)

            def relu(b, p):
                use(act, S["hn"], b)
                nc.scalar.activation(h[:, p, :], h[:, p, :], ACT.Relu).then_inc(S["h"], 1)
                use(act, S["turned"], b)
                use(act, S["projected"], b, 2)
                nc.scalar.activation(hT[:, p, :], ps[:, 4 + p, 0:D], ACT.Copy).then_inc(S["hT"], 1)

            node_blocks(act, turned_sum, relu)

        @block.tensor
        def _(pe):
            def turn_sum(b, p):
                use(pe, S["agg"], b)
                use(pe, S["aggT"], b, 2)
                for c in range(2):
                    last = nc.tensor.transpose(ps[:, p, c * P:(c + 1) * P], agg[:, p, c * P:(c + 1) * P], m.ident[:, :])
                last.then_inc(S["agg_turned"], 1)
                use(pe, S["aggT"], b)
                use(pe, S["y_sum"], b, 2)
                for c in range(2):
                    last = nc.tensor.matmul(ps[:, 2 + p, 0:D], aggT[:, p, c * P:(c + 1) * P], wv[:, c, :], start=(c == 0), stop=(c == 1))
                last.then_inc(S["valued"], 1)

            def turn(b, p):
                use(pe, S["h"], b)
                use(pe, S["hT"], b, 2)
                for c in range(2):
                    last = nc.tensor.transpose(ps[:, 4 + p, c * P:(c + 1) * P], h[:, p, c * P:(c + 1) * P], m.ident[:, :])
                last.then_inc(S["turned"], 1)

            def project(b, p):
                use(pe, S["hT"], b)
                use(pe, S["row"], b, 2)
                for c in range(2):
                    last = nc.tensor.matmul(ps[:, 6 + p, 0:W2], hT[:, p, c * P:(c + 1) * P], w[:, c, :], start=(c == 0), stop=(c == 1))
                last.then_inc(S["projected"], 1)

            node_blocks(pe, turn_sum, turn, project)

        @block.vector
        def _(dve):
            idle = dve.alloc_register("between_idle")
            dve.reg_mov(idle, 0)

            def normalize_sum(b, p):
                use(dve, S["agg_turned"], b, 2)
                nc.vector.tensor_scalar(agg[:, p, :], acc_rows(m, b, 0, D), per_den[:, bass.ds(b, 1)], None, ALU.mult).then_inc(S["agg"], 1)

            def output(b, p):
                landed(dve, S[f"skip{p}"], b, p)
                nc.vector.scalar_tensor_tensor(y[:, p, :], bv, share[:, bass.ds(b, 1)], y[:, p, :], ALU.mult, ALU.add).then_inc(S["y_bias"], 1)
                use(dve, S["y_bias"], b)
                use(dve, S["valued"], b)
                nc.vector.tensor_tensor(y[:, p, :], y[:, p, :], ps[:, 2 + p, 0:D], ALU.add).then_inc(S["y_sum"], 1)
                use(dve, S["y_sum"], b)
                prelu(nc, dve, S, b, y[:, p, :], low[:, p, :], slope, low[:, p, :], "p2").then_inc(S["y"], 1)
                use(dve, S["y"], b)
                landed(dve, S[f"x{p}"], b, p)
                vacated(dve, S[f"x2_stored{p}"], b, p)
                nc.vector.tensor_tensor(x2[:, p, :], x[:, p, :], low[:, p, :], ALU.add).then_inc(S["x2"], 1)
                use(dve, S["x2"], b)
                layernorm_stats(nc, dve, S, x2[:, p, :], st[:, p, :], b, idle)
                use(dve, S["ln_rstd"], b)
                use(dve, S["turned"], b, 2)
                vacated(dve, S[f"h_stored{p}"], b, p)
                nc.vector.tensor_scalar(h[:, p, :], x2[:, p, :], st[:, p, 6:7], st[:, p, 9:10], ALU.subtract, ALU.mult).then_inc(S["hn"], 1)

            def rows(b, p):
                use(dve, S["projected"], b)
                vacated(dve, S[f"row_stored{p}"], b, p)
                nc.vector.tensor_copy(row[:, p, :], ps[:, 6 + p, 0:W2]).then_inc(S["row"], 1)
                use(dve, S["row"], b)
                nc.vector.tensor_copy(m.self_logit[:, bass.ds(b, 1), :], row[:, p, D:W2].unsqueeze(1)).then_inc(S["self"], 1)
                split3(nc, dve, S, lambda s: one(tab[:, bass.ds(b, 1), s, :]), row[:, p, D + 2 * H2:W2], rest[:, p:p + 1, :], b, p, "ad")

            node_blocks(dve, normalize_sum, output, rows)


def prepare_ffn(nc, m, args, sp_):
    ts = Space(m.tabs[:, :].bitcast(F32))
    w1_t, w2_t, raw1, raw2 = ts.take(2, FFN), ts.take(FFN // P, D), ts.take(FFN // P, D), ts.take(2, FFN)
    b1 = sp_.take(FFN // P)
    vectors = {"bias1": args.bias1, "ln1_g": args.ln1_g, "ln1_b": args.ln1_b, "ln2_g": args.ln2_g, "ln2_b": args.ln2_b, "b2": args.b2}
    rows = {n: sp_.take(D) for n in vectors}
    ps = m.psum
    FC = FFN // P
    with ExitStack() as ctx:
        S = Sems(nc, ctx, "pffn")
        block = ctx.enter_context(nc.Block())

        @block.sync
        def _(sp):
            sp.dma_start(raw1, args.W1.rearrange("(f p) n -> p f n", p=P)).then_inc(S["load"], 16)
            sp.dma_start(raw2, args.W2.rearrange("(c p) n -> p c n", p=P)).then_inc(S["load"], 16)
            sp.dma_start(b1, args.b1.rearrange("(f p) -> p f", p=P), allow_slow_non_contiguous=True).then_inc(S["load"], 16)
            for n, vector in vectors.items():
                sp.dma_start(rows[n], as_row(vector)).then_inc(S["load"], 16)
            sp.wait_ge(S["load"], 16 * (3 + len(vectors)))

        @block.tensor
        def _(pe):
            pe.wait_ge(S["load"], 16 * (3 + len(vectors)))
            for f in range(FC):
                for c in range(2):
                    nc.tensor.transpose(ps[:, 2 * c + f // 4, (f % 4) * P:(f % 4 + 1) * P], raw1[:, f, c * P:(c + 1) * P], m.ident[:, :])
                    last = nc.tensor.transpose(ps[:, 4 + f // 2, (f % 2) * D + c * P:(f % 2) * D + (c + 1) * P], raw2[:, c, f * P:(f + 1) * P], m.ident[:, :])
            last.then_inc(S["turned"], 1)

        @block.vector
        def _(dve):
            dve.wait_ge(S["turned"], 1)
            nc.vector.tensor_copy(w1_t.rearrange("p c (a n) -> p (c a) n", a=2), ps[:, 0:4, :])
            nc.vector.tensor_copy(w2_t.rearrange("p (a f) n -> p a (f n)", a=4), ps[:, 4:8, :]).then_inc(S["done"], 1)
    return w1_t, w2_t, b1, rows


def nodes_ffn(nc, m, args, dram, weights, keep, own, sp_):
    w1_t, w2_t, b1, rows = weights
    FC = FFN // P
    more = Space(m.tabs[:, :].bitcast(F32), 4 * 2 * FFN)
    xs, h1, x2, t1, t2, z, u, uT, v, o = (more.take(2, D) for _ in range(10))
    g = more.take(2, FC, P)
    st, st2 = sp_.take(2, 10), sp_.take(2, 10)
    ps = m.psum
    with ExitStack() as ctx:
        S = Sems(nc, ctx, "ffn")
        block = ctx.enter_context(nc.Block())

        @block.sync
        def _(sp):
            def load(b, p):
                use(sp, S["own"], b, 2)
                sp.dma_start(xs[:, p, :], rows_of(dram.t2, b, D)).then_inc(S[f"xs{p}"], 16)
                use(sp, S["own_sum"], b, 2)
                sp.dma_start(h1[:, p, :], rows_of(dram.h1, b)).then_inc(S[f"h{p}"], 16)
                use(sp, S["out"], b, 2)
                sp.dma_start(x2[:, p, :], rows_of(dram.x2, b)).then_inc(S[f"x2{p}"], 16)

            node_blocks(sp, load)

        @block.gpsimd
        def _(pool):
            def own_rows(b, p):
                landed(pool, S[f"xs{p}"], b, p)
                use(pool, S["z"], b, 2)
                nc.gpsimd.tensor_tensor(by_heads(t2[:, p, :], H2), by_heads(xs[:, p, :], H2), spread(one(own[:, bass.ds(b, 1), :]), D // H2), ALU.mult).then_inc(S["own"], 1)
                use(pool, S["own"], b)
                nc.gpsimd.tensor_tensor(t2[:, p, :], t2[:, p, :], rows["bias1"], ALU.add).then_inc(S["own_bias"], 1)
                use(pool, S["own_bias"], b)
                landed(pool, S[f"h{p}"], b, p)
                nc.gpsimd.tensor_tensor(t2[:, p, :], t2[:, p, :], h1[:, p, :], ALU.add).then_inc(S["own_sum"], 1)
                inverse_root(nc, pool, S, m, st[:, p, :], b, "l1")

            def finish(b, p):
                inverse_root(nc, pool, S, m, st2[:, p, :], b, "l2")
                use(pool, S["vn"], b)
                vacated(pool, S[f"out_stored{p}"], b, p)
                nc.gpsimd.tensor_tensor(o[:, p, :], o[:, p, :], rows["ln2_g"], ALU.mult).then_inc(S["out_g"], 1)
                use(pool, S["out_g"], b)
                nc.gpsimd.tensor_tensor(o[:, p, :], o[:, p, :], rows["ln2_b"], ALU.add).then_inc(S["out_b"], 1)
                use(pool, S["out_b"], b)
                landed(pool, S[f"x2{p}"], b, p)
                nc.gpsimd.tensor_tensor(o[:, p, :], o[:, p, :], x2[:, p, :], ALU.add).then_inc(S["out"], 1)

            node_blocks(pool, own_rows, None, finish)

        @block.scalar
        def _(act):
            def turned(b, p):
                use(act, S["turned"], b)
                use(act, S["up"], b, 2)
                nc.scalar.activation(uT[:, p, :], ps[:, p, 0:D], ACT.Copy).then_inc(S["uT"], 1)

            def gelu(b, p):
                use(act, S["up"], b)
                use(act, S["down"], b, 2)
                for f in range(FC):
                    last = nc.scalar.activation(g[:, p, f, :], ps[:, 2 + 2 * p + f // 4, (f % 4) * P:(f % 4 + 1) * P], ACT.Gelu, bias=b1[:, f:f + 1])
                last.then_inc(S["gelu"], 1)

            def store(b, p):
                use(act, S["out"], b)
                act.dma_start(rows_of(args.out, b), o[:, p, :]).then_inc(S[f"out_stored{p}"], 16)

            node_blocks(act, turned, gelu, store)
            act.wait_ge(S["out_stored0"], 16 * (NB - NB // 2))
            act.wait_ge(S["out_stored1"], 16 * (NB // 2))

        @block.tensor
        def _(pe):
            def turn(b, p):
                use(pe, S["u"], b)
                use(pe, S["uT"], b, 2)
                for c in range(2):
                    last = nc.tensor.transpose(ps[:, p, c * P:(c + 1) * P], u[:, p, c * P:(c + 1) * P], m.ident[:, :])
                last.then_inc(S["turned"], 1)

            def up(b, p):
                use(pe, S["uT"], b)
                use(pe, S["gelu"], b, 2)
                for f in range(FC):
                    for c in range(2):
                        last = nc.tensor.matmul(ps[:, 2 + 2 * p + f // 4, (f % 4) * P:(f % 4 + 1) * P], w1_t[:, c, f * P:(f + 1) * P],
                                                uT[:, p, c * P:(c + 1) * P], start=(c == 0), stop=(c == 1))
                last.then_inc(S["up"], 1)

            def down(b, p):
                use(pe, S["gelu"], b)
                use(pe, S["v"], b, 2)
                for f in range(FC):
                    last = nc.tensor.matmul(ps[:, 6 + p, 0:D], g[:, p, f, :], w2_t[:, f, :], start=(f == 0), stop=(f == FC - 1))
                last.then_inc(S["down"], 1)

            node_blocks(pe, turn, up, down)

        @block.vector
        def _(dve):
            idle = dve.alloc_register("ffn_idle")
            dve.reg_mov(idle, 0)

            def attention(b, p):
                use(dve, S["z"], b, 2)
                nc.vector.tensor_tensor(by_heads(t1[:, p, :], H2), by_heads(acc_rows(m, b, 0, D), H2), spread(one(keep[:, bass.ds(b, 1), :]), D // H2), ALU.mult).then_inc(S["kept"], 1)
                use(dve, S["kept"], b)
                use(dve, S["own_sum"], b)
                nc.vector.tensor_tensor(z[:, p, :], t1[:, p, :], t2[:, p, :], ALU.add).then_inc(S["z"], 1)
                use(dve, S["z"], b)
                layernorm_stats(nc, dve, S, z[:, p, :], st[:, p, :], b, idle, "l1")
                use(dve, S["l1_rstd"], b)
                nc.vector.tensor_scalar(z[:, p, :], z[:, p, :], st[:, p, 6:7], st[:, p, 9:10], ALU.subtract, ALU.mult).then_inc(S["zn"], 1)
                use(dve, S["zn"], b)
                use(dve, S["turned"], b, 2)
                use(dve, S["v_sum"], b, 2)
                nc.vector.tensor_tensor(z[:, p, :], z[:, p, :], rows["ln1_g"], ALU.mult).then_inc(S["zg"], 1)
                use(dve, S["zg"], b)
                nc.vector.tensor_tensor(u[:, p, :], z[:, p, :], rows["ln1_b"], ALU.add).then_inc(S["u"], 1)

            def output(b, p):
                use(dve, S["down"], b)
                nc.vector.tensor_tensor(v[:, p, :], ps[:, 6 + p, 0:D], rows["b2"], ALU.add).then_inc(S["v"], 1)
                use(dve, S["v"], b)
                nc.vector.tensor_tensor(v[:, p, :], v[:, p, :], u[:, p, :], ALU.add).then_inc(S["v_sum"], 1)
                use(dve, S["v_sum"], b)
                layernorm_stats(nc, dve, S, v[:, p, :], st2[:, p, :], b, idle, "l2")
                use(dve, S["l2_rstd"], b)
                vacated(dve, S[f"out_stored{p}"], b, p)
                nc.vector.tensor_scalar(o[:, p, :], v[:, p, :], st2[:, p, 6:7], st2[:, p, 9:10], ALU.subtract, ALU.mult).then_inc(S["vn"], 1)

            node_blocks(dve, attention, None, output)


class Held:
    pass


def build_program(nc, x, edges, weights, gat_W, att_src0, att_dst0, gat_bias, prelu1, Wq, bq, Wk, bk, Wv, bv, Wskip, bskip, prelu2,
                  W_src, W_dst, att_src1, att_dst1, bias1, ln1_g, ln1_b, ln2_g, ln2_b, ffn1, b1, ffn2, b2, out):
    args = Held()
    (args.x, args.gat_W, args.att_src0, args.att_dst0, args.gat_bias, args.prelu1) = (x, gat_W, att_src0, att_dst0, gat_bias, prelu1)
    (args.Wq, args.bq, args.Wk, args.bk, args.Wv, args.bv, args.Wskip, args.bskip, args.prelu2) = (Wq, bq, Wk, bk, Wv, bv, Wskip, bskip, prelu2)
    (args.W_src, args.W_dst, args.att_src1, args.att_dst1, args.bias1) = (W_src, W_dst, att_src1, att_dst1, bias1)
    (args.ln1_g, args.ln1_b, args.ln2_g, args.ln2_b, args.W1, args.b1, args.W2, args.b2, args.out) = (ln1_g, ln1_b, ln2_g, ln2_b, ffn1, b1, ffn2, b2, out)
    m, dram = Held(), Held()
    dram.edges, dram.weights = edges, weights
    with ExitStack() as ctx:
        def sb(name, shape, dt=F32):
            return ctx.enter_context(nc.sbuf_tensor(name, shape, dt))

        def dr(name, shape, dt=F32):
            return nc.dram_tensor(name, shape, dt, kind="Internal").ap()

        dram.rel16 = dr("visit_positions", [NV * P], BF16)
        dram.scal = dr("visit_scalars", [4, NV])
        dram.dst_s = dr("visit_dst", [NV // G, HB, G, P])
        dram.rows = dr("batch_rows", [NV // G, 6, G])
        dram.t0 = dr("table_gat", [NP, W0])
        dram.t1 = dr("table_attn", [NP, W1])
        dram.t2 = dr("table_typed", [NP, W2])
        dram.skip = dr("skip_rows", [NP, D])
        dram.x2 = dr("x_after_layer0", [NP, D])
        dram.kept = dr("edge_tables", [P, 4, NV])
        dram.h1 = dr("h_layer1", [NP, D])
        m.arena = sb("arena", [P, 2 * G * W2])
        m.acc = sb("acc", [P, NB * WA])
        m.tabs = sb("tabs", [P, NB * 3 * WQ], BF16)
        m.src_t = sb("src_t", [P, NV], I32)
        m.rel_t, m.mask_t = sb("rel_t", [P, NV]), sb("mask_t", [P, NV])
        rest = Space(m.tabs[:, NB * 3 * 2 * H2:NB * 3 * WQ].bitcast(F32))
        m.last_t, m.type_t, m.type0_t, m.weight_t = (rest.take(NV) for _ in range(4))
        m.self_logit = rest.take(NB, 4 * H2)
        m.blocks = sb("blocks", [1, NV], I32)
        m.iota, m.pcol, m.ident = sb("iota", [P, P]), sb("pcol", [P, 1]), sb("ident", [P, P])
        m.half, m.ones = sb("half", [P, 1]), sb("ones", [P, 1])
        m.ints, m.ints2 = sb("ints", [P, G + HB], I32), sb("ints2", [P, G + HB], I32)
        m.ints_t, m.ints_t2 = sb("ints_t", [HB, P], I32), sb("ints_t2", [HB, P], I32)
        m.visit_col, m.head_rows, m.head_rows_t = sb("visit_col", [P, G]), sb("head_rows", [P, HB]), sb("head_rows_t", [HB, P])
        m.head_int = sb("head_int", [P, 2 * HB], I32)
        m.rel_row = sb("rel_row", [P, 2, G * P], BF16)
        m.onehot_t = sb("onehot_t", [P, G, P], BF16)
        m.onehot, m.dist = sb("onehot", [P, 4, P]), sb("dist", [P, 4, P])
        m.dst_s, m.rows = sb("dst_s", [P, 2, P]), sb("rows", [HB, 2, 6 * G])
        m.seg_bias, m.seg_max, m.seg_tmp = sb("seg_bias", [P, 1, P + 1]), sb("seg_max", [P, 3, P]), sb("seg_tmp", [P, 3, P])
        m.ends, m.end_max = sb("ends", [P, 2, G]), sb("end_max", [P, 2])
        m.fore_max, m.back_max = sb("fore_max", [HB, 2, G + 1]), sb("back_max", [HB, 1, G + 1])
        m.joined, m.join_tmp = sb("joined", [HB, 2, G]), sb("join_tmp", [HB, 3, G])
        m.first_hot, m.growth, m.shrink = sb("first_hot", [HB, P]), sb("growth", [HB, HB]), sb("shrink", [P, HB])
        m.raw, m.logit, m.shifted = sb("raw", [P, P]), sb("logit", [P, P]), sb("shifted", [P, P])
        m.both, m.edge_scale = sb("both", [P, G, 2 * HB]), sb("edge_scale", [P, G, HB])
        m.weight, m.neg_weight = sb("weight", [P, 2, G]), sb("neg_weight", [P, 2, G])
        m.junk = sb("junk", [P, 2, WQ])
        m.idx = sb("idx", [P, 2, G], I32)
        m.psum = ctx.enter_context(nc.psum_tensor("psum", [P, 8, 512], F32))

        constants(nc, m)
        visits(nc, m, dram)
        space = Space(m.arena)
        w = prepare_gat(nc, m, args, space)
        nodes_in(nc, m, args, dram, w, space)
        edge_pass(nc, m, dram, Phase(m, "gat", H0, dram.t0, W0, W0, H0, (6, 8, 10, 12, 14)))
        space = Space(m.arena)
        keep, own = head_factors(nc, m, dram, H0, 0, H0, 1e-16, space, "fgat")
        w = prepare_attn(nc, m, args, space)
        nodes_mid(nc, m, dram, w, keep, own, space)
        edge_pass(nc, m, dram, Phase(m, "attn", 1, dram.t1, W1, WQ, WQ, (8, 9, 11, 13, 15)))
        space = Space(m.arena)
        w = prepare_typed(nc, m, args, dram, space)
        nodes_between(nc, m, args, dram, w, space)
        edge_pass(nc, m, dram, Phase(m, "typed", H2, dram.t2, W2, WA, 2 * H2, (6, 8, 10, 12, 14)))
        space = Space(m.arena)
        keep, own = head_factors(nc, m, dram, H2, 0, 2 * H2, 0.0, space, "ftyped")
        w = prepare_ffn(nc, m, args, space)
        nodes_ffn(nc, m, args, dram, w, keep, own, space)


_INS = ["x", "edges", "weights", "L0_gnn_gat_W", "L0_gnn_att_src", "L0_gnn_att_dst", "L0_gnn_gat_bias", "L0_gnn_prelu1_a",
        "L0_gnn_Wq", "L0_gnn_bq", "L0_gnn_Wk", "L0_gnn_bk", "L0_gnn_Wv", "L0_gnn_bv", "L0_gnn_Wskip", "L0_gnn_bskip",
        "L0_gnn_prelu2_a", "L1_gnn_W_src", "L1_gnn_W_dst", "L1_gnn_att_src", "L1_gnn_att_dst", "L1_gnn_bias", "L1_gnn_ln1_g",
        "L1_gnn_ln1_b", "L1_gnn_ln2_g", "L1_gnn_ln2_b", "L1_gnn_ffn_W1", "L1_gnn_ffn_b1", "L1_gnn_ffn_W2", "L1_gnn_ffn_b2"]


def kernel(**inputs):
    import numpy as _np
    import concourse.bacc as _bacc
    from concourse import mybir as _mybir
    from concourse.bass_utils import run_bass_kernel_spmd as _run

    def tiled(a, fill):
        return _np.concatenate([a, _np.full((NT + 1) * P - a.shape[0], fill, a.dtype)]).reshape(NT + 1, P)

    given = {k: _np.ascontiguousarray(v) for k, v in inputs.items()}
    dst = given["dst"]
    given["edges"] = _np.stack([tiled(given["src"], 0), tiled(dst, PAD_NODE), tiled(dst[1:], PAD_NODE),
                                tiled(given["edge_type_2"], 0)], axis=1).reshape(NT + 1, 4 * P)
    given["weights"] = tiled(given["edge_weight"], 0)
    given["x"] = _np.concatenate([given["x"], _np.zeros((NP - N, D), given["x"].dtype)])

    nc = _bacc.Bacc("TRN2", target_bir_lowering=False, num_devices=1)
    arrays, args = {}, []
    for name in _INS:
        a = _np.ascontiguousarray(given[name])
        arrays[f"in_{name}_dram"] = a
        args.append(nc.dram_tensor(f"in_{name}_dram", a.shape, _mybir.dt.from_np(a.dtype), kind="ExternalInput").ap())
    args.append(nc.dram_tensor("out_0_dram", (NP, D), _mybir.dt.float32, kind="ExternalOutput").ap())
    build_program(nc, *args)
    r = _run(nc, [arrays], core_ids=[0])
    return r.results[0]["out_0_dram"][:N]
```

```python
import concourse.bass as bass
from concourse import mybir
from contextlib import ExitStack

F32 = mybir.dt.float32
I32 = mybir.dt.int32
BF16 = mybir.dt.bfloat16
ALU = mybir.AluOpType
ACT = mybir.ActivationFunctionType
DVE_ENGINE = mybir.EngineType.DVE
PE_ENGINE = mybir.EngineType.PE

P = 128
N = 6250
E = 100000
D = 256
NB = (N + P - 1) // P
NP = NB * P
NT = (E + P - 1) // P
PAD_NODE = NP - 1
G = 16
VISITS = NT + NB - 1
NBATCH = (VISITS + G - 1) // G
assert NBATCH % 2 == 0
VC = (NBATCH * G + P - 1) // P
NV = VC * P
HB = 8
BIG = 1e30
DST_SCALE = 1e30
FAR = 1000.0
H0, H2, FFN = 4, 8, 1024
W0 = D + 2 * H0
W1 = D + 4
W2 = D + 4 * H2
WA = D + 2 * H2
WQ = D + 2
EPS = 1e-5


class Sems:

    def __init__(self, nc, ctx, prefix):
        self.nc, self.prefix, self.made = nc, prefix, {}
        ctx.callback(self.clear)

    def __getitem__(self, name):
        if name not in self.made:
            self.made[name] = self.nc.alloc_semaphore(f"{self.prefix}_{name}")
        return self.made[name]

    def clear(self):
        self.nc.clear_and_free_semaphores(list(self.made.values()))
        self.nc.all_engine_barrier()


class Chain:

    def __init__(self, eng, sem):
        self.eng, self.sem, self.n = eng, sem, 0

    def step(self, ins):
        self.n += 1
        ins.then_inc(self.sem, 1)
        self.eng.wait_ge(self.sem, self.n)


def wait_apart(eng, sem, value, reg):
    if isinstance(value, int):
        eng.wait_ge(sem, value)
    else:
        eng.reg_mov(reg, value)
        eng.wait_ge(sem, 1)
        eng.wait_ge(sem, reg)


def spread(ap, n):
    return ap.unsqueeze(2).to_broadcast([ap.shape[0], ap.shape[1], n])


def constants(nc, m):
    with ExitStack() as ctx:
        S = Sems(nc, ctx, "const")
        block = ctx.enter_context(nc.Block())

        @block.gpsimd
        def _(pool):
            nc.gpsimd.iota(m.iota[:, :], [[1, P]], base=0, channel_multiplier=0,
                           allow_small_or_imprecise_dtypes=True).then_inc(S["iota"], 1)
            nc.gpsimd.iota(m.pcol[:, :], [[0, 1]], base=0, channel_multiplier=1,
                           allow_small_or_imprecise_dtypes=True).then_inc(S["iota"], 1)
            nc.gpsimd.iota(m.ints[:, 0:G], [[-1, G]], base=0, channel_multiplier=1).then_inc(S["iota"], 1)
            nc.gpsimd.iota(m.ints[:, G:G + HB], [[-G, HB]], base=0, channel_multiplier=1).then_inc(S["iota"], 1)
            nc.gpsimd.iota(m.ints_t[:, :], [[1, P]], base=0, channel_multiplier=-G).then_inc(S["iota"], 1)

        @block.vector
        def _(dve):
            c = Chain(dve, S["dve"])
            dve.wait_ge(S["iota"], 5)
            nc.vector.memset(m.half[:, :], -0.5)
            nc.vector.memset(m.ones[:, :], 1.0)
            nc.vector.memset(m.seg_bias[:, :, 0:1], -BIG)
            nc.vector.memset(m.seg_bias[:, :, P:P + 1], -BIG)
            nc.vector.memset(m.back_max[:, :, G:G + 1], -BIG)
            nc.vector.tensor_scalar(m.ident[:, :], m.iota[:, :], m.pcol[:, 0:1], None, ALU.is_equal)
            nc.vector.tensor_scalar(m.ints2[:, 0:G], m.ints[:, 0:G], G - 1, None, ALU.bitwise_and)
            nc.vector.tensor_scalar(m.ints2[:, G:G + HB], m.ints[:, G:G + HB], 4, None, ALU.arith_shift_right)
            c.step(nc.vector.tensor_scalar(m.ints_t2[:, :], m.ints_t[:, :], 4, None, ALU.arith_shift_right))
            nc.vector.tensor_scalar(m.visit_col[:, :], m.ints2[:, 0:G], 0, None, ALU.is_equal)
            nc.vector.tensor_scalar(m.head_rows[:, :], m.ints2[:, G:G + HB], 0, None, ALU.is_equal)
            c.step(nc.vector.tensor_scalar(m.head_rows_t[:, :], m.ints_t2[:, :], 0, None, ALU.is_equal))


def visits(nc, m, dram):
    with ExitStack() as ctx:
        S = Sems(nc, ctx, "meta")
        rec = m.arena[:, 0:4 * P].bitcast(I32)
        wrec = m.arena[:, 512:512 + P]
        dst_f, src_f, next_f, rel, et_f, last_f = (m.arena[:, 640 + P * i:640 + P * (i + 1)] for i in range(6))
        in_block, tmp, dst_s = (m.arena[:, 1408 + P * i:1408 + P * (i + 1)] for i in range(3))
        rel16 = m.arena[:, 1792:1856].bitcast(BF16)
        scal = m.arena[:, 1856:1860]
        last_dst = m.arena[:, 1860:1860 + VC].bitcast(I32)
        last_blk = m.arena[:, 1868:1868 + VC].bitcast(I32)
        v_end = m.arena[:, 1876:1876 + VC]
        v_idx = m.arena[:, 1884:1884 + VC]
        t_idx = m.arena[:, 1892:1892 + VC]
        blk = m.arena[:, 1900:1900 + VC]
        blk128 = m.arena[:, 1908:1908 + VC]
        tile_i = m.arena[:, 1916:1916 + VC].bitcast(I32)
        before = m.arena[:, 2048:2048 + NV // 2].bitcast(BF16)
        v_row = m.arena[:, 3072:3072 + NV]
        one16 = m.arena[:, 4096:4097].bitcast(BF16)
        rows = m.acc[0:1, 0:4 * NV].rearrange("p (a v) -> p a v", a=4)
        outs = m.acc[0:1, 4 * NV:10 * NV].rearrange("p (a v) -> p a v", a=6)
        both = m.acc[0:1, 10 * NV:11 * NV]
        ps = m.psum
        tables = [m.src_t, m.rel_t, m.last_t, m.type_t, m.weight_t]
        block = ctx.enter_context(nc.Block())

        @block.sync
        def _(sp):
            sp.wait_ge(S["preset"], 1)
            for c in range(VC):
                k = min(P, NT - c * P)
                if k > 0:
                    sp.dma_start(last_dst[0:k, c:c + 1], dram.edges[c * P:c * P + k, 2 * P - 1:2 * P], allow_slow_non_contiguous=True).then_inc(S["last_dst"], 16)
            for c in range(VC):
                sp.wait_ge(S["chunk"], c + 1)
                sp.dma_start(dram.rel16[c * P * P:(c + 1) * P * P].rearrange("(v e) -> v e", e=P), rel16).then_inc(S["stored"], 16)
                sp.dma_start(dram.scal[:, c * P:(c + 1) * P].rearrange("a v -> v a"), scal, allow_slow_non_contiguous=True).then_inc(S["stored"], 16)
                for h in range(HB):
                    sp.dma_start(dram.dst_s[c * (P // G):(c + 1) * (P // G), h, :, :], dst_s).then_inc(S["stored"], 16)
            sp.wait_ge(S["kept"], 1)
            for i, t in enumerate((m.last_t, m.type_t, m.type0_t, m.weight_t)):
                sp.dma_start(dram.kept[:, i, :], t[:, :]).then_inc(S["kept_stored"], 16)
            sp.wait_ge(S["kept_stored"], 64)
            sp.wait_ge(S["stored"], VC * 16 * (2 + HB))
            sp.dma_start(rows, dram.scal.rearrange("(p a) v -> p a v", p=1)).then_inc(S["rows"], 16)
            sp.wait_ge(S["outs"], 1)
            for a in range(6):
                sp.dma_start(dram.rows[:, a, :].rearrange("(p k) g -> p k g", p=1),
                             outs[:, a, :].rearrange("p (k g) -> p k g", g=G)).then_inc(S["end"], 16)
            sp.wait_ge(S["end"], 96)

        @block.gpsimd
        def _(pool):
            nc.gpsimd.iota(v_idx, [[P, VC]], base=0, channel_multiplier=1,
                           allow_small_or_imprecise_dtypes=True).then_inc(S["iota"], 1)
            nc.gpsimd.iota(v_row, [[1, NV]], base=0, channel_multiplier=0,
                           allow_small_or_imprecise_dtypes=True).then_inc(S["iota"], 1)
            pool.wait_ge(S["tiles"], 1)
            for c in range(VC):
                if c:
                    pool.wait_ge(S["chunk"], c)
                    pool.wait_ge(S["turned"], c)
                pool.indirect_dma_start(rec, None, dram.edges, bass.IndirectOffsetOnAxis(ap=tile_i[:, c:c + 1], axis=0)).then_inc(S["rec"], 16)
                pool.indirect_dma_start(wrec, None, dram.weights, bass.IndirectOffsetOnAxis(ap=tile_i[:, c:c + 1], axis=0)).then_inc(S["wrec"], 16)
                pool.wait_ge(S["rec"], 16 * (c + 1))
                pool.wait_ge(S["wrec"], 16 * (c + 1))

        @block.tensor
        def _(pe):
            for c in range(VC):
                pe.wait_ge(S["before"], c + 1)
                for q in range(VC):
                    last = nc.tensor.matmul(ps[:, c, q:q + 1], before[:, q * P:(q + 1) * P], one16[:, 0:1], start=True, stop=True)
                last.then_inc(S["counted"], 1)
            for c in range(VC):
                pe.wait_ge(S["chunk"], c + 1)
                pe.wait_ge(S["wrec"], 16 * (c + 1))
                pe.wait_ge(S["summed"], 1)
                if c:
                    pe.wait_ge(S["tables"], c)
                for i, a in enumerate([src_f, rel, last_f, et_f, wrec]):
                    last = nc.tensor.transpose(ps[:, i, 0:P], a, m.ident[:, :])
                last.then_inc(S["turned"], 1)

        @block.vector
        def _(dve):
            c_ = Chain(dve, S["dve"])
            nc.vector.memset(one16[:, 0:1], 1.0)
            nc.vector.memset(last_dst, 1 << 20).then_inc(S["preset"], 1)
            dve.wait_ge(S["iota"], 2)
            dve.wait_ge(S["last_dst"], 16 * sum(c * P < NT for c in range(VC)))
            c_.step(nc.vector.tensor_scalar(last_blk, last_dst, 7, None, ALU.arith_shift_right))
            c_.step(nc.vector.tensor_tensor(v_end, last_blk, v_idx, ALU.add))
            for c in range(VC):
                if c:
                    dve.wait_ge(S["counted"], c)
                nc.vector.tensor_scalar(before, v_row, v_end[:, c:c + 1], None, ALU.is_gt).then_inc(S["before"], 1)
            dve.wait_ge(S["counted"], VC)
            c_.step(nc.vector.tensor_copy(t_idx, ps[:, 0, 0:VC]))
            for c in range(1, VC):
                c_.step(nc.vector.tensor_tensor(t_idx, t_idx, ps[:, c, 0:VC], ALU.add))
            nc.vector.tensor_copy(tile_i, t_idx).then_inc(S["tiles"], 1)
            nc.vector.tensor_copy(blk128, t_idx).then_inc(S["summed"], 1)
            c_.step(nc.vector.tensor_tensor(blk, v_idx, t_idx, ALU.subtract))
            c_.step(nc.vector.tensor_scalar(blk, blk, float(NB - 1), None, ALU.min))
            dve.wait_ge(S["summed"], 1)
            c_.step(nc.vector.tensor_scalar(blk128, blk, float(P), None, ALU.mult))
            for c in range(VC):
                dve.wait_ge(S["rec"], 16 * (c + 1))
                if c:
                    dve.wait_ge(S["stored"], c * 16 * (2 + HB))
                    dve.wait_ge(S["turned"], c)
                nc.vector.tensor_copy(src_f, rec[:, 0:P])
                nc.vector.tensor_copy(dst_f, rec[:, P:2 * P])
                nc.vector.tensor_copy(next_f, rec[:, 2 * P:3 * P])
                c_.step(nc.vector.tensor_copy(et_f, rec[:, 3 * P:4 * P]))
                nc.vector.tensor_scalar(dst_s, dst_f, DST_SCALE, None, ALU.mult)
                nc.vector.tensor_tensor(last_f, dst_f, next_f, ALU.not_equal)
                nc.vector.tensor_copy(scal[:, 0:1], dst_f[:, 0:1])
                nc.vector.tensor_copy(scal[:, 1:2], dst_f[:, P - 1:P])
                nc.vector.tensor_copy(scal[:, 3:4], blk[:, c:c + 1])
                c_.step(nc.vector.tensor_scalar(tmp, dst_f, blk128[:, c:c + 1], None, ALU.subtract))
                c_.step(nc.vector.tensor_scalar(in_block, tmp, 0.0, None, ALU.is_ge))
                c_.step(nc.vector.scalar_tensor_tensor(in_block, tmp, float(P - 1), in_block, ALU.is_le, ALU.mult))
                c_.step(nc.vector.tensor_scalar(rel, tmp, -FAR, None, ALU.add))
                c_.step(nc.vector.tensor_tensor(rel, rel, in_block, ALU.mult))
                c_.step(nc.vector.tensor_scalar(rel, rel, FAR, None, ALU.add))
                c_.step(nc.vector.tensor_copy(rel16, rel))
                nc.vector.tensor_copy(scal[:, 2:3], rel[:, 0:1]).then_inc(S["chunk"], 1)
                dve.wait_ge(S["turned"], c + 1)
                for i, t in enumerate(tables):
                    last = nc.vector.tensor_copy(t[:, c * P:(c + 1) * P], ps[:, i, 0:P])
                last.then_inc(S["tables"], 1)
            dve.wait_ge(S["tables"], VC)
            nc.vector.tensor_scalar(m.mask_t[:, :], m.rel_t[:, :], FAR / 2, -BIG, ALU.is_gt, ALU.mult)
            nc.vector.tensor_scalar(m.type0_t[:, :], m.type_t[:, :], 0.0, None, ALU.is_equal).then_inc(S["kept"], 1)
            dve.wait_ge(S["rows"], 16)
            first, lastd, rel0, blkr = (rows[:, a, :] for a in range(4))
            same, cont = both, outs[:, 4, :]
            nc.vector.tensor_copy(m.blocks[:, :], blkr)
            nc.vector.tensor_copy(outs[:, 5, :], rel0)
            nc.vector.memset(cont[:, 0:1], 0.0)
            nc.vector.memset(outs[:, 1, NV - 1:NV], -BIG)
            nc.vector.memset(outs[:, 3, NV - 1:NV], -BIG)
            nc.vector.tensor_tensor(same, first, lastd, ALU.is_equal)
            c_.step(nc.vector.tensor_tensor(cont[:, 1:NV], first[:, 1:NV], lastd[:, 0:NV - 1], ALU.is_equal))
            nc.vector.tensor_tensor(outs[:, 0, :], same, cont, ALU.mult)
            nc.vector.tensor_tensor(outs[:, 1, 0:NV - 1], same[:, 0:NV - 1], cont[:, 1:NV], ALU.mult)
            nc.vector.tensor_scalar(outs[:, 2, :], cont, -1.0, BIG, ALU.add, ALU.mult)
            c_.step(nc.vector.tensor_scalar(outs[:, 3, 0:NV - 1], cont[:, 1:NV], -1.0, BIG, ALU.add, ALU.mult))
            nc.vector.tensor_scalar(outs[:, 0, :], outs[:, 0, :], -1.0, BIG, ALU.add, ALU.mult)
            nc.vector.tensor_scalar(outs[:, 1, 0:NV - 1], outs[:, 1, 0:NV - 1], -1.0, BIG, ALU.add, ALU.mult).then_inc(S["outs"], 1)


class Phase:

    def __init__(self, m, name, heads, table, width, summed, keys, at_scan):
        self.name, self.H, self.R = name, heads, heads * G
        self.table, self.W, self.WS = table, width, summed
        self.keys = keys
        self.dot = name == "attn"
        self.typed = name == "typed"
        self.X = m.arena[:, 0:2 * G * width].rearrange("p (a g w) -> p a g w", a=2, g=G)
        self.tab = m.tabs[:, 0:NB * 3 * keys].rearrange("p (b s k) -> p b s k", b=NB, s=3)
        self.at_scan = at_scan
        self.ahead, self.expand_at = (1, 2) if self.dot else (2, 10)


    def expands(self, g):
        each = 4 if self.dot else 3
        return [i for i in range(each * (g - self.expand_at), each * (g - self.expand_at + 1)) if 0 <= i < G]


def edge_pass(nc, m, dram, ph):
    H, R, X, K = ph.H, ph.R, ph.X, ph.keys
    ps = m.psum
    banks = (0, 1) if ph.dot else (0, 1, 3, 5)
    SB = len(banks)

    def sum_ps(g):
        return ps[:, banks[g % SB], 0:ph.WS]

    exp_ps = ps[:, 2:4, :]
    exp_all = ps[:, 2, 0:G * K].rearrange("p (g k) -> p g k", g=G) if not ph.dot else None
    logit_ps = ps[0:R, 4, 0:P]
    max_ps = ps[:, 4, P:P + R]
    edge_ps = ps[0:H, 6, 0:2 * G].rearrange("p (a g) -> p a g", a=2)
    join_ps = ps[0:R, 6, 64:64 + 2 * G].rearrange("p (a g) -> p a g", a=2)
    grow_ps = ps[:, 7, 0:H]
    logit, shifted = m.logit[:, 0:R], m.shifted[:, 0:R]

    def by_head(ap):
        return ap.rearrange("p (h g) -> p h g", h=H)

    def by_visit(ap):
        return ap.rearrange("p (h g) -> p g h", h=H)

    with ExitStack() as ctx:
        S = Sems(nc, ctx, ph.name)
        block = ctx.enter_context(nc.Block())


        def steps(eng, chain, step):
            chain(0, 0)
            step(0, 0, 2)
            step(1, 1, 2)
            with eng.Fori(1, NBATCH // 2 - 1) as j:
                step(j * 2, 0, 2)
                step(j * 2 + 1, 1, 2)
            step(NBATCH - 2, 0, 1)
            step(NBATCH - 1, 1, 0)

        @block.sync
        def _(sp):
            def load(k, p, half):
                if not (isinstance(k, int) and k < 2):
                    sp.wait_ge(S["onehot_t"], k - 1)
                sp.dma_start(m.rel_row[:, p, :], dram.rel16[bass.ds(k * (G * P), G * P)].rearrange("(a n) -> a n", a=1).to_broadcast([P, G * P])).then_inc(S[f"rel{p}"], 16)
                if not (isinstance(k, int) and k < 2):
                    sp.wait_ge(S["growth"], k - 1)
                sp.dma_start(m.rows[0:H, p, :], dram.rows[bass.ds(k, 1), :, :].rearrange("k a g -> k (a g)").to_broadcast([H, 6 * G])).then_inc(S[f"rows{p}"], 16)
                if not (isinstance(k, int) and k < 2):
                    sp.wait_ge(S["maxes"], k - 1)
                sp.dma_start(m.dst_s[0:R, p, :], dram.dst_s[bass.ds(k, 1), 0:H, :, :].rearrange("k h g e -> (k h g) e")).then_inc(S[f"dst{p}"], 16)

            load(0, 0, 0)
            load(1, 1, 0)
            with sp.Fori(1, NBATCH // 2) as j:
                load(j * 2, 0, j)
                load(j * 2 + 1, 1, j)

        @block.gpsimd
        def _(pool):
            idle = pool.alloc_register(f"{ph.name}_idle")
            pool.reg_mov(idle, 0)

            def gather(k, p, uses):
                first = isinstance(k, int)
                if not first:
                    pool.wait_ge(S[f"gathered{p}"], uses * (16 * G))
                nc.gpsimd.tensor_copy(m.idx[:, p, :], m.src_t[:, bass.ds(k * G, G)]).then_inc(S["indices"], 1)
                pool.wait_ge(S["indices"], k + 1)
                for g in range(G):
                    if not first:
                        wait_apart(pool, S["summed"], (k - 2) * G + (g + 1), idle)
                    pool.indirect_dma_start(X[:, p, g, :], None, ph.table,
                                            bass.IndirectOffsetOnAxis(ap=m.idx[:, p, g:g + 1], axis=0)).then_inc(S[f"gathered{p}"], 16)

            gather(0, 0, 0)
            gather(1, 1, 0)
            with pool.Fori(1, NBATCH // 2) as j:
                gather(j * 2, 0, j)
                gather(j * 2 + 1, 1, j)

        @block.scalar
        def _(act):
            def weigh(k, p):
                act.wait_ge(S["grown"], k + 1)
                nc.scalar.activation(m.shrink[:, 0:H], grow_ps, ACT.Exp).then_inc(S["shrink"], 1)
                act.wait_ge(S["shifted"], k + 1)
                if ph.dot:
                    nc.scalar.activation(m.weight[:, p, 0:G], shifted, ACT.Exp).then_inc(S["weights"], 1)
                    act.wait_ge(S["weights"], k + 1)
                    nc.scalar.activation(m.neg_weight[:, p, 0:G], m.weight[:, p, 0:G], ACT.Copy, scale=-1.0).then_inc(S["neg"], 1)
                    act.wait_ge(S["neg"], k + 1)
                else:
                    nc.scalar.activation(X[:, p, :, D:D + H], by_visit(shifted), ACT.Exp).then_inc(S["weights"], 1)

            def distance(k, p, g):
                if not (isinstance(k, int) and k * G + g < 4):
                    act.wait_ge(S["onehot"], k * G + (g - 3))
                nc.scalar.activation(m.dist[:, g % 4, :], m.iota[:, :], ACT.Abs, scale=-1.0,
                                     bias=m.rel_t[:, bass.ds(k * G + g, 1)]).then_inc(S["distance"], 1)

            def step(k, p, left):
                distance(k, p, 0)
                for g in range(G):
                    if g + 1 < G:
                        distance(k, p, g + 1)
                    act.wait_ge(S["distance"], k * G + (g + 1))
                    if not (isinstance(k, int) and k * G + g < 4):
                        act.wait_ge(S["summed"], k * G + (g - 3))
                    if ph.dot:
                        nc.scalar.activation(m.onehot[:, g % 4, :], m.dist[:, g % 4, :], ACT.Relu,
                                             scale=m.neg_weight[:, p, g:g + 1], bias=m.weight[:, p, g:g + 1]).then_inc(S["onehot"], 1)
                    else:
                        nc.scalar.activation(m.onehot[:, g % 4, :], m.dist[:, g % 4, :], ACT.Relu,
                                             scale=-1.0, bias=m.ones[:, 0:1]).then_inc(S["onehot"], 1)
                if left:
                    weigh(k + 1, 1 - p)

            steps(act, weigh, step)

        @block.tensor
        def _(pe):
            idle = pe.alloc_register(f"{ph.name}_idle_pe")
            pe.reg_mov(idle, 0)

            def blocks_of(k):
                return nc.values_load_multi_w_load_instructions(
                    m.blocks[0:1, bass.ds(k * G, G)], engines=[PE_ENGINE], min_val=0, max_val=NB - 1,
                    skip_runtime_bounds_check_because="visits() keeps them within the blocks")[1]

            def expand(k, p, g, blk):
                out = exp_ps[:, g % 2, 0:K] if ph.dot else exp_all[:, g, :]
                if g == 0:
                    pe.wait_ge(S["onehot_t"], k + 1)
                if ph.dot and not (isinstance(k, int) and k == 0 and g < 2):
                    pe.wait_ge(S["dotted"], k * G + (g - 1))
                for s in range(3):
                    last = nc.tensor.matmul(out, m.onehot_t[:, g, :], ph.tab[:, bass.ds(blk, 1), s, :].rearrange("p a k -> p (a k)"),
                                            start=(s == 0), stop=(s == 2))
                if ph.dot or g == G - 1:
                    last.then_inc(S["expanded"], 1)

            def turn_logits(k):
                wait_apart(pe, S["logits"], k + 1, idle)
                nc.tensor.transpose(logit_ps, logit, m.ident[:, :]).then_inc(S["turned"], 1)

            def edge_values(k):
                wait_apart(pe, S["scanned"], k + 1, idle)
                nc.tensor.matmul(edge_ps, m.head_rows[0:R, 0:H], m.ends[0:R, :, :], start=True, stop=True).then_inc(S["ends"], 1)

            def spread_joined(k):
                wait_apart(pe, S["joined"], k + 1, idle)
                nc.tensor.matmul(join_ps, m.head_rows_t[0:H, 0:R], m.joined[0:H, :, :], start=True, stop=True).then_inc(S["spread"], 1)

            def spread_growth(k):
                wait_apart(pe, S["growth"], k + 1, idle)
                nc.tensor.matmul(grow_ps, m.first_hot[0:H, :], m.growth[0:H, 0:H], start=True, stop=True).then_inc(S["grown"], 1)

            def turn_max(k):
                wait_apart(pe, S["maxes"], k + 1, idle)
                nc.tensor.transpose(max_ps, m.seg_max[0:R, 2, :], m.ident[0:R, 0:R]).then_inc(S["max_turned"], 1)

            def chain(k, p):
                blks = blocks_of(k)
                for g in range(G):
                    expand(k, p, g, blks[g])
                turn_logits(k)
                edge_values(k)
                spread_joined(k)
                turn_max(k)
                spread_growth(k)
                if not ph.dot:
                    blks = blocks_of(k + 1)
                    for g in range(G):
                        expand(k + 1, 1 - p, g, blks[g])

            def step(k, p, left):
                for g in range(G):
                    if left >= ph.ahead:
                        if g == ph.expand_at:
                            blks = blocks_of(k + ph.ahead)
                        for i in ph.expands(g):
                            expand(k + ph.ahead, p if ph.ahead == 2 else 1 - p, i, blks[i])
                    pe.wait_ge(S["onehot"], k * G + (g + 1))
                    if not ph.dot:
                        pe.wait_ge(S["scaled"], k * G + (g + 1))
                    if not (isinstance(k, int) and k * G + g < SB):
                        pe.wait_ge(S["added"], k * G + (g + 1 - SB))
                    nc.tensor.matmul(sum_ps(g), m.onehot[:, g % 4, :], X[:, p, g, 0:ph.WS],
                                     start=True, stop=True).then_inc(S["summed"], 1)
                    if left:
                        if g == ph.at_scan:
                            turn_logits(k + 1)
                        if g == ph.at_scan + 3:
                            edge_values(k + 1)
                        if g == ph.at_scan + 5:
                            spread_joined(k + 1)
                        if g == ph.at_scan + 8:
                            turn_max(k + 1)
                            spread_growth(k + 1)

            steps(pe, chain, step)

        @block.vector
        def _(dve):
            own = S["dve"]
            PER_BATCH = {"gat": 20, "attn": 17, "typed": 23}[ph.name]
            number = {}

            def then(ins, name):
                number[name] = len(number) + 1
                ins.then_inc(own, 1)

            def wait(k, name):
                dve.wait_ge(own, k * PER_BATCH + number[name])

            cols = lambda k: bass.ds(k * G, G)
            raw, both = m.raw[:, 0:R], m.both
            bias, ahead, local = m.seg_bias[0:R, 0, :], m.seg_max[0:R, 0, :], m.seg_max[0:R, 1, :]
            first_b, last_b, tmp = m.seg_tmp[0:R, 0, :], m.seg_tmp[0:R, 1, :], m.seg_tmp[0:R, 2, :]
            back, tot, t = m.back_max[0:H, 0, :], m.joined[0:H, :, :], m.join_tmp[0:H, :, :]

            def fore(p):
                return m.fore_max[0:H, p, :]

            def row(p):
                return m.rows[0:H, p, :].rearrange("h (a g) -> h a g", a=6)

            def transposed_onehot(k, p, j):
                dve.wait_ge(S[f"rel{p}"], (j + 1) * 16)
                nc.vector.tensor_scalar(m.onehot_t[:, :, :].rearrange("p g e -> p (g e)"), m.rel_row[:, p, :],
                                        m.pcol[:, 0:1], None, ALU.is_equal).then_inc(S["onehot_t"], 1)

            def segments(k, p, j):
                number.clear()
                dve.wait_ge(S[f"dst{p}"], (j + 1) * 16)
                dst = m.dst_s[0:R, p, :]
                then(nc.vector.tensor_tensor(bias[:, 1:P], dst[:, 0:P - 1], dst[:, 1:P], ALU.subtract), "segments")
                then(nc.vector.tensor_scalar(first_b, dst, -1.0, dst[:, 0:1], ALU.mult, ALU.add), "first_bias")
                then(nc.vector.tensor_scalar(last_b, dst, dst[:, P - 1:P], None, ALU.subtract), "last_bias")

            def dot(k, p, g, j):
                dve.wait_ge(S["expanded"], k * G + (g + 1))
                if g == 0:
                    dve.wait_ge(S[f"gathered{p}"], (j + 1) * (16 * G))
                nc.vector.tensor_tensor_reduce(out=m.junk[:, g % 2, 0:K], in0=exp_ps[:, g % 2, 0:K], in1=X[:, p, g, 0:K], scale=1.0,
                                               scalar=0.0, op0=ALU.mult, op1=ALU.add,
                                               accum_out=m.raw[:, g:g + 1]).then_inc(S["dotted"], 1)

            def logits_sum(k, p, j):
                dve.wait_ge(S["expanded"], k + 1)
                dve.wait_ge(S[f"gathered{p}"], (j + 1) * (16 * G))
                if ph.typed:
                    then(nc.vector.tensor_tensor(both[:, :, :], X[:, p, :, D:D + 2 * H], exp_all, ALU.add), "both")
                else:
                    then(nc.vector.tensor_tensor(by_visit(raw), X[:, p, :, D:D + H], exp_all, ALU.add), "raw")

            def logits_by_type(k, p, j):
                wait(k, "both")
                then(nc.vector.tensor_tensor(both[:, :, 0:H], both[:, :, 0:H], spread(m.type0_t[:, cols(k)], H), ALU.mult), "type0")
                then(nc.vector.tensor_tensor(both[:, :, H:2 * H], both[:, :, H:2 * H], spread(m.type_t[:, cols(k)], H), ALU.mult), "type1")

            def logits_of_type(k, p, j):
                wait(k, "type1")
                then(nc.vector.tensor_tensor(by_visit(raw), both[:, :, 0:H], both[:, :, H:2 * H], ALU.add), "raw")

            def leaky(k, p, j):
                wait(k, "raw")
                then(nc.vector.scalar_tensor_tensor(raw, raw, 0.2, raw, ALU.mult, ALU.max), "leaky")

            def masked(k, p, j):
                if ph.dot:
                    dve.wait_ge(S["dotted"], (k + 1) * G)
                    nc.vector.tensor_tensor(logit, raw, m.mask_t[:, cols(k)], ALU.add).then_inc(S["logits"], 1)
                else:
                    wait(k, "leaky")
                    mask = m.mask_t[:, cols(k)].unsqueeze(1).to_broadcast([P, H, G])
                    nc.vector.tensor_tensor(by_head(logit), by_head(raw), mask, ALU.add).then_inc(S["logits"], 1)

            def scan_ahead(k, p, j):
                dve.wait_ge(S["turned"], k + 1)
                wait(k, "last_bias")
                then(nc.vector.tensor_tensor_scan(ahead, bias[:, 0:P], logit_ps, -BIG, ALU.add, ALU.max), "ahead")

            def scan_back(k, p, j):
                wait(k, "ahead")
                then(nc.vector.tensor_tensor_scan(local[:, ::-1], bias[:, 1:P + 1][:, ::-1], ahead[:, ::-1], -BIG, ALU.add, ALU.max), "local")

            def ends(k, p, j):
                wait(k, "local")
                then(nc.vector.tensor_scalar(m.ends[0:R, 0, :], m.visit_col[0:R, :], local[:, 0:1], None, ALU.mult), "end0")
                nc.vector.tensor_scalar(m.ends[0:R, 1, :], m.visit_col[0:R, :], local[:, P - 1:P], None, ALU.mult).then_inc(S["scanned"], 1)

            def join_scans(k, p, j):
                dve.wait_ge(S[f"rows{p}"], (j + 1) * 16)
                dve.wait_ge(S["ends"], k + 1)
                then(nc.vector.tensor_tensor_scan(fore(p)[:, 1:G + 1], row(p)[:, 0, :], edge_ps[:, 1, :], fore(p)[:, 0:1], ALU.add, ALU.max), "fore")
                then(nc.vector.tensor_tensor_scan(back[:, 0:G][:, ::-1], row(p)[:, 1, :][:, ::-1], edge_ps[:, 0, :][:, ::-1], -BIG, ALU.add, ALU.max), "back")
                then(nc.vector.tensor_scalar(m.first_hot[0:H, :], m.iota[0:H, :], row(p)[:, 5, 0:1], None, ALU.is_equal), "first_hot")

            def join_others(k, p, j):
                wait(k, "back")
                then(nc.vector.tensor_tensor(t[:, 0, :], fore(p)[:, 0:G], row(p)[:, 2, :], ALU.add), "from_before")
                then(nc.vector.tensor_tensor(t[:, 1, :], back[:, 1:G + 1], row(p)[:, 3, :], ALU.add), "from_behind")

            def joined(k, p, j):
                wait(k, "from_behind")
                then(nc.vector.tensor_tensor(tot[:, 0, :], t[:, 0, :], back[:, 0:G], ALU.max), "joined0")
                nc.vector.tensor_tensor(tot[:, 1, :], t[:, 1, :], fore(p)[:, 1:G + 1], ALU.max).then_inc(S["joined"], 1)

            def carry(k, p, j):
                dve.wait_ge(S["joined"], k + 1)
                then(nc.vector.tensor_copy(m.fore_max[0:H, 1 - p, 0:1], tot[:, 1, G - 1:G]), "carry")
                then(nc.vector.tensor_tensor(m.join_tmp[0:H, 2, 0:1], fore(p)[:, 0:1], tot[:, 0, 0:1], ALU.subtract), "grown")

            def growth(k, p, j):
                wait(k, "grown")
                nc.vector.tensor_scalar(m.growth[0:H, 0:H], m.ident[0:H, 0:H], m.join_tmp[0:H, 2, 0:1], row(p)[:, 4, 0:1],
                                        ALU.mult, ALU.mult).then_inc(S["growth"], 1)

            def end_maxes(k, p, j):
                dve.wait_ge(S["spread"], k + 1)
                for i in range(2):
                    then(nc.vector.tensor_tensor_reduce(out=m.junk[0:R, i, 0:G], in0=join_ps[:, i, :], in1=m.visit_col[0:R, :], scale=1.0,
                                                        scalar=0.0, op0=ALU.mult, op1=ALU.add, accum_out=m.end_max[0:R, i:i + 1]), f"end_max{i}")

            def with_first(k, p, j):
                wait(k, "end_max1")
                then(nc.vector.scalar_tensor_tensor(tmp, first_b, m.end_max[0:R, 0:1], local, ALU.add, ALU.max), "with_first")

            def with_last(k, p, j):
                wait(k, "with_first")
                nc.vector.scalar_tensor_tensor(m.seg_max[0:R, 2, :], last_b, m.end_max[0:R, 1:2], tmp, ALU.add, ALU.max).then_inc(S["maxes"], 1)

            def shift(k, p, j):
                dve.wait_ge(S["max_turned"], k + 1)
                if not ph.dot:
                    last = m.last_t[:, cols(k)]
                    then(nc.vector.tensor_tensor(X[:, p, :, D + H:D + 2 * H], by_visit(max_ps), spread(last, H), ALU.mult), "maximum")
                nc.vector.tensor_tensor(shifted, logit, max_ps, ALU.subtract).then_inc(S["shifted"], 1)

            c = ph.at_scan
            summing = {"gat": [(3, 0, logits_sum), (3, 1, leaky), (4, 0, masked)],
                       "attn": [(5, 1, masked)],
                       "typed": [(2, 1, logits_sum), (3, 0, logits_by_type), (3, 1, logits_of_type), (4, 0, leaky), (4, 1, masked)]}[ph.name]
            softmax = [(0, 1, segments)] + summing + [
                (c, 1, scan_ahead), (c + 1, 0, scan_back), (c + 1, 1, ends),
                (c + 3, 0, join_scans), (c + 3, 1, join_others), (c + 4, 0, joined), (c + 4, 1, carry),
                (c + 5, 0, growth), (c + 5, 1, end_maxes), (c + 6, 0, with_first), (c + 6, 1, with_last), (c + 8, 0, shift)]

            def add(k, p, g, blk):
                dve.wait_ge(S["summed"], k * G + (g + 1))
                if not (isinstance(k, int) and k * G + g == 0):
                    dve.wait_ge(S["added"], k * G + g)
                if g == 0:
                    dve.wait_ge(S["rescaled"], (k + 1) * (2 if not ph.dot else 1))
                row = m.acc[:, bass.ds(blk * WA, ph.WS)]
                nc.vector.tensor_tensor(row, row, sum_ps(g), ALU.add).then_inc(S["added"], 1)

            def rescale(k, p, blk):
                dve.wait_ge(S["shrink"], k + 1)
                if not (isinstance(k, int) and k == 0):
                    dve.wait_ge(S["added"], k * G)
                if ph.dot:
                    row = m.acc[:, bass.ds(blk * WA, ph.WS)]
                    nc.vector.tensor_scalar(row, row, m.shrink[:, 0:1], None, ALU.mult).then_inc(S["rescaled"], 1)
                    return
                row = m.acc[:, bass.ds(blk * WA, D)].rearrange("p (h c) -> p h c", h=H)
                den = m.acc[:, bass.ds(blk * WA + D, H)]
                nc.vector.tensor_tensor(row, row, spread(m.shrink[:, 0:H], D // H), ALU.mult).then_inc(S["rescaled"], 1)
                nc.vector.tensor_tensor(den, den, m.shrink[:, 0:H], ALU.mult).then_inc(S["rescaled"], 1)

            def scale_rows(k, p, g):
                if g == 0:
                    dve.wait_ge(S["weights"], k + 1)
                    if ph.typed:
                        if not (isinstance(k, int) and k == 0):
                            dve.wait_ge(S["scaled"], k * G)
                        nc.vector.tensor_tensor(m.edge_scale[:, :, 0:H], X[:, p, :, D:D + H], spread(m.weight_t[:, bass.ds(k * G, G)], H),
                                                ALU.mult).then_inc(S["edge_scale"], 1)
                        dve.wait_ge(S["edge_scale"], k + 1)
                row = X[:, p, g, 0:D].rearrange("p (h c) -> p h c", h=H)
                w = m.edge_scale[:, g, 0:H] if ph.typed else X[:, p, g, D:D + H]
                nc.vector.tensor_tensor(row, row, spread(w, D // H), ALU.mult).then_inc(S["scaled"], 1)

            def lead(k, p, g, more):
                if ph.dot:
                    return
                if g < G:
                    scale_rows(k, p, g)
                elif more:
                    scale_rows(k + 1, 1 - p, g - G)

            def chain(k, p):
                transposed_onehot(k, p, 0)
                for at, place, part in softmax:
                    part(k, p, 0)
                    if ph.dot and part is segments:
                        for g in range(G):
                            dot(k, p, g, 0)
                assert len(number) == PER_BATCH, number
                if not ph.dot:
                    transposed_onehot(k + 1, 1 - p, 0)
                lead(k, p, 0, True)
                lead(k, p, 1, True)

            def step(k, p, left):
                blks = nc.values_load_multi_w_load_instructions(
                    m.blocks[0:1, bass.ds(k * G, G)], engines=[DVE_ENGINE], min_val=0, max_val=NB - 1,
                    skip_runtime_bounds_check_because="visits() keeps them within the blocks")[1]
                j = (k + 1) // 2
                j2 = (k + 2) // 2
                rescale(k, p, blks[0])

                def between(g, place):
                    for at, there, part in softmax:
                        if left and (at, there) == (g, place):
                            part(k + 1, 1 - p, j)

                for g in range(G):
                    if ph.dot and left and g == 0:
                        transposed_onehot(k + 1, 1 - p, j)
                    if not ph.dot and left == 2 and g == ph.expand_at - 2:
                        transposed_onehot(k + 2, p, j2)
                    lead(k, p, g + 2, left)
                    if left and ph.dot:
                        for i in ph.expands(g):
                            dot(k + 1, 1 - p, i, j)
                    between(g, 0)
                    add(k, p, g, blks[g])
                    between(g, 1)
                if left:
                    assert len(number) == PER_BATCH, number

            nc.vector.memset(m.acc[:, :], 0.0).then_inc(S["cleared"], 1)
            nc.vector.memset(m.fore_max[:, 0, 0:1], -BIG).then_inc(S["cleared"], 1)
            dve.wait_ge(S["cleared"], 2)
            steps(dve, chain, step)


class Space:

    def __init__(self, tensor, at=0):
        self.tensor, self.at = tensor, at

    def take(self, *shape):
        n = 1
        for s in shape:
            n *= s
        ap = self.tensor[:, self.at:self.at + n]
        self.at += n
        assert self.at <= self.tensor.shape[1], self.at
        if len(shape) == 2:
            ap = ap.rearrange("p (a b) -> p a b", a=shape[0])
        if len(shape) == 3:
            ap = ap.rearrange("p (a b c) -> p a b c", a=shape[0], b=shape[1])
        return ap


def node_blocks(eng, *stages):
    lag = len(stages) - 1
    start = lag + 1 if lag % 2 == 0 else lag + 2
    assert (NB - start) % 2 == 0

    def turn(i, p):
        for s, stage in reversed(list(enumerate(stages))):
            b = i - s
            if stage is not None and (not isinstance(b, int) or 0 <= b < NB):
                stage(b, (p - s) % 2)

    for i in range(start):
        turn(i, i % 2)
    with eng.Fori(0, (NB - start) // 2) as j:
        turn(j * 2 + start, start % 2)
        turn(j * 2 + (start + 1), (start + 1) % 2)
    for i in range(NB, NB + lag):
        turn(i, i % 2)


def landed(eng, sem, b, p):
    eng.wait_ge(sem, (b - p) * 8 + 16)


def vacated(eng, sem, b, p):
    if not (isinstance(b, int) and b < 2):
        eng.wait_ge(sem, (b - p) * 8)


def use(eng, sem, b, ahead=0):
    if isinstance(b, int):
        if b - ahead >= 0:
            eng.wait_ge(sem, b - ahead + 1)
    else:
        eng.wait_ge(sem, b + (1 - ahead))


def as_row(v, n=P):
    return v.rearrange("(a n) -> a n", a=1).to_broadcast([n, v.shape[0]])


def rows_of(t, b, width=None):
    return t[bass.ds(b * P, P), 0:(width or t.shape[1])]


def head_mask_into(nc, m, chain, mask, C, heads):
    shift = {64: 6, 32: 5}[C]
    a = m.head_int[:, 0:2 * heads].rearrange("p (c h) -> p c h", c=2)
    chain.step(nc.vector.tensor_scalar(a, a, shift, None, ALU.arith_shift_right))
    chain.step(nc.vector.tensor_scalar(mask, a, 0, None, ALU.is_equal))


def split3(nc, dve, S, tab, value, rest, b, p, tag):
    nc.vector.tensor_copy(tab(0), value).then_inc(S[tag + "_hi"], 1)
    use(dve, S[tag + "_hi"], b)
    nc.vector.tensor_tensor(rest[:, 0], value, tab(0), ALU.subtract).then_inc(S[tag + "_r1"], 1)
    use(dve, S[tag + "_r1"], b)
    nc.vector.tensor_copy(tab(1), rest[:, 0]).then_inc(S[tag + "_mid"], 1)
    use(dve, S[tag + "_mid"], b)
    nc.vector.tensor_tensor(tab(2), rest[:, 0], tab(1), ALU.subtract).then_inc(S[tag + "_lo"], 1)


def prepare_gat(nc, m, args, sp_):
    w = sp_.take(2, W0)
    raw = sp_.take(2, D)
    turned = sp_.take(2, D)
    att = sp_.take(2, 2)
    mask = sp_.take(2, H0)
    att_m = sp_.take(2, 2 * H0)
    ps = m.psum
    with ExitStack() as ctx:
        S = Sems(nc, ctx, "pgat")
        block = ctx.enter_context(nc.Block())

        @block.sync
        def _(sp):
            sp.dma_start(raw, args.gat_W.rearrange("(c p) n -> p c n", p=P)).then_inc(S["load"], 16)
            for i, a in enumerate((args.att_src0, args.att_dst0)):
                sp.dma_start(att[:, :, i], a.rearrange("h k -> (h k)").rearrange("(c p) -> p c", p=P), allow_slow_non_contiguous=True).then_inc(S["load"], 16)
            sp.wait_ge(S["load"], 48)

        @block.gpsimd
        def _(pool):
            nc.gpsimd.iota(m.head_int[:, 0:2 * H0], [[P, 2], [-64, H0]], base=0, channel_multiplier=1).then_inc(S["iota"], 1)

        @block.tensor
        def _(pe):
            pe.wait_ge(S["load"], 48)
            for kc in range(2):
                for cc in range(2):
                    last = nc.tensor.transpose(ps[:, cc, kc * P:(kc + 1) * P], raw[:, kc, cc * P:(cc + 1) * P], m.ident[:, :])
            last.then_inc(S["turned"], 1)
            pe.wait_ge(S["masked"], 1)
            for kc in range(2):
                for cc in range(2):
                    last = nc.tensor.matmul(ps[:, 2, kc * 8:kc * 8 + 8], turned[:, cc, kc * P:(kc + 1) * P], att_m[:, cc, :], start=(cc == 0), stop=(cc == 1))
            last.then_inc(S["logit_w"], 1)

        @block.vector
        def _(dve):
            c = Chain(dve, S["dve"])
            dve.wait_ge(S["iota"], 1)
            head_mask_into(nc, m, c, mask, 64, H0)
            dve.wait_ge(S["load"], 48)
            dve.wait_ge(S["turned"], 1)
            nc.vector.tensor_copy(turned, ps[:, 0:2, 0:D])
            nc.vector.tensor_copy(w[:, :, 0:D], raw)
            for i in range(2):
                for cc in range(2):
                    last = nc.vector.tensor_scalar(att_m[:, cc, i * H0:(i + 1) * H0], mask[:, cc, :], att[:, cc, i:i + 1], None, ALU.mult)
            last.then_inc(S["masked"], 1)
            dve.wait_ge(S["logit_w"], 1)
            nc.vector.tensor_copy(w[:, :, D:W0], ps[:, 2, 0:16].rearrange("p (k j) -> p k j", k=2)).then_inc(S["done"], 1)
    return w


def layernorm_stats(nc, dve, S, x, st, b, idle, tag="ln"):
    nc.vector.bn_stats(st[:, 0:6], x).then_inc(S[tag + "_stats"], 1)
    wait_apart(dve, S[tag + "_stats"], b + 1, idle)
    nc.vector.bn_aggr(st[:, 6:8], st[:, 0:6]).then_inc(S[tag + "_aggr"], 1)
    use(dve, S[tag + "_aggr"], b)
    nc.vector.tensor_scalar(st[:, 8:9], st[:, 7:8], EPS, None, ALU.add).then_inc(S[tag + "_var"], 1)


def inverse_root(nc, pool, S, m, st, b, tag="ln"):
    use(pool, S[tag + "_var"], b)
    nc.gpsimd.tensor_tensor(st[:, 9:10], st[:, 8:9], m.half[:, :], ALU.pow).then_inc(S[tag + "_rstd"], 1)


def nodes_in(nc, m, args, dram, w, sp_):
    x, h, hT, row, st, rest = sp_.take(2, D), sp_.take(2, D), sp_.take(2, D), sp_.take(2, W0), sp_.take(2, 10), sp_.take(2, H0)
    tab = m.tabs[:, 0:NB * 3 * H0].rearrange("p (b s k) -> p b s k", b=NB, s=3)
    ps = m.psum
    with ExitStack() as ctx:
        S = Sems(nc, ctx, "in")
        block = ctx.enter_context(nc.Block())

        @block.sync
        def _(sp):
            def load(b, p):
                use(sp, S["hn"], b, 2)
                sp.dma_start(x[:, p, :], rows_of(args.x, b)).then_inc(S[f"x{p}"], 16)

            node_blocks(sp, load)

        @block.scalar
        def _(act):
            def first(b, p):
                use(act, S["hn"], b)
                use(act, S["turned"], b, 2)
                nc.scalar.activation(h[:, p, :], h[:, p, :], ACT.Relu).then_inc(S["h"], 1)

            def second(b, p):
                use(act, S["turned"], b)
                use(act, S["mm"], b, 2)
                nc.scalar.activation(hT[:, p, :], ps[:, p, 0:D], ACT.Copy).then_inc(S["hT"], 1)
                use(act, S["row"], b)
                act.dma_start(rows_of(dram.t0, b), row[:, p, :]).then_inc(S[f"stored{p}"], 16)

            node_blocks(act, first, second)
            act.wait_ge(S["stored0"], 16 * (NB - NB // 2))
            act.wait_ge(S["stored1"], 16 * (NB // 2))

        @block.gpsimd
        def _(pool):
            def rstd(b, p):
                inverse_root(nc, pool, S, m, st[:, p, :], b)

            node_blocks(pool, rstd)

        @block.tensor
        def _(pe):
            def turn(b, p):
                use(pe, S["h"], b)
                use(pe, S["hT"], b, 2)
                for c in range(2):
                    last = nc.tensor.transpose(ps[:, p, c * P:(c + 1) * P], h[:, p, c * P:(c + 1) * P], m.ident[:, :])
                last.then_inc(S["turned"], 1)

            def project(b, p):
                use(pe, S["hT"], b)
                use(pe, S["row"], b, 2)
                for c in range(2):
                    last = nc.tensor.matmul(ps[:, 2 + p, 0:W0], hT[:, p, c * P:(c + 1) * P], w[:, c, :], start=(c == 0), stop=(c == 1))
                last.then_inc(S["mm"], 1)

            node_blocks(pe, turn, project)

        @block.vector
        def _(dve):
            idle = dve.alloc_register("in_idle")
            dve.reg_mov(idle, 0)

            def normalize(b, p):
                landed(dve, S[f"x{p}"], b, p)
                layernorm_stats(nc, dve, S, x[:, p, :], st[:, p, :], b, idle)
                use(dve, S["ln_rstd"], b)
                use(dve, S["turned"], b, 2)
                nc.vector.tensor_scalar(h[:, p, :], x[:, p, :], st[:, p, 6:7], st[:, p, 9:10], ALU.subtract, ALU.mult).then_inc(S["hn"], 1)

            def finish(b, p):
                use(dve, S["mm"], b)
                vacated(dve, S[f"stored{p}"], b, p)
                nc.vector.tensor_copy(row[:, p, :], ps[:, 2 + p, 0:W0]).then_inc(S["row"], 1)
                use(dve, S["row"], b)
                a = row[:, p, D + H0:W0]
                nc.vector.tensor_copy(m.self_logit[:, bass.ds(b, 1), 0:2 * H0], row[:, p, D:W0].unsqueeze(1)).then_inc(S["self"], 1)
                split3(nc, dve, S, lambda s: tab[:, bass.ds(b, 1), s, :].rearrange("p a k -> p (a k)"), a, rest[:, p:p + 1, :], b, p, "ad")

            node_blocks(dve, normalize, finish)


def acc_rows(m, b, at, n):
    return m.acc[:, bass.ds(b * WA + at, n)]


def by_heads(ap, H):
    return ap.rearrange("p (h c) -> p h c", h=H)


def one(ap):
    return ap.rearrange("p a k -> p (a k)")


def head_factors(nc, m, dram, H, src_at, dst_at, eps, sp_, name):
    keep, own = sp_.take(NB, H), sp_.take(NB, H)
    t = [sp_.take(NB, H) for _ in range(5)]
    acc = m.acc[:, :].rearrange("p (b w) -> p b w", b=NB)
    den, top = acc[:, :, D:D + H], acc[:, :, D + H:D + 2 * H]
    src, dst = m.self_logit[:, :, src_at:src_at + H], m.self_logit[:, :, dst_at:dst_at + H]
    with ExitStack() as ctx:
        S = Sems(nc, ctx, name)
        block = ctx.enter_context(nc.Block())

        @block.scalar
        def _(act):
            act.wait_ge(S["shifted"], 2)
            nc.scalar.activation(t[3], t[1], ACT.Exp).then_inc(S["exp"], 1)
            nc.scalar.activation(t[4], t[2], ACT.Exp).then_inc(S["exp"], 1)

        @block.vector
        def _(dve):
            c = Chain(dve, S["dve"])
            c.step(nc.vector.tensor_tensor(t[0], src, dst, ALU.add))
            c.step(nc.vector.scalar_tensor_tensor(t[0], t[0], 0.2, t[0], ALU.mult, ALU.max))
            c.step(nc.vector.tensor_scalar(t[1], den, 0.5, None, ALU.is_lt))
            c.step(nc.vector.scalar_tensor_tensor(t[1], t[1], -BIG, top, ALU.mult, ALU.add))
            c.step(nc.vector.tensor_tensor(t[2], t[0], t[1], ALU.max))
            nc.vector.tensor_tensor(t[1], t[1], t[2], ALU.subtract).then_inc(S["shifted"], 1)
            dve.wait_ge(S["shifted"], 1)
            nc.vector.tensor_tensor(t[2], t[0], t[2], ALU.subtract).then_inc(S["shifted"], 1)
            dve.wait_ge(S["exp"], 2)
            c.step(nc.vector.tensor_tensor(t[0], den, t[3], ALU.mult))
            c.step(nc.vector.tensor_tensor(t[0], t[0], t[4], ALU.add))
            c.step(nc.vector.tensor_scalar(t[0], t[0], eps, None, ALU.add))
            c.step(nc.vector.reciprocal(t[0], t[0]))
            nc.vector.tensor_tensor(keep, t[3], t[0], ALU.mult)
            c.step(nc.vector.tensor_tensor(own, t[4], t[0], ALU.mult))
    return keep, own


def prepare_attn(nc, m, args, sp_):
    w, wskip = sp_.take(2, WQ), sp_.take(2, D)
    qrow, gat_b, slope, skip_b = sp_.take(WQ), sp_.take(D), sp_.take(D), sp_.take(D)
    at = sp_.at
    wq, wk, wq_t, wk_t = sp_.take(2, D), sp_.take(2, D), sp_.take(2, D), sp_.take(2, WQ)
    bq, bqs = sp_.take(2), sp_.take(2, P)
    ps = m.psum
    with ExitStack() as ctx:
        S = Sems(nc, ctx, "pattn")
        block = ctx.enter_context(nc.Block())

        @block.sync
        def _(sp):
            for t, a in ((wq, args.Wq), (wk, args.Wk), (wskip, args.Wskip)):
                sp.dma_start(t, a.rearrange("(c p) n -> p c n", p=P)).then_inc(S["load"], 16)
            sp.dma_start(bq, args.bq.rearrange("(c p) -> p c", p=P), allow_slow_non_contiguous=True).then_inc(S["load"], 16)
            sp.dma_start(wk_t[:, :, D], args.bk.rearrange("(c p) -> p c", p=P), allow_slow_non_contiguous=True).then_inc(S["load"], 16)
            for t, a in ((gat_b, args.gat_bias), (slope, args.prelu1), (skip_b, args.bskip)):
                sp.dma_start(t, as_row(a)).then_inc(S["load"], 16)
            sp.wait_ge(S["load"], 128)

        @block.tensor
        def _(pe):
            pe.wait_ge(S["load"], 128)
            for i, t in enumerate((wq, wk)):
                for r in range(2):
                    for c in range(2):
                        last = nc.tensor.transpose(ps[:, 2 * i + c, r * P:(r + 1) * P], t[:, r, c * P:(c + 1) * P], m.ident[:, :])
            last.then_inc(S["turned"], 1)
            pe.wait_ge(S["copied"], 1)
            for r in range(2):
                for c in range(2):
                    nc.tensor.matmul(ps[:, 4 + r, 0:WQ], wq_t[:, c, r * P:(r + 1) * P], wk_t[:, c, :], start=(c == 0), stop=(c == 1))
            for c in range(2):
                last = nc.tensor.matmul(ps[:, 6, 0:WQ], bqs[:, c, :], wk_t[:, c, :], start=(c == 0), stop=(c == 1))
            last.then_inc(S["product"], 1)

        @block.vector
        def _(dve):
            nc.vector.memset(wk_t[:, :, D + 1], 0.0)
            dve.wait_ge(S["load"], 128)
            dve.wait_ge(S["turned"], 1)
            nc.vector.tensor_copy(wq_t, ps[:, 0:2, 0:D])
            nc.vector.tensor_copy(wk_t[:, :, 0:D], ps[:, 2:4, 0:D])
            nc.vector.tensor_copy(bqs, spread(bq, P)).then_inc(S["copied"], 1)
            dve.wait_ge(S["product"], 1)
            nc.vector.tensor_scalar(w, ps[:, 4:6, 0:WQ], float(D) ** -0.5, None, ALU.mult)
            nc.vector.tensor_scalar(qrow, ps[:, 6, 0:WQ], float(D) ** -0.5, None, ALU.mult).then_inc(S["done"], 1)
    sp_.at = at
    return w, wskip, qrow, gat_b, slope, skip_b


def prelu(nc, dve, S, b, x, low, slope, out, tag):
    nc.vector.scalar_tensor_tensor(low, x, 0.0, slope, ALU.min, ALU.mult).then_inc(S[tag + "_low"], 1)
    use(dve, S[tag + "_low"], b)
    return nc.vector.scalar_tensor_tensor(out, x, 0.0, low, ALU.max, ALU.add)


def nodes_mid(nc, m, dram, weights, keep, own, sp_):
    w, wskip, qrow, gat_b, slope, skip_b = weights
    h, t1, t2, low = (sp_.take(2, D) for _ in range(4))
    x1 = sp_.take(2, W1)
    xT, q, rest, skip = sp_.take(2, D), sp_.take(2, WQ), sp_.take(2, WQ), sp_.take(2, D)
    tab = m.tabs[:, 0:NB * 3 * WQ].rearrange("p (b s k) -> p b s k", b=NB, s=3)
    ps = m.psum
    with ExitStack() as ctx:
        S = Sems(nc, ctx, "mid")
        block = ctx.enter_context(nc.Block())

        def part(b, s):
            return one(tab[:, bass.ds(b, 1), s, :])

        @block.sync
        def _(sp):
            def load(b, p):
                use(sp, S["own"], b, 2)
                sp.dma_start(h[:, p, :], rows_of(dram.t0, b, D)).then_inc(S[f"h{p}"], 16)

            def store(b, p):
                use(sp, S["skip"], b)
                sp.dma_start(rows_of(dram.skip, b), skip[:, p, :]).then_inc(S[f"skip_stored{p}"], 16)

            node_blocks(sp, load, store)
            sp.wait_ge(S["skip_stored0"], 16 * (NB - NB // 2))
            sp.wait_ge(S["skip_stored1"], 16 * (NB // 2))

        @block.gpsimd
        def _(pool):
            def own_rows(b, p):
                landed(pool, S[f"h{p}"], b, p)
                use(pool, S["joined"], b, 2)
                nc.gpsimd.tensor_tensor(by_heads(t2[:, p, :], H0), by_heads(h[:, p, :], H0), spread(one(own[:, bass.ds(b, 1), :]), D // H0), ALU.mult).then_inc(S["own"], 1)
                use(pool, S["own"], b)
                nc.gpsimd.tensor_tensor(t2[:, p, :], t2[:, p, :], gat_b, ALU.add).then_inc(S["own_bias"], 1)

            node_blocks(pool, own_rows)

        @block.scalar
        def _(act):
            def turned(b, p):
                use(act, S["x1"], b)
                act.dma_start(rows_of(dram.t1, b), x1[:, p, :]).then_inc(S[f"x1_stored{p}"], 16)
                use(act, S["turned"], b)
                use(act, S["projected"], b, 2)
                nc.scalar.activation(xT[:, p, :], ps[:, p, 0:D], ACT.Copy).then_inc(S["xT"], 1)

            def parts(b, p):
                use(act, S["q"], b)
                nc.scalar.activation(part(b, 0), q[:, p, :], ACT.Copy).then_inc(S["hi"], 1)
                use(act, S["rest"], b)
                nc.scalar.activation(part(b, 1), rest[:, p, :], ACT.Copy).then_inc(S["mid"], 1)

            node_blocks(act, turned, parts)
            act.wait_ge(S["x1_stored0"], 16 * (NB - NB // 2))
            act.wait_ge(S["x1_stored1"], 16 * (NB // 2))

        @block.tensor
        def _(pe):
            def turn(b, p):
                use(pe, S["x1"], b)
                use(pe, S["xT"], b, 2)
                for c in range(2):
                    last = nc.tensor.transpose(ps[:, p, c * P:(c + 1) * P], x1[:, p, c * P:(c + 1) * P], m.ident[:, :])
                last.then_inc(S["turned"], 1)

            def project(b, p):
                use(pe, S["xT"], b)
                use(pe, S["q"], b, 2)
                use(pe, S["skip"], b, 2)
                for at, width, ww in ((2, WQ, w), (4, D, wskip)):
                    for c in range(2):
                        last = nc.tensor.matmul(ps[:, at + p, 0:width], xT[:, p, c * P:(c + 1) * P], ww[:, c, :], start=(c == 0), stop=(c == 1))
                last.then_inc(S["projected"], 1)

            node_blocks(pe, turn, project)

        @block.vector
        def _(dve):
            def output(b, p):
                use(dve, S["joined"], b, 2)
                nc.vector.tensor_tensor(by_heads(t1[:, p, :], H0), by_heads(acc_rows(m, b, 0, D), H0), spread(one(keep[:, bass.ds(b, 1), :]), D // H0), ALU.mult).then_inc(S["kept"], 1)
                use(dve, S["kept"], b)
                use(dve, S["own_bias"], b)
                use(dve, S["x1"], b, 2)
                nc.vector.tensor_tensor(t1[:, p, :], t1[:, p, :], t2[:, p, :], ALU.add).then_inc(S["joined"], 1)
                use(dve, S["joined"], b)
                vacated(dve, S[f"x1_stored{p}"], b, p)
                use(dve, S["turned"], b, 2)
                prelu(nc, dve, S, b, t1[:, p, :], low[:, p, :], slope, x1[:, p, 0:D], "p1").then_inc(S["x1"], 1)

            def tables(b, p):
                use(dve, S["projected"], b)
                use(dve, S["lo"], b, 2)
                use(dve, S["mid"], b, 2)
                nc.vector.tensor_tensor(q[:, p, :], ps[:, 2 + p, 0:WQ], qrow, ALU.add).then_inc(S["q"], 1)
                vacated(dve, S[f"skip_stored{p}"], b, p)
                nc.vector.tensor_tensor(skip[:, p, :], ps[:, 4 + p, 0:D], skip_b, ALU.add).then_inc(S["skip"], 1)
                use(dve, S["hi"], b)
                nc.vector.tensor_tensor(rest[:, p, :], q[:, p, :], part(b, 0), ALU.subtract).then_inc(S["rest"], 1)
                use(dve, S["rest"], b)
                use(dve, S["mid"], b)
                nc.vector.tensor_tensor(part(b, 2), rest[:, p, :], part(b, 1), ALU.subtract).then_inc(S["lo"], 1)

            nc.vector.memset(x1[:, :, D:D + 1], 1.0)
            nc.vector.memset(x1[:, :, D + 1:W1], 0.0)
            node_blocks(dve, output, tables)


def prepare_typed(nc, m, args, dram, sp_):
    w, wv = sp_.take(2, W2), sp_.take(2, D)
    bv, slope = sp_.take(D), sp_.take(D)
    per_den, share = sp_.take(NB), sp_.take(NB)
    at = sp_.at
    ws, wd = sp_.take(2, D), sp_.take(2, D)
    att, mask, att_m = sp_.take(2, 4), sp_.take(2, H2), sp_.take(2, 4 * H2)
    acc = m.acc[:, :].rearrange("p (b w) -> p b w", b=NB)
    ps = m.psum
    with ExitStack() as ctx:
        S = Sems(nc, ctx, "ptyped")
        block = ctx.enter_context(nc.Block())

        @block.sync
        def _(sp):
            for t, a in ((ws, args.W_src), (wd, args.W_dst), (wv, args.Wv)):
                sp.dma_start(t, a.rearrange("(c p) n -> p c n", p=P)).then_inc(S["load"], 16)
            for i, a in enumerate((args.att_src1, args.att_dst1)):
                for ty in range(2):
                    sp.dma_start(att[:, :, 2 * i + ty], a[ty, :, :].rearrange("h k -> (h k)").rearrange("(c p) -> p c", p=P),
                                 allow_slow_non_contiguous=True).then_inc(S["load"], 16)
            for t, a in ((bv, args.bv), (slope, args.prelu2)):
                sp.dma_start(t, as_row(a)).then_inc(S["load"], 16)
            for i, t in enumerate((m.last_t, m.type_t, m.type0_t, m.weight_t)):
                sp.dma_start(t[:, :], dram.kept[:, i, :]).then_inc(S["load"], 16)
            sp.wait_ge(S["load"], 208)

        @block.gpsimd
        def _(pool):
            nc.gpsimd.iota(m.head_int[:, 0:2 * H2], [[P, 2], [-32, H2]], base=0, channel_multiplier=1).then_inc(S["iota"], 1)

        @block.tensor
        def _(pe):
            pe.wait_ge(S["load"], 208)
            for r in range(2):
                for c in range(2):
                    nc.tensor.transpose(ps[:, c, r * P:(r + 1) * P], ws[:, r, c * P:(c + 1) * P], m.ident[:, :])
            pe.wait_ge(S["masked"], 1)
            for r in range(2):
                for i, t in enumerate((ws, wd)):
                    for c in range(2):
                        last = nc.tensor.matmul(ps[:, 2 + r, 16 * i:16 * i + 16], t[:, c, r * P:(r + 1) * P], att_m[:, c, 16 * i:16 * i + 16],
                                                start=(c == 0), stop=(c == 1))
            last.then_inc(S["product"], 1)

        @block.vector
        def _(dve):
            c_ = Chain(dve, S["dve"])
            c_.step(nc.vector.tensor_scalar(share, acc[:, :, D], 1e-16, None, ALU.add))
            c_.step(nc.vector.reciprocal(per_den, share))
            c_.step(nc.vector.tensor_tensor(share, per_den, acc[:, :, D], ALU.mult))
            dve.wait_ge(S["iota"], 1)
            head_mask_into(nc, m, c_, mask, 32, H2)
            dve.wait_ge(S["load"], 208)
            for i in range(4):
                for c in range(2):
                    last = nc.vector.tensor_scalar(att_m[:, c, i * H2:(i + 1) * H2], mask[:, c, :], att[:, c, i:i + 1], None, ALU.mult)
            last.then_inc(S["masked"], 1)
            dve.wait_ge(S["product"], 1)
            nc.vector.tensor_copy(w[:, :, 0:D], ps[:, 0:2, 0:D])
            nc.vector.tensor_copy(w[:, :, D:W2], ps[:, 2:4, 0:4 * H2]).then_inc(S["done"], 1)
    sp_.at = at
    return w, wv, bv, slope, per_den, share


def nodes_between(nc, m, args, dram, weights, sp_):
    w, wv, bv, slope, per_den, share = weights
    agg, aggT, y, low, x, x2, h, hT = (sp_.take(2, D) for _ in range(8))
    row, st, rest = sp_.take(2, W2), sp_.take(2, 10), sp_.take(2, 2 * H2)
    tab = m.tabs[:, 0:NB * 3 * 2 * H2].rearrange("p (b s k) -> p b s k", b=NB, s=3)
    ps = m.psum
    with ExitStack() as ctx:
        S = Sems(nc, ctx, "between")
        block = ctx.enter_context(nc.Block())

        @block.sync
        def _(sp):
            def load(b, p):
                use(sp, S["y"], b, 2)
                sp.dma_start(y[:, p, :], rows_of(dram.skip, b)).then_inc(S[f"skip{p}"], 16)
                use(sp, S["x2"], b, 2)
                sp.dma_start(x[:, p, :], rows_of(args.x, b)).then_inc(S[f"x{p}"], 16)

            def store_x(b, p):
                use(sp, S["x2"], b)
                sp.dma_start(rows_of(dram.x2, b), x2[:, p, :]).then_inc(S[f"x2_stored{p}"], 16)
                use(sp, S["h"], b)
                sp.dma_start(rows_of(dram.h1, b), h[:, p, :]).then_inc(S[f"h_stored{p}"], 16)

            def store_row(b, p):
                use(sp, S["row"], b)
                sp.dma_start(rows_of(dram.t2, b), row[:, p, :]).then_inc(S[f"row_stored{p}"], 16)

            node_blocks(sp, load, store_x, store_row)
            for name in ("x2_stored", "h_stored", "row_stored"):
                sp.wait_ge(S[name + "0"], 16 * (NB - NB // 2))
                sp.wait_ge(S[name + "1"], 16 * (NB // 2))

        @block.gpsimd
        def _(pool):
            node_blocks(pool, lambda b, p: inverse_root(nc, pool, S, m, st[:, p, :], b))

        @block.scalar
        def _(act):
            def turned_sum(b, p):
                use(act, S["agg_turned"], b)
                use(act, S["valued"], b, 2)
                nc.scalar.activation(aggT[:, p, :], ps[:, p, 0:D], ACT.Copy).then_inc(S["aggT"], 1)

            def relu(b, p):
                use(act, S["hn"], b)
                nc.scalar.activation(h[:, p, :], h[:, p, :], ACT.Relu).then_inc(S["h"], 1)
                use(act, S["turned"], b)
                use(act, S["projected"], b, 2)
                nc.scalar.activation(hT[:, p, :], ps[:, 4 + p, 0:D], ACT.Copy).then_inc(S["hT"], 1)

            node_blocks(act, turned_sum, relu)

        @block.tensor
        def _(pe):
            def turn_sum(b, p):
                use(pe, S["agg"], b)
                use(pe, S["aggT"], b, 2)
                for c in range(2):
                    last = nc.tensor.transpose(ps[:, p, c * P:(c + 1) * P], agg[:, p, c * P:(c + 1) * P], m.ident[:, :])
                last.then_inc(S["agg_turned"], 1)
                use(pe, S["aggT"], b)
                use(pe, S["y_sum"], b, 2)
                for c in range(2):
                    last = nc.tensor.matmul(ps[:, 2 + p, 0:D], aggT[:, p, c * P:(c + 1) * P], wv[:, c, :], start=(c == 0), stop=(c == 1))
                last.then_inc(S["valued"], 1)

            def turn(b, p):
                use(pe, S["h"], b)
                use(pe, S["hT"], b, 2)
                for c in range(2):
                    last = nc.tensor.transpose(ps[:, 4 + p, c * P:(c + 1) * P], h[:, p, c * P:(c + 1) * P], m.ident[:, :])
                last.then_inc(S["turned"], 1)

            def project(b, p):
                use(pe, S["hT"], b)
                use(pe, S["row"], b, 2)
                for c in range(2):
                    last = nc.tensor.matmul(ps[:, 6 + p, 0:W2], hT[:, p, c * P:(c + 1) * P], w[:, c, :], start=(c == 0), stop=(c == 1))
                last.then_inc(S["projected"], 1)

            node_blocks(pe, turn_sum, turn, project)

        @block.vector
        def _(dve):
            idle = dve.alloc_register("between_idle")
            dve.reg_mov(idle, 0)

            def normalize_sum(b, p):
                use(dve, S["agg_turned"], b, 2)
                nc.vector.tensor_scalar(agg[:, p, :], acc_rows(m, b, 0, D), per_den[:, bass.ds(b, 1)], None, ALU.mult).then_inc(S["agg"], 1)

            def output(b, p):
                landed(dve, S[f"skip{p}"], b, p)
                nc.vector.scalar_tensor_tensor(y[:, p, :], bv, share[:, bass.ds(b, 1)], y[:, p, :], ALU.mult, ALU.add).then_inc(S["y_bias"], 1)
                use(dve, S["y_bias"], b)
                use(dve, S["valued"], b)
                nc.vector.tensor_tensor(y[:, p, :], y[:, p, :], ps[:, 2 + p, 0:D], ALU.add).then_inc(S["y_sum"], 1)
                use(dve, S["y_sum"], b)
                prelu(nc, dve, S, b, y[:, p, :], low[:, p, :], slope, low[:, p, :], "p2").then_inc(S["y"], 1)
                use(dve, S["y"], b)
                landed(dve, S[f"x{p}"], b, p)
                vacated(dve, S[f"x2_stored{p}"], b, p)
                nc.vector.tensor_tensor(x2[:, p, :], x[:, p, :], low[:, p, :], ALU.add).then_inc(S["x2"], 1)
                use(dve, S["x2"], b)
                layernorm_stats(nc, dve, S, x2[:, p, :], st[:, p, :], b, idle)
                use(dve, S["ln_rstd"], b)
                use(dve, S["turned"], b, 2)
                vacated(dve, S[f"h_stored{p}"], b, p)
                nc.vector.tensor_scalar(h[:, p, :], x2[:, p, :], st[:, p, 6:7], st[:, p, 9:10], ALU.subtract, ALU.mult).then_inc(S["hn"], 1)

            def rows(b, p):
                use(dve, S["projected"], b)
                vacated(dve, S[f"row_stored{p}"], b, p)
                nc.vector.tensor_copy(row[:, p, :], ps[:, 6 + p, 0:W2]).then_inc(S["row"], 1)
                use(dve, S["row"], b)
                nc.vector.tensor_copy(m.self_logit[:, bass.ds(b, 1), :], row[:, p, D:W2].unsqueeze(1)).then_inc(S["self"], 1)
                split3(nc, dve, S, lambda s: one(tab[:, bass.ds(b, 1), s, :]), row[:, p, D + 2 * H2:W2], rest[:, p:p + 1, :], b, p, "ad")

            node_blocks(dve, normalize_sum, output, rows)


def prepare_ffn(nc, m, args, sp_):
    ts = Space(m.tabs[:, :].bitcast(F32))
    w1_t, w2_t, raw1, raw2 = ts.take(2, FFN), ts.take(FFN // P, D), ts.take(FFN // P, D), ts.take(2, FFN)
    b1 = sp_.take(FFN // P)
    vectors = {"bias1": args.bias1, "ln1_g": args.ln1_g, "ln1_b": args.ln1_b, "ln2_g": args.ln2_g, "ln2_b": args.ln2_b, "b2": args.b2}
    rows = {n: sp_.take(D) for n in vectors}
    ps = m.psum
    FC = FFN // P
    with ExitStack() as ctx:
        S = Sems(nc, ctx, "pffn")
        block = ctx.enter_context(nc.Block())

        @block.sync
        def _(sp):
            sp.dma_start(raw1, args.W1.rearrange("(f p) n -> p f n", p=P)).then_inc(S["load"], 16)
            sp.dma_start(raw2, args.W2.rearrange("(c p) n -> p c n", p=P)).then_inc(S["load"], 16)
            sp.dma_start(b1, args.b1.rearrange("(f p) -> p f", p=P), allow_slow_non_contiguous=True).then_inc(S["load"], 16)
            for n, vector in vectors.items():
                sp.dma_start(rows[n], as_row(vector)).then_inc(S["load"], 16)
            sp.wait_ge(S["load"], 16 * (3 + len(vectors)))

        @block.tensor
        def _(pe):
            pe.wait_ge(S["load"], 16 * (3 + len(vectors)))
            for f in range(FC):
                for c in range(2):
                    nc.tensor.transpose(ps[:, 2 * c + f // 4, (f % 4) * P:(f % 4 + 1) * P], raw1[:, f, c * P:(c + 1) * P], m.ident[:, :])
                    last = nc.tensor.transpose(ps[:, 4 + f // 2, (f % 2) * D + c * P:(f % 2) * D + (c + 1) * P], raw2[:, c, f * P:(f + 1) * P], m.ident[:, :])
            last.then_inc(S["turned"], 1)

        @block.vector
        def _(dve):
            dve.wait_ge(S["turned"], 1)
            nc.vector.tensor_copy(w1_t.rearrange("p c (a n) -> p (c a) n", a=2), ps[:, 0:4, :])
            nc.vector.tensor_copy(w2_t.rearrange("p (a f) n -> p a (f n)", a=4), ps[:, 4:8, :]).then_inc(S["done"], 1)
    return w1_t, w2_t, b1, rows


def nodes_ffn(nc, m, args, dram, weights, keep, own, sp_):
    w1_t, w2_t, b1, rows = weights
    FC = FFN // P
    more = Space(m.tabs[:, :].bitcast(F32), 4 * 2 * FFN)
    xs, h1, x2, t1, t2, z, u, uT, v, o = (more.take(2, D) for _ in range(10))
    g = more.take(2, FC, P)
    st, st2 = sp_.take(2, 10), sp_.take(2, 10)
    ps = m.psum
    with ExitStack() as ctx:
        S = Sems(nc, ctx, "ffn")
        block = ctx.enter_context(nc.Block())

        @block.sync
        def _(sp):
            def load(b, p):
                use(sp, S["own"], b, 2)
                sp.dma_start(xs[:, p, :], rows_of(dram.t2, b, D)).then_inc(S[f"xs{p}"], 16)
                use(sp, S["own_sum"], b, 2)
                sp.dma_start(h1[:, p, :], rows_of(dram.h1, b)).then_inc(S[f"h{p}"], 16)
                use(sp, S["out"], b, 2)
                sp.dma_start(x2[:, p, :], rows_of(dram.x2, b)).then_inc(S[f"x2{p}"], 16)

            node_blocks(sp, load)

        @block.gpsimd
        def _(pool):
            def own_rows(b, p):
                landed(pool, S[f"xs{p}"], b, p)
                use(pool, S["z"], b, 2)
                nc.gpsimd.tensor_tensor(by_heads(t2[:, p, :], H2), by_heads(xs[:, p, :], H2), spread(one(own[:, bass.ds(b, 1), :]), D // H2), ALU.mult).then_inc(S["own"], 1)
                use(pool, S["own"], b)
                nc.gpsimd.tensor_tensor(t2[:, p, :], t2[:, p, :], rows["bias1"], ALU.add).then_inc(S["own_bias"], 1)
                use(pool, S["own_bias"], b)
                landed(pool, S[f"h{p}"], b, p)
                nc.gpsimd.tensor_tensor(t2[:, p, :], t2[:, p, :], h1[:, p, :], ALU.add).then_inc(S["own_sum"], 1)
                inverse_root(nc, pool, S, m, st[:, p, :], b, "l1")

            def finish(b, p):
                inverse_root(nc, pool, S, m, st2[:, p, :], b, "l2")
                use(pool, S["vn"], b)
                vacated(pool, S[f"out_stored{p}"], b, p)
                nc.gpsimd.tensor_tensor(o[:, p, :], o[:, p, :], rows["ln2_g"], ALU.mult).then_inc(S["out_g"], 1)
                use(pool, S["out_g"], b)
                nc.gpsimd.tensor_tensor(o[:, p, :], o[:, p, :], rows["ln2_b"], ALU.add).then_inc(S["out_b"], 1)
                use(pool, S["out_b"], b)
                landed(pool, S[f"x2{p}"], b, p)
                nc.gpsimd.tensor_tensor(o[:, p, :], o[:, p, :], x2[:, p, :], ALU.add).then_inc(S["out"], 1)

            node_blocks(pool, own_rows, None, finish)

        @block.scalar
        def _(act):
            def turned(b, p):
                use(act, S["turned"], b)
                use(act, S["up"], b, 2)
                nc.scalar.activation(uT[:, p, :], ps[:, p, 0:D], ACT.Copy).then_inc(S["uT"], 1)

            def gelu(b, p):
                use(act, S["up"], b)
                use(act, S["down"], b, 2)
                for f in range(FC):
                    last = nc.scalar.activation(g[:, p, f, :], ps[:, 2 + 2 * p + f // 4, (f % 4) * P:(f % 4 + 1) * P], ACT.Gelu, bias=b1[:, f:f + 1])
                last.then_inc(S["gelu"], 1)

            def store(b, p):
                use(act, S["out"], b)
                act.dma_start(rows_of(args.out, b), o[:, p, :]).then_inc(S[f"out_stored{p}"], 16)

            node_blocks(act, turned, gelu, store)
            act.wait_ge(S["out_stored0"], 16 * (NB - NB // 2))
            act.wait_ge(S["out_stored1"], 16 * (NB // 2))

        @block.tensor
        def _(pe):
            def turn(b, p):
                use(pe, S["u"], b)
                use(pe, S["uT"], b, 2)
                for c in range(2):
                    last = nc.tensor.transpose(ps[:, p, c * P:(c + 1) * P], u[:, p, c * P:(c + 1) * P], m.ident[:, :])
                last.then_inc(S["turned"], 1)

            def up(b, p):
                use(pe, S["uT"], b)
                use(pe, S["gelu"], b, 2)
                for f in range(FC):
                    for c in range(2):
                        last = nc.tensor.matmul(ps[:, 2 + 2 * p + f // 4, (f % 4) * P:(f % 4 + 1) * P], w1_t[:, c, f * P:(f + 1) * P],
                                                uT[:, p, c * P:(c + 1) * P], start=(c == 0), stop=(c == 1))
                last.then_inc(S["up"], 1)

            def down(b, p):
                use(pe, S["gelu"], b)
                use(pe, S["v"], b, 2)
                for f in range(FC):
                    last = nc.tensor.matmul(ps[:, 6 + p, 0:D], g[:, p, f, :], w2_t[:, f, :], start=(f == 0), stop=(f == FC - 1))
                last.then_inc(S["down"], 1)

            node_blocks(pe, turn, up, down)

        @block.vector
        def _(dve):
            idle = dve.alloc_register("ffn_idle")
            dve.reg_mov(idle, 0)

            def attention(b, p):
                use(dve, S["z"], b, 2)
                nc.vector.tensor_tensor(by_heads(t1[:, p, :], H2), by_heads(acc_rows(m, b, 0, D), H2), spread(one(keep[:, bass.ds(b, 1), :]), D // H2), ALU.mult).then_inc(S["kept"], 1)
                use(dve, S["kept"], b)
                use(dve, S["own_sum"], b)
                nc.vector.tensor_tensor(z[:, p, :], t1[:, p, :], t2[:, p, :], ALU.add).then_inc(S["z"], 1)
                use(dve, S["z"], b)
                layernorm_stats(nc, dve, S, z[:, p, :], st[:, p, :], b, idle, "l1")
                use(dve, S["l1_rstd"], b)
                nc.vector.tensor_scalar(z[:, p, :], z[:, p, :], st[:, p, 6:7], st[:, p, 9:10], ALU.subtract, ALU.mult).then_inc(S["zn"], 1)
                use(dve, S["zn"], b)
                use(dve, S["turned"], b, 2)
                use(dve, S["v_sum"], b, 2)
                nc.vector.tensor_tensor(z[:, p, :], z[:, p, :], rows["ln1_g"], ALU.mult).then_inc(S["zg"], 1)
                use(dve, S["zg"], b)
                nc.vector.tensor_tensor(u[:, p, :], z[:, p, :], rows["ln1_b"], ALU.add).then_inc(S["u"], 1)

            def output(b, p):
                use(dve, S["down"], b)
                nc.vector.tensor_tensor(v[:, p, :], ps[:, 6 + p, 0:D], rows["b2"], ALU.add).then_inc(S["v"], 1)
                use(dve, S["v"], b)
                nc.vector.tensor_tensor(v[:, p, :], v[:, p, :], u[:, p, :], ALU.add).then_inc(S["v_sum"], 1)
                use(dve, S["v_sum"], b)
                layernorm_stats(nc, dve, S, v[:, p, :], st2[:, p, :], b, idle, "l2")
                use(dve, S["l2_rstd"], b)
                vacated(dve, S[f"out_stored{p}"], b, p)
                nc.vector.tensor_scalar(o[:, p, :], v[:, p, :], st2[:, p, 6:7], st2[:, p, 9:10], ALU.subtract, ALU.mult).then_inc(S["vn"], 1)

            node_blocks(dve, attention, None, output)


class Held:
    pass


def build_program(nc, x, edges, weights, gat_W, att_src0, att_dst0, gat_bias, prelu1, Wq, bq, Wk, bk, Wv, bv, Wskip, bskip, prelu2,
                  W_src, W_dst, att_src1, att_dst1, bias1, ln1_g, ln1_b, ln2_g, ln2_b, ffn1, b1, ffn2, b2, out):
    args = Held()
    (args.x, args.gat_W, args.att_src0, args.att_dst0, args.gat_bias, args.prelu1) = (x, gat_W, att_src0, att_dst0, gat_bias, prelu1)
    (args.Wq, args.bq, args.Wk, args.bk, args.Wv, args.bv, args.Wskip, args.bskip, args.prelu2) = (Wq, bq, Wk, bk, Wv, bv, Wskip, bskip, prelu2)
    (args.W_src, args.W_dst, args.att_src1, args.att_dst1, args.bias1) = (W_src, W_dst, att_src1, att_dst1, bias1)
    (args.ln1_g, args.ln1_b, args.ln2_g, args.ln2_b, args.W1, args.b1, args.W2, args.b2, args.out) = (ln1_g, ln1_b, ln2_g, ln2_b, ffn1, b1, ffn2, b2, out)
    m, dram = Held(), Held()
    dram.edges, dram.weights = edges, weights
    with ExitStack() as ctx:
        def sb(name, shape, dt=F32):
            return ctx.enter_context(nc.sbuf_tensor(name, shape, dt))

        def dr(name, shape, dt=F32):
            return nc.dram_tensor(name, shape, dt, kind="Internal").ap()

        dram.rel16 = dr("visit_positions", [NV * P], BF16)
        dram.scal = dr("visit_scalars", [4, NV])
        dram.dst_s = dr("visit_dst", [NV // G, HB, G, P])
        dram.rows = dr("batch_rows", [NV // G, 6, G])
        dram.t0 = dr("table_gat", [NP, W0])
        dram.t1 = dr("table_attn", [NP, W1])
        dram.t2 = dr("table_typed", [NP, W2])
        dram.skip = dr("skip_rows", [NP, D])
        dram.x2 = dr("x_after_layer0", [NP, D])
        dram.kept = dr("edge_tables", [P, 4, NV])
        dram.h1 = dr("h_layer1", [NP, D])
        m.arena = sb("arena", [P, 2 * G * W2])
        m.acc = sb("acc", [P, NB * WA])
        m.tabs = sb("tabs", [P, NB * 3 * WQ], BF16)
        m.src_t = sb("src_t", [P, NV], I32)
        m.rel_t, m.mask_t = sb("rel_t", [P, NV]), sb("mask_t", [P, NV])
        rest = Space(m.tabs[:, NB * 3 * 2 * H2:NB * 3 * WQ].bitcast(F32))
        m.last_t, m.type_t, m.type0_t, m.weight_t = (rest.take(NV) for _ in range(4))
        m.self_logit = rest.take(NB, 4 * H2)
        m.blocks = sb("blocks", [1, NV], I32)
        m.iota, m.pcol, m.ident = sb("iota", [P, P]), sb("pcol", [P, 1]), sb("ident", [P, P])
        m.half, m.ones = sb("half", [P, 1]), sb("ones", [P, 1])
        m.ints, m.ints2 = sb("ints", [P, G + HB], I32), sb("ints2", [P, G + HB], I32)
        m.ints_t, m.ints_t2 = sb("ints_t", [HB, P], I32), sb("ints_t2", [HB, P], I32)
        m.visit_col, m.head_rows, m.head_rows_t = sb("visit_col", [P, G]), sb("head_rows", [P, HB]), sb("head_rows_t", [HB, P])
        m.head_int = sb("head_int", [P, 2 * HB], I32)
        m.rel_row = sb("rel_row", [P, 2, G * P], BF16)
        m.onehot_t = sb("onehot_t", [P, G, P], BF16)
        m.onehot, m.dist = sb("onehot", [P, 4, P]), sb("dist", [P, 4, P])
        m.dst_s, m.rows = sb("dst_s", [P, 2, P]), sb("rows", [HB, 2, 6 * G])
        m.seg_bias, m.seg_max, m.seg_tmp = sb("seg_bias", [P, 1, P + 1]), sb("seg_max", [P, 3, P]), sb("seg_tmp", [P, 3, P])
        m.ends, m.end_max = sb("ends", [P, 2, G]), sb("end_max", [P, 2])
        m.fore_max, m.back_max = sb("fore_max", [HB, 2, G + 1]), sb("back_max", [HB, 1, G + 1])
        m.joined, m.join_tmp = sb("joined", [HB, 2, G]), sb("join_tmp", [HB, 3, G])
        m.first_hot, m.growth, m.shrink = sb("first_hot", [HB, P]), sb("growth", [HB, HB]), sb("shrink", [P, HB])
        m.raw, m.logit, m.shifted = sb("raw", [P, P]), sb("logit", [P, P]), sb("shifted", [P, P])
        m.both, m.edge_scale = sb("both", [P, G, 2 * HB]), sb("edge_scale", [P, G, HB])
        m.weight, m.neg_weight = sb("weight", [P, 2, G]), sb("neg_weight", [P, 2, G])
        m.junk = sb("junk", [P, 2, WQ])
        m.idx = sb("idx", [P, 2, G], I32)
        m.psum = ctx.enter_context(nc.psum_tensor("psum", [P, 8, 512], F32))

        constants(nc, m)
        visits(nc, m, dram)
        space = Space(m.arena)
        w = prepare_gat(nc, m, args, space)
        nodes_in(nc, m, args, dram, w, space)
        edge_pass(nc, m, dram, Phase(m, "gat", H0, dram.t0, W0, W0, H0, 5))
        space = Space(m.arena)
        keep, own = head_factors(nc, m, dram, H0, 0, H0, 1e-16, space, "fgat")
        w = prepare_attn(nc, m, args, space)
        nodes_mid(nc, m, dram, w, keep, own, space)
        edge_pass(nc, m, dram, Phase(m, "attn", 1, dram.t1, W1, WQ, WQ, 6))
        space = Space(m.arena)
        w = prepare_typed(nc, m, args, dram, space)
        nodes_between(nc, m, args, dram, w, space)
        edge_pass(nc, m, dram, Phase(m, "typed", H2, dram.t2, W2, WA, 2 * H2, 5))
        space = Space(m.arena)
        keep, own = head_factors(nc, m, dram, H2, 0, 2 * H2, 0.0, space, "ftyped")
        w = prepare_ffn(nc, m, args, space)
        nodes_ffn(nc, m, args, dram, w, keep, own, space)


_INS = ["x", "edges", "weights", "L0_gnn_gat_W", "L0_gnn_att_src", "L0_gnn_att_dst", "L0_gnn_gat_bias", "L0_gnn_prelu1_a",
        "L0_gnn_Wq", "L0_gnn_bq", "L0_gnn_Wk", "L0_gnn_bk", "L0_gnn_Wv", "L0_gnn_bv", "L0_gnn_Wskip", "L0_gnn_bskip",
        "L0_gnn_prelu2_a", "L1_gnn_W_src", "L1_gnn_W_dst", "L1_gnn_att_src", "L1_gnn_att_dst", "L1_gnn_bias", "L1_gnn_ln1_g",
        "L1_gnn_ln1_b", "L1_gnn_ln2_g", "L1_gnn_ln2_b", "L1_gnn_ffn_W1", "L1_gnn_ffn_b1", "L1_gnn_ffn_W2", "L1_gnn_ffn_b2"]


def kernel(**inputs):
    import numpy as _np
    import concourse.bacc as _bacc
    from concourse import mybir as _mybir
    from concourse.bass_utils import run_bass_kernel_spmd as _run

    def tiled(a, fill):
        return _np.concatenate([a, _np.full((NT + 1) * P - a.shape[0], fill, a.dtype)]).reshape(NT + 1, P)

    given = {k: _np.ascontiguousarray(v) for k, v in inputs.items()}
    dst = given["dst"]
    given["edges"] = _np.stack([tiled(given["src"], 0), tiled(dst, PAD_NODE), tiled(dst[1:], PAD_NODE),
                                tiled(given["edge_type_2"], 0)], axis=1).reshape(NT + 1, 4 * P)
    given["weights"] = tiled(given["edge_weight"], 0)
    given["x"] = _np.concatenate([given["x"], _np.zeros((NP - N, D), given["x"].dtype)])

    nc = _bacc.Bacc("TRN2", target_bir_lowering=False, num_devices=1)
    arrays, args = {}, []
    for name in _INS:
        a = _np.ascontiguousarray(given[name])
        arrays[f"in_{name}_dram"] = a
        args.append(nc.dram_tensor(f"in_{name}_dram", a.shape, _mybir.dt.from_np(a.dtype), kind="ExternalInput").ap())
    args.append(nc.dram_tensor("out_0_dram", (NP, D), _mybir.dt.float32, kind="ExternalOutput").ap())
    build_program(nc, *args)
    r = _run(nc, [arrays], core_ids=[0])
    return r.results[0]["out_0_dram"][:N]
```

```python
import concourse.bass as bass
from concourse import mybir
from contextlib import ExitStack

F32 = mybir.dt.float32
I32 = mybir.dt.int32
BF16 = mybir.dt.bfloat16
ALU = mybir.AluOpType
ACT = mybir.ActivationFunctionType
DVE_ENGINE = mybir.EngineType.DVE
PE_ENGINE = mybir.EngineType.PE

P = 128
N = 6250
E = 100000
D = 256
NB = (N + P - 1) // P
NP = NB * P
NT = (E + P - 1) // P
PAD_NODE = NP - 1
G = 16
HALF = G // 2
VISITS = NT + NB - 1
NBATCH = (VISITS + G - 1) // G
assert NBATCH % 2 == 0
VC = (NBATCH * G + P - 1) // P
NV = VC * P
HB = 8
BIG = 1e30
DST_SCALE = 1e30
FAR = 1000.0
H0, H2, FFN = 4, 8, 1024
W0 = D + 2 * H0
W1 = D + 4
W2 = D + 4 * H2
WA = D + 2 * H2
WQ = D + 2
EPS = 1e-5


class Sems:

    def __init__(self, nc, ctx, prefix):
        self.nc, self.prefix, self.made = nc, prefix, {}
        ctx.callback(self.clear)

    def __getitem__(self, name):
        if name not in self.made:
            self.made[name] = self.nc.alloc_semaphore(f"{self.prefix}_{name}")
        return self.made[name]

    def clear(self):
        self.nc.clear_and_free_semaphores(list(self.made.values()))
        self.nc.all_engine_barrier()


class Chain:

    def __init__(self, eng, sem):
        self.eng, self.sem, self.n = eng, sem, 0

    def step(self, ins):
        self.n += 1
        ins.then_inc(self.sem, 1)
        self.eng.wait_ge(self.sem, self.n)


def wait_apart(eng, sem, value, reg):
    if isinstance(value, int):
        eng.wait_ge(sem, value)
    else:
        eng.reg_mov(reg, value)
        eng.wait_ge(sem, 1)
        eng.wait_ge(sem, reg)


def spread(ap, n):
    return ap.unsqueeze(2).to_broadcast([ap.shape[0], ap.shape[1], n])


def constants(nc, m):
    with ExitStack() as ctx:
        S = Sems(nc, ctx, "const")
        block = ctx.enter_context(nc.Block())

        @block.gpsimd
        def _(pool):
            nc.gpsimd.iota(m.iota[:, :], [[1, P]], base=0, channel_multiplier=0,
                           allow_small_or_imprecise_dtypes=True).then_inc(S["iota"], 1)
            nc.gpsimd.iota(m.pcol[:, :], [[0, 1]], base=0, channel_multiplier=1,
                           allow_small_or_imprecise_dtypes=True).then_inc(S["iota"], 1)
            nc.gpsimd.iota(m.ints[:, 0:G], [[-1, G]], base=0, channel_multiplier=1).then_inc(S["iota"], 1)
            nc.gpsimd.iota(m.ints[:, G:G + HB], [[-G, HB]], base=0, channel_multiplier=1).then_inc(S["iota"], 1)
            nc.gpsimd.iota(m.ints_t[:, :], [[1, P]], base=0, channel_multiplier=-G).then_inc(S["iota"], 1)

        @block.vector
        def _(dve):
            c = Chain(dve, S["dve"])
            dve.wait_ge(S["iota"], 5)
            nc.vector.memset(m.half[:, :], -0.5)
            nc.vector.memset(m.ones[:, :], 1.0)
            nc.vector.memset(m.seg_bias[:, :, 0:1], -BIG)
            nc.vector.memset(m.seg_bias[:, :, P:P + 1], -BIG)
            nc.vector.memset(m.back_max[:, :, G:G + 1], -BIG)
            nc.vector.tensor_scalar(m.ident[:, :], m.iota[:, :], m.pcol[:, 0:1], None, ALU.is_equal)
            nc.vector.tensor_scalar(m.ints2[:, 0:G], m.ints[:, 0:G], G - 1, None, ALU.bitwise_and)
            nc.vector.tensor_scalar(m.ints2[:, G:G + HB], m.ints[:, G:G + HB], 4, None, ALU.arith_shift_right)
            c.step(nc.vector.tensor_scalar(m.ints_t2[:, :], m.ints_t[:, :], 4, None, ALU.arith_shift_right))
            nc.vector.tensor_scalar(m.visit_col[:, :], m.ints2[:, 0:G], 0, None, ALU.is_equal)
            nc.vector.tensor_scalar(m.head_rows[:, :], m.ints2[:, G:G + HB], 0, None, ALU.is_equal)
            c.step(nc.vector.tensor_scalar(m.head_rows_t[:, :], m.ints_t2[:, :], 0, None, ALU.is_equal))


def visits(nc, m, dram):
    with ExitStack() as ctx:
        S = Sems(nc, ctx, "meta")
        second = Space(m.arena, 5120)
        rec = [m.arena[:, 0:4 * P].bitcast(I32), second.take(4 * P).bitcast(I32)]
        wrec = [m.arena[:, 512:512 + P], second.take(P)]
        dst_f, src_f, next_f, rel, et_f, last_f = (m.arena[:, 640 + P * i:640 + P * (i + 1)] for i in range(6))
        in_block, tmp = (m.arena[:, 1408 + P * i:1408 + P * (i + 1)] for i in range(2))
        dst_s = [m.arena[:, 1408 + 2 * P:1408 + 3 * P], second.take(P)]
        rel16 = [m.arena[:, 1792:1856].bitcast(BF16), second.take(P // 2).bitcast(BF16)]
        scal = [m.arena[:, 1856:1860], second.take(4)]
        last_dst = m.arena[:, 1860:1860 + VC].bitcast(I32)
        last_blk = m.arena[:, 1868:1868 + VC].bitcast(I32)
        v_end = m.arena[:, 1876:1876 + VC]
        v_idx = m.arena[:, 1884:1884 + VC]
        t_idx = m.arena[:, 1892:1892 + VC]
        blk = m.arena[:, 1900:1900 + VC]
        blk128 = m.arena[:, 1908:1908 + VC]
        tile_i = m.arena[:, 1916:1916 + VC].bitcast(I32)
        before = m.arena[:, 2048:2048 + NV // 2].bitcast(BF16)
        v_row = m.arena[:, 3072:3072 + NV]
        one16 = m.arena[:, 4096:4097].bitcast(BF16)
        rows = m.acc[0:1, 0:4 * NV].rearrange("p (a v) -> p a v", a=4)
        outs = m.acc[0:1, 4 * NV:10 * NV].rearrange("p (a v) -> p a v", a=6)
        both = m.acc[0:1, 10 * NV:11 * NV]
        ps = m.psum
        tables = [m.src_t, m.rel_t, m.last_t, m.type_t, m.weight_t]
        block = ctx.enter_context(nc.Block())

        @block.sync
        def _(sp):
            sp.wait_ge(S["preset"], 1)
            for c in range(VC):
                k = min(P, NT - c * P)
                if k > 0:
                    sp.dma_start(last_dst[0:k, c:c + 1], dram.edges[c * P:c * P + k, 2 * P - 1:2 * P], allow_slow_non_contiguous=True).then_inc(S["last_dst"], 16)
            for c in range(VC):
                sp.wait_ge(S["chunk"], c + 1)
                sp.dma_start(dram.rel16[c * P * P:(c + 1) * P * P].rearrange("(v e) -> v e", e=P), rel16[c % 2]).then_inc(S[f"stored{c % 2}"], 16)
                sp.dma_start(dram.scal[:, c * P:(c + 1) * P].rearrange("a v -> v a"), scal[c % 2], allow_slow_non_contiguous=True).then_inc(S[f"stored{c % 2}"], 16)
                for h in range(HB):
                    sp.dma_start(dram.dst_s[c * (P // G):(c + 1) * (P // G), h, :, :], dst_s[c % 2]).then_inc(S[f"stored{c % 2}"], 16)
            sp.wait_ge(S["kept"], 1)
            for i, t in enumerate((m.last_t, m.type_t, m.type0_t, m.weight_t)):
                sp.dma_start(dram.kept[:, i, :], t[:, :]).then_inc(S["kept_stored"], 16)
            sp.wait_ge(S["kept_stored"], 64)
            sp.wait_ge(S["stored0"], (VC - VC // 2) * 16 * (2 + HB))
            sp.wait_ge(S["stored1"], VC // 2 * 16 * (2 + HB))
            sp.dma_start(rows, dram.scal.rearrange("(p a) v -> p a v", p=1)).then_inc(S["rows"], 16)
            sp.wait_ge(S["outs"], 1)
            for a in range(6):
                sp.dma_start(dram.rows[:, a, :].rearrange("(p k) g -> p k g", p=1),
                             outs[:, a, :].rearrange("p (k g) -> p k g", g=G)).then_inc(S["end"], 16)
            sp.wait_ge(S["end"], 96)

        @block.gpsimd
        def _(pool):
            nc.gpsimd.iota(v_idx, [[P, VC]], base=0, channel_multiplier=1,
                           allow_small_or_imprecise_dtypes=True).then_inc(S["iota"], 1)
            nc.gpsimd.iota(v_row, [[1, NV]], base=0, channel_multiplier=0,
                           allow_small_or_imprecise_dtypes=True).then_inc(S["iota"], 1)
            pool.wait_ge(S["tiles"], 1)
            for c in range(VC):
                if c > 1:
                    pool.wait_ge(S["chunk"], c - 1)
                    pool.wait_ge(S["turned"], c - 1)
                pool.indirect_dma_start(rec[c % 2], None, dram.edges, bass.IndirectOffsetOnAxis(ap=tile_i[:, c:c + 1], axis=0)).then_inc(S["rec"], 16)
                pool.indirect_dma_start(wrec[c % 2], None, dram.weights, bass.IndirectOffsetOnAxis(ap=tile_i[:, c:c + 1], axis=0)).then_inc(S["wrec"], 16)
                pool.wait_ge(S["rec"], 16 * (c + 1))
                pool.wait_ge(S["wrec"], 16 * (c + 1))

        @block.tensor
        def _(pe):
            for c in range(VC):
                pe.wait_ge(S["before"], c + 1)
                for q in range(VC):
                    last = nc.tensor.matmul(ps[:, c, q:q + 1], before[:, q * P:(q + 1) * P], one16[:, 0:1], start=True, stop=True)
                last.then_inc(S["counted"], 1)
            for c in range(VC):
                pe.wait_ge(S["chunk"], c + 1)
                pe.wait_ge(S["wrec"], 16 * (c + 1))
                pe.wait_ge(S["summed"], 1)
                if c:
                    pe.wait_ge(S["tables"], c)
                for i, a in enumerate([src_f, rel, last_f, et_f, wrec[c % 2]]):
                    last = nc.tensor.transpose(ps[:, i, 0:P], a, m.ident[:, :])
                last.then_inc(S["turned"], 1)

        @block.vector
        def _(dve):
            c_ = Chain(dve, S["dve"])
            nc.vector.memset(one16[:, 0:1], 1.0)
            nc.vector.memset(last_dst, 1 << 20).then_inc(S["preset"], 1)
            dve.wait_ge(S["iota"], 2)
            dve.wait_ge(S["last_dst"], 16 * sum(c * P < NT for c in range(VC)))
            c_.step(nc.vector.tensor_scalar(last_blk, last_dst, 7, None, ALU.arith_shift_right))
            c_.step(nc.vector.tensor_tensor(v_end, last_blk, v_idx, ALU.add))
            for c in range(VC):
                if c:
                    dve.wait_ge(S["counted"], c)
                nc.vector.tensor_scalar(before, v_row, v_end[:, c:c + 1], None, ALU.is_gt).then_inc(S["before"], 1)
            dve.wait_ge(S["counted"], VC)
            c_.step(nc.vector.tensor_copy(t_idx, ps[:, 0, 0:VC]))
            for c in range(1, VC):
                c_.step(nc.vector.tensor_tensor(t_idx, t_idx, ps[:, c, 0:VC], ALU.add))
            nc.vector.tensor_copy(tile_i, t_idx).then_inc(S["tiles"], 1)
            nc.vector.tensor_copy(blk128, t_idx).then_inc(S["summed"], 1)
            c_.step(nc.vector.tensor_tensor(blk, v_idx, t_idx, ALU.subtract))
            c_.step(nc.vector.tensor_scalar(blk, blk, float(NB - 1), None, ALU.min))
            dve.wait_ge(S["summed"], 1)
            c_.step(nc.vector.tensor_scalar(blk128, blk, float(P), None, ALU.mult))
            for c in range(VC):
                dve.wait_ge(S["rec"], 16 * (c + 1))
                if c:
                    dve.wait_ge(S["turned"], c)
                if c > 1:
                    dve.wait_ge(S[f"stored{c % 2}"], c // 2 * 16 * (2 + HB))
                nc.vector.tensor_copy(src_f, rec[c % 2][:, 0:P])
                nc.vector.tensor_copy(dst_f, rec[c % 2][:, P:2 * P])
                nc.vector.tensor_copy(next_f, rec[c % 2][:, 2 * P:3 * P])
                c_.step(nc.vector.tensor_copy(et_f, rec[c % 2][:, 3 * P:4 * P]))
                nc.vector.tensor_scalar(dst_s[c % 2], dst_f, DST_SCALE, None, ALU.mult)
                nc.vector.tensor_tensor(last_f, dst_f, next_f, ALU.not_equal)
                nc.vector.tensor_copy(scal[c % 2][:, 0:1], dst_f[:, 0:1])
                nc.vector.tensor_copy(scal[c % 2][:, 1:2], dst_f[:, P - 1:P])
                nc.vector.tensor_copy(scal[c % 2][:, 3:4], blk[:, c:c + 1])
                c_.step(nc.vector.tensor_scalar(tmp, dst_f, blk128[:, c:c + 1], None, ALU.subtract))
                c_.step(nc.vector.tensor_scalar(in_block, tmp, 0.0, None, ALU.is_ge))
                c_.step(nc.vector.scalar_tensor_tensor(in_block, tmp, float(P - 1), in_block, ALU.is_le, ALU.mult))
                c_.step(nc.vector.tensor_scalar(rel, tmp, -FAR, None, ALU.add))
                c_.step(nc.vector.tensor_tensor(rel, rel, in_block, ALU.mult))
                c_.step(nc.vector.tensor_scalar(rel, rel, FAR, None, ALU.add))
                c_.step(nc.vector.tensor_copy(rel16[c % 2], rel))
                nc.vector.tensor_copy(scal[c % 2][:, 2:3], rel[:, 0:1]).then_inc(S["chunk"], 1)
                dve.wait_ge(S["turned"], c + 1)
                for i, t in enumerate(tables):
                    last = nc.vector.tensor_copy(t[:, c * P:(c + 1) * P], ps[:, i, 0:P])
                last.then_inc(S["tables"], 1)
            dve.wait_ge(S["tables"], VC)
            nc.vector.tensor_scalar(m.mask_t[:, :], m.rel_t[:, :], FAR / 2, -BIG, ALU.is_gt, ALU.mult)
            nc.vector.tensor_scalar(m.type0_t[:, :], m.type_t[:, :], 0.0, None, ALU.is_equal).then_inc(S["kept"], 1)
            dve.wait_ge(S["rows"], 16)
            first, lastd, rel0, blkr = (rows[:, a, :] for a in range(4))
            same, cont = both, outs[:, 4, :]
            nc.vector.tensor_copy(m.blocks[:, :], blkr)
            nc.vector.tensor_copy(outs[:, 5, :], rel0)
            nc.vector.memset(cont[:, 0:1], 0.0)
            nc.vector.memset(outs[:, 1, NV - 1:NV], -BIG)
            nc.vector.memset(outs[:, 3, NV - 1:NV], -BIG)
            nc.vector.tensor_tensor(same, first, lastd, ALU.is_equal)
            c_.step(nc.vector.tensor_tensor(cont[:, 1:NV], first[:, 1:NV], lastd[:, 0:NV - 1], ALU.is_equal))
            nc.vector.tensor_tensor(outs[:, 0, :], same, cont, ALU.mult)
            nc.vector.tensor_tensor(outs[:, 1, 0:NV - 1], same[:, 0:NV - 1], cont[:, 1:NV], ALU.mult)
            nc.vector.tensor_scalar(outs[:, 2, :], cont, -1.0, BIG, ALU.add, ALU.mult)
            c_.step(nc.vector.tensor_scalar(outs[:, 3, 0:NV - 1], cont[:, 1:NV], -1.0, BIG, ALU.add, ALU.mult))
            nc.vector.tensor_scalar(outs[:, 0, :], outs[:, 0, :], -1.0, BIG, ALU.add, ALU.mult)
            nc.vector.tensor_scalar(outs[:, 1, 0:NV - 1], outs[:, 1, 0:NV - 1], -1.0, BIG, ALU.add, ALU.mult).then_inc(S["outs"], 1)


class Phase:

    def __init__(self, m, name, heads, table, width, summed, keys, at_scan):
        self.name, self.H, self.R = name, heads, heads * G
        self.table, self.W, self.WS = table, width, summed
        self.keys = keys
        self.dot = name == "attn"
        self.typed = name == "typed"
        self.X = m.arena[:, 0:2 * G * width].rearrange("p (a g w) -> p a g w", a=2, g=G)
        self.tab = m.tabs[:, 0:NB * 3 * keys].rearrange("p (b s k) -> p b s k", b=NB, s=3)
        self.at_scan = at_scan
        self.ahead, self.expand_at = (1, 1) if self.dot else (2, 8)


    def expands(self, g):
        each = 4 if self.dot else 2
        return [i for i in range(each * (g - self.expand_at), each * (g - self.expand_at + 1)) if 0 <= i < G]


def edge_pass(nc, m, dram, ph):
    H, R, X, K = ph.H, ph.R, ph.X, ph.keys
    ps = m.psum
    banks = (0, 1, 7) if ph.dot else (0, 1, 3, 5)
    SB = len(banks)

    def sum_ps(g, p):
        return ps[:, banks[(g + (p if ph.dot else 0)) % SB], 0:ph.WS]

    def visits_since(g, p):
        return SB - 1 if ph.dot and p == 0 and g < 2 else SB

    exp_banks = (2, 3, 5)
    exp_all = ps[:, 2, 0:G * K].rearrange("p (g k) -> p g k", g=G) if not ph.dot else None
    logit_ps = ps[0:R, 4, 0:P]
    max_ps = ps[:, 4, P:P + R]
    edge_ps = ps[0:H, 6, 0:2 * G].rearrange("p (a g) -> p a g", a=2)
    join_ps = ps[0:R, 6, 64:64 + 2 * G].rearrange("p (a g) -> p a g", a=2)
    grow_ps = ps[:, 6, 2 * P:2 * P + H]
    logit, shifted = m.logit[:, 0:R], m.shifted[:, 0:R]

    def by_head(ap):
        return ap.rearrange("p (h g) -> p h g", h=H)

    def by_visit(ap):
        return ap.rearrange("p (h g) -> p g h", h=H)

    with ExitStack() as ctx:
        S = Sems(nc, ctx, ph.name)
        block = ctx.enter_context(nc.Block())


        def steps(eng, chain, step):
            chain(0, 0)
            step(0, 0, 2)
            step(1, 1, 2)
            with eng.Fori(1, NBATCH // 2 - 1) as j:
                step(j * 2, 0, 2)
                step(j * 2 + 1, 1, 2)
            step(NBATCH - 2, 0, 1)
            step(NBATCH - 1, 1, 0)

        @block.sync
        def _(sp):
            def load(k, p, half):
                if not (isinstance(k, int) and k < 2):
                    sp.wait_ge(S["onehot_t"], k - 1)
                sp.dma_start(m.rel_row[:, p, :], dram.rel16[bass.ds(k * (G * P), G * P)].rearrange("(a n) -> a n", a=1).to_broadcast([P, G * P])).then_inc(S[f"rel{p}"], 16)
                if not (isinstance(k, int) and k < 2):
                    sp.wait_ge(S["growth"], k - 1)
                sp.dma_start(m.rows[0:H, p, :], dram.rows[bass.ds(k, 1), :, :].rearrange("k a g -> k (a g)").to_broadcast([H, 6 * G])).then_inc(S[f"rows{p}"], 16)
                if not (isinstance(k, int) and k < 2):
                    sp.wait_ge(S["maxes"], k - 1)
                sp.dma_start(m.dst_s[0:R, p, :], dram.dst_s[bass.ds(k, 1), 0:H, :, :].rearrange("k h g e -> (k h g) e")).then_inc(S[f"dst{p}"], 16)

            load(0, 0, 0)
            load(1, 1, 0)
            with sp.Fori(1, NBATCH // 2) as j:
                load(j * 2, 0, j)
                load(j * 2 + 1, 1, j)

        @block.gpsimd
        def _(pool):
            idle = pool.alloc_register(f"{ph.name}_idle")
            pool.reg_mov(idle, 0)

            def gather(k, p, uses):
                first = isinstance(k, int)
                if not first:
                    for half in range(2):
                        pool.wait_ge(S[f"gathered{p}_{half}"], uses * (16 * HALF))
                nc.gpsimd.tensor_copy(m.idx[:, p, :], m.src_t[:, bass.ds(k * G, G)]).then_inc(S["indices"], 1)
                pool.wait_ge(S["indices"], k + 1)
                for g in range(G):
                    if not first:
                        wait_apart(pool, S["summed"], (k - 2) * G + (g + 1), idle)
                    pool.indirect_dma_start(X[:, p, g, :], None, ph.table,
                                            bass.IndirectOffsetOnAxis(ap=m.idx[:, p, g:g + 1], axis=0)).then_inc(S[f"gathered{p}_{g // HALF}"], 16)

            gather(0, 0, 0)
            gather(1, 1, 0)
            with pool.Fori(1, NBATCH // 2) as j:
                gather(j * 2, 0, j)
                gather(j * 2 + 1, 1, j)

        @block.scalar
        def _(act):
            def weigh(k, p):
                act.wait_ge(S["grown"], k + 1)
                nc.scalar.activation(m.shrink[:, 0:H], grow_ps, ACT.Exp).then_inc(S["shrink"], 1)
                act.wait_ge(S["shifted"], k + 1)
                if ph.dot:
                    nc.scalar.activation(m.weight[:, p, 0:G], shifted, ACT.Exp).then_inc(S["weights"], 1)
                    act.wait_ge(S["weights"], k + 1)
                    nc.scalar.activation(m.neg_weight[:, p, 0:G], m.weight[:, p, 0:G], ACT.Copy, scale=-1.0).then_inc(S["neg"], 1)
                    act.wait_ge(S["neg"], k + 1)
                else:
                    nc.scalar.activation(X[:, p, :, D:D + H], by_visit(shifted), ACT.Exp).then_inc(S["weights"], 1)

            def distance(k, p, g):
                if not (isinstance(k, int) and k * G + g < 4):
                    act.wait_ge(S["onehot"], k * G + (g - 3))
                nc.scalar.activation(m.dist[:, g % 4, :], m.iota[:, :], ACT.Abs, scale=-1.0,
                                     bias=m.rel_t[:, bass.ds(k * G + g, 1)]).then_inc(S["distance"], 1)

            def chain(k, p):
                weigh(k, p)
                for g in range(3):
                    distance(k, p, g)

            def step(k, p, left):
                for g in range(G):
                    if g + 3 < G:
                        distance(k, p, g + 3)
                    elif left:
                        distance(k + 1, 1 - p, g + 3 - G)
                    act.wait_ge(S["distance"], k * G + (g + 1))
                    if not (isinstance(k, int) and k * G + g < 4):
                        act.wait_ge(S["summed"], k * G + (g - 3))
                    if ph.dot:
                        nc.scalar.activation(m.onehot[:, g % 4, :], m.dist[:, g % 4, :], ACT.Relu,
                                             scale=m.neg_weight[:, p, g:g + 1], bias=m.weight[:, p, g:g + 1]).then_inc(S["onehot"], 1)
                    else:
                        nc.scalar.activation(m.onehot[:, g % 4, :], m.dist[:, g % 4, :], ACT.Relu,
                                             scale=-1.0, bias=m.ones[:, 0:1]).then_inc(S["onehot"], 1)
                if left:
                    weigh(k + 1, 1 - p)

            steps(act, chain, step)

        @block.tensor
        def _(pe):
            idle = pe.alloc_register(f"{ph.name}_idle_pe")
            pe.reg_mov(idle, 0)

            def blocks_of(k):
                return nc.values_load_multi_w_load_instructions(
                    m.blocks[0:1, bass.ds(k * G, G)], engines=[PE_ENGINE], min_val=0, max_val=NB - 1,
                    skip_runtime_bounds_check_because="visits() keeps them within the blocks")[1]

            def expand(k, p, g, blk):
                out = ps[:, exp_banks[g % 3], 0:K] if ph.dot else exp_all[:, g, :]
                if g == 0:
                    pe.wait_ge(S["onehot_t"], k + 1)
                if ph.dot and not (isinstance(k, int) and k == 0 and g < 3):
                    pe.wait_ge(S["dotted"], k * G + (g - 2 if g > 2 else 0))
                for s in range(3):
                    last = nc.tensor.matmul(out, m.onehot_t[:, g, :], ph.tab[:, bass.ds(blk, 1), s, :].rearrange("p a k -> p (a k)"),
                                            start=(s == 0), stop=(s == 2))
                if ph.dot or g == G - 1:
                    last.then_inc(S["expanded"], 1)

            def turn_logits(k):
                wait_apart(pe, S["logits"], k + 1, idle)
                nc.tensor.transpose(logit_ps, logit, m.ident[:, :]).then_inc(S["turned"], 1)

            def edge_values(k):
                wait_apart(pe, S["scanned"], k + 1, idle)
                nc.tensor.matmul(edge_ps, m.head_rows[0:R, 0:H], m.ends[0:R, :, :], start=True, stop=True).then_inc(S["ends"], 1)

            def spread_joined(k):
                wait_apart(pe, S["joined"], k + 1, idle)
                nc.tensor.matmul(join_ps, m.head_rows_t[0:H, 0:R], m.joined[0:H, :, :], start=True, stop=True).then_inc(S["spread"], 1)

            def turn_max(k):
                wait_apart(pe, S["maxes"], k + 1, idle)
                nc.tensor.matmul(grow_ps, m.first_hot[0:H, :], m.growth[0:H, 0:H], start=True, stop=True).then_inc(S["grown"], 1)
                nc.tensor.transpose(max_ps, m.seg_max[0:R, 2, :], m.ident[0:R, 0:R]).then_inc(S["max_turned"], 1)

            def chain(k, p):
                blks = blocks_of(k)
                for g in range(G):
                    expand(k, p, g, blks[g])
                turn_logits(k)
                edge_values(k)
                spread_joined(k)
                turn_max(k)
                if not ph.dot:
                    blks = blocks_of(k + 1)
                    for g in range(G):
                        expand(k + 1, 1 - p, g, blks[g])

            def step(k, p, left):
                for g in range(G):
                    if left >= ph.ahead:
                        if g == ph.expand_at:
                            blks = blocks_of(k + ph.ahead)
                        for i in ph.expands(g):
                            expand(k + ph.ahead, p if ph.ahead == 2 else 1 - p, i, blks[i])
                    pe.wait_ge(S["onehot"], k * G + (g + 1))
                    if not ph.dot:
                        pe.wait_ge(S["scaled"], k * G + (g + 1))
                    if not (isinstance(k, int) and k * G + g < SB):
                        pe.wait_ge(S["added"], k * G + (g + 1 - visits_since(g, p)))
                    nc.tensor.matmul(sum_ps(g, p), m.onehot[:, g % 4, :], X[:, p, g, 0:ph.WS],
                                     start=True, stop=True).then_inc(S["summed"], 1)
                    if left:
                        if g == ph.at_scan:
                            turn_logits(k + 1)
                        if g == ph.at_scan + 3:
                            edge_values(k + 1)
                        if g == ph.at_scan + 5:
                            spread_joined(k + 1)
                        if g == ph.at_scan + 8:
                            turn_max(k + 1)

            steps(pe, chain, step)

        @block.vector
        def _(dve):
            own = S["dve"]
            PER_BATCH = {"gat": 20, "attn": 17, "typed": 23}[ph.name]
            number = {}

            def then(ins, name):
                number[name] = len(number) + 1
                ins.then_inc(own, 1)

            def wait(k, name):
                dve.wait_ge(own, k * PER_BATCH + number[name])

            cols = lambda k: bass.ds(k * G, G)
            raw, both = m.raw[:, 0:R], m.both
            bias, ahead, local = m.seg_bias[0:R, 0, :], m.seg_max[0:R, 0, :], m.seg_max[0:R, 1, :]
            first_b, last_b, tmp = m.seg_tmp[0:R, 0, :], m.seg_tmp[0:R, 1, :], m.seg_tmp[0:R, 2, :]
            back, tot, t = m.back_max[0:H, 0, :], m.joined[0:H, :, :], m.join_tmp[0:H, :, :]

            def fore(p):
                return m.fore_max[0:H, p, :]

            def row(p):
                return m.rows[0:H, p, :].rearrange("h (a g) -> h a g", a=6)

            def transposed_onehot(k, p, j):
                dve.wait_ge(S[f"rel{p}"], (j + 1) * 16)
                nc.vector.tensor_scalar(m.onehot_t[:, :, :].rearrange("p g e -> p (g e)"), m.rel_row[:, p, :],
                                        m.pcol[:, 0:1], None, ALU.is_equal).then_inc(S["onehot_t"], 1)

            def segments(k, p, j):
                number.clear()
                dve.wait_ge(S[f"dst{p}"], (j + 1) * 16)
                dst = m.dst_s[0:R, p, :]
                then(nc.vector.tensor_tensor(bias[:, 1:P], dst[:, 0:P - 1], dst[:, 1:P], ALU.subtract), "segments")
                then(nc.vector.tensor_scalar(first_b, dst, -1.0, dst[:, 0:1], ALU.mult, ALU.add), "first_bias")
                then(nc.vector.tensor_scalar(last_b, dst, dst[:, P - 1:P], None, ALU.subtract), "last_bias")

            def dot(k, p, g, j):
                dve.wait_ge(S["expanded"], k * G + (g + 1))
                if g % HALF == 0:
                    dve.wait_ge(S[f"gathered{p}_{g // HALF}"], (j + 1) * (16 * HALF))
                if not (isinstance(k, int) and k == 0 and g < 2):
                    dve.wait_ge(S["dotted"], k * G + (g - 1))
                nc.vector.tensor_tensor_reduce(out=m.junk[:, g % 2, 0:K], in0=ps[:, exp_banks[g % 3], 0:K], in1=X[:, p, g, 0:K], scale=1.0,
                                               scalar=0.0, op0=ALU.mult, op1=ALU.add,
                                               accum_out=m.raw[:, g:g + 1]).then_inc(S["dotted"], 1)

            def logits_sum(k, p, j):
                dve.wait_ge(S["expanded"], k + 1)
                for half in range(2):
                    dve.wait_ge(S[f"gathered{p}_{half}"], (j + 1) * (16 * HALF))
                if ph.typed:
                    then(nc.vector.tensor_tensor(both[:, :, :], X[:, p, :, D:D + 2 * H], exp_all, ALU.add), "both")
                else:
                    then(nc.vector.tensor_tensor(by_visit(raw), X[:, p, :, D:D + H], exp_all, ALU.add), "raw")

            def logits_by_type(k, p, j):
                wait(k, "both")
                then(nc.vector.tensor_tensor(both[:, :, 0:H], both[:, :, 0:H], spread(m.type0_t[:, cols(k)], H), ALU.mult), "type0")
                then(nc.vector.tensor_tensor(both[:, :, H:2 * H], both[:, :, H:2 * H], spread(m.type_t[:, cols(k)], H), ALU.mult), "type1")

            def logits_of_type(k, p, j):
                wait(k, "type1")
                then(nc.vector.tensor_tensor(by_visit(raw), both[:, :, 0:H], both[:, :, H:2 * H], ALU.add), "raw")

            def leaky(k, p, j):
                wait(k, "raw")
                then(nc.vector.scalar_tensor_tensor(raw, raw, 0.2, raw, ALU.mult, ALU.max), "leaky")

            def masked(k, p, j):
                if ph.dot:
                    dve.wait_ge(S["dotted"], (k + 1) * G)
                    nc.vector.tensor_tensor(logit, raw, m.mask_t[:, cols(k)], ALU.add).then_inc(S["logits"], 1)
                else:
                    wait(k, "leaky")
                    mask = m.mask_t[:, cols(k)].unsqueeze(1).to_broadcast([P, H, G])
                    nc.vector.tensor_tensor(by_head(logit), by_head(raw), mask, ALU.add).then_inc(S["logits"], 1)

            def scan_ahead(k, p, j):
                dve.wait_ge(S["turned"], k + 1)
                wait(k, "last_bias")
                then(nc.vector.tensor_tensor_scan(ahead, bias[:, 0:P], logit_ps, -BIG, ALU.add, ALU.max), "ahead")

            def scan_back(k, p, j):
                wait(k, "ahead")
                then(nc.vector.tensor_tensor_scan(local[:, ::-1], bias[:, 1:P + 1][:, ::-1], ahead[:, ::-1], -BIG, ALU.add, ALU.max), "local")

            def ends(k, p, j):
                wait(k, "local")
                then(nc.vector.tensor_scalar(m.ends[0:R, 0, :], m.visit_col[0:R, :], local[:, 0:1], None, ALU.mult), "end0")
                nc.vector.tensor_scalar(m.ends[0:R, 1, :], m.visit_col[0:R, :], local[:, P - 1:P], None, ALU.mult).then_inc(S["scanned"], 1)

            def join_scans(k, p, j):
                dve.wait_ge(S[f"rows{p}"], (j + 1) * 16)
                dve.wait_ge(S["ends"], k + 1)
                then(nc.vector.tensor_tensor_scan(fore(p)[:, 1:G + 1], row(p)[:, 0, :], edge_ps[:, 1, :], fore(p)[:, 0:1], ALU.add, ALU.max), "fore")
                then(nc.vector.tensor_tensor_scan(back[:, 0:G][:, ::-1], row(p)[:, 1, :][:, ::-1], edge_ps[:, 0, :][:, ::-1], -BIG, ALU.add, ALU.max), "back")
                then(nc.vector.tensor_scalar(m.first_hot[0:H, :], m.iota[0:H, :], row(p)[:, 5, 0:1], None, ALU.is_equal), "first_hot")

            def join_others(k, p, j):
                wait(k, "back")
                then(nc.vector.tensor_tensor(t[:, 0, :], fore(p)[:, 0:G], row(p)[:, 2, :], ALU.add), "from_before")
                then(nc.vector.tensor_tensor(t[:, 1, :], back[:, 1:G + 1], row(p)[:, 3, :], ALU.add), "from_behind")

            def joined(k, p, j):
                wait(k, "from_behind")
                then(nc.vector.tensor_tensor(tot[:, 0, :], t[:, 0, :], back[:, 0:G], ALU.max), "joined0")
                nc.vector.tensor_tensor(tot[:, 1, :], t[:, 1, :], fore(p)[:, 1:G + 1], ALU.max).then_inc(S["joined"], 1)

            def carry(k, p, j):
                dve.wait_ge(S["joined"], k + 1)
                then(nc.vector.tensor_copy(m.fore_max[0:H, 1 - p, 0:1], tot[:, 1, G - 1:G]), "carry")
                then(nc.vector.tensor_tensor(m.join_tmp[0:H, 2, 0:1], fore(p)[:, 0:1], tot[:, 0, 0:1], ALU.subtract), "grown")

            def growth(k, p, j):
                wait(k, "grown")
                nc.vector.tensor_scalar(m.growth[0:H, 0:H], m.ident[0:H, 0:H], m.join_tmp[0:H, 2, 0:1], row(p)[:, 4, 0:1],
                                        ALU.mult, ALU.mult).then_inc(S["growth"], 1)

            def end_maxes(k, p, j):
                dve.wait_ge(S["spread"], k + 1)
                for i in range(2):
                    then(nc.vector.tensor_tensor_reduce(out=m.junk[0:R, i, 0:G], in0=join_ps[:, i, :], in1=m.visit_col[0:R, :], scale=1.0,
                                                        scalar=0.0, op0=ALU.mult, op1=ALU.add, accum_out=m.end_max[0:R, i:i + 1]), f"end_max{i}")

            def with_first(k, p, j):
                wait(k, "end_max1")
                then(nc.vector.scalar_tensor_tensor(tmp, first_b, m.end_max[0:R, 0:1], local, ALU.add, ALU.max), "with_first")

            def with_last(k, p, j):
                wait(k, "with_first")
                dve.wait_ge(S["growth"], k + 1)
                nc.vector.scalar_tensor_tensor(m.seg_max[0:R, 2, :], last_b, m.end_max[0:R, 1:2], tmp, ALU.add, ALU.max).then_inc(S["maxes"], 1)

            def shift(k, p, j):
                dve.wait_ge(S["max_turned"], k + 1)
                if not ph.dot:
                    last = m.last_t[:, cols(k)]
                    then(nc.vector.tensor_tensor(X[:, p, :, D + H:D + 2 * H], by_visit(max_ps), spread(last, H), ALU.mult), "maximum")
                nc.vector.tensor_tensor(shifted, logit, max_ps, ALU.subtract).then_inc(S["shifted"], 1)

            c = ph.at_scan
            summing = {"gat": [(3, 0, logits_sum), (3, 1, leaky), (4, 0, masked)],
                       "attn": [(4, 1, masked)],
                       "typed": [(2, 1, logits_sum), (3, 0, logits_by_type), (3, 1, logits_of_type), (4, 0, leaky), (4, 1, masked)]}[ph.name]
            softmax = summing + [
                (c, 1, scan_ahead), (c + 1, 0, scan_back), (c + 1, 1, ends),
                (c + 3, 0, join_scans), (c + 3, 1, join_others), (c + 4, 0, joined), (c + 4, 1, carry),
                (c + 5, 0, growth), (c + 5, 1, end_maxes), (c + 6, 0, with_first), (c + 6, 1, with_last), (c + 8, 0, shift)]

            def add(k, p, g, blk):
                dve.wait_ge(S["summed"], k * G + (g + 1))
                if not (isinstance(k, int) and k * G + g == 0):
                    dve.wait_ge(S["added"], k * G + g)
                if g == 0:
                    dve.wait_ge(S["rescaled"], (k + 1) * (2 if not ph.dot else 1))
                row = m.acc[:, bass.ds(blk * WA, ph.WS)]
                nc.vector.tensor_tensor(row, row, sum_ps(g, p), ALU.add).then_inc(S["added"], 1)

            def rescale(k, p, blk):
                dve.wait_ge(S["shrink"], k + 1)
                if not (isinstance(k, int) and k == 0):
                    dve.wait_ge(S["added"], k * G)
                if ph.dot:
                    row = m.acc[:, bass.ds(blk * WA, ph.WS)]
                    nc.vector.tensor_scalar(row, row, m.shrink[:, 0:1], None, ALU.mult).then_inc(S["rescaled"], 1)
                    return
                row = m.acc[:, bass.ds(blk * WA, D)].rearrange("p (h c) -> p h c", h=H)
                den = m.acc[:, bass.ds(blk * WA + D, H)]
                nc.vector.tensor_tensor(row, row, spread(m.shrink[:, 0:H], D // H), ALU.mult).then_inc(S["rescaled"], 1)
                nc.vector.tensor_tensor(den, den, m.shrink[:, 0:H], ALU.mult).then_inc(S["rescaled"], 1)

            def scale_rows(k, p, g):
                if g == 0:
                    dve.wait_ge(S["weights"], k + 1)
                    if ph.typed:
                        if not (isinstance(k, int) and k == 0):
                            dve.wait_ge(S["scaled"], k * G)
                        nc.vector.tensor_tensor(m.edge_scale[:, :, 0:H], X[:, p, :, D:D + H], spread(m.weight_t[:, bass.ds(k * G, G)], H),
                                                ALU.mult).then_inc(S["edge_scale"], 1)
                        dve.wait_ge(S["edge_scale"], k + 1)
                row = X[:, p, g, 0:D].rearrange("p (h c) -> p h c", h=H)
                w = m.edge_scale[:, g, 0:H] if ph.typed else X[:, p, g, D:D + H]
                nc.vector.tensor_tensor(row, row, spread(w, D // H), ALU.mult).then_inc(S["scaled"], 1)

            def lead(k, p, g, more):
                if ph.dot:
                    return
                if g < G:
                    scale_rows(k, p, g)
                elif more:
                    scale_rows(k + 1, 1 - p, g - G)

            def chain(k, p):
                transposed_onehot(k, p, 0)
                segments(k, p, 0)
                if ph.dot:
                    for g in range(G):
                        dot(k, p, g, 0)
                for at, place, part in softmax:
                    part(k, p, 0)
                assert len(number) == PER_BATCH, number
                if not ph.dot:
                    transposed_onehot(k + 1, 1 - p, 0)
                lead(k, p, 0, True)
                lead(k, p, 1, True)

            def step(k, p, left):
                j = (k + 1) // 2
                j2 = (k + 2) // 2
                lead(k, p, 2, left)
                if left:
                    if ph.dot:
                        transposed_onehot(k + 1, 1 - p, j)
                    segments(k + 1, 1 - p, j)
                blks = nc.values_load_multi_w_load_instructions(
                    m.blocks[0:1, bass.ds(k * G, G)], engines=[DVE_ENGINE], min_val=0, max_val=NB - 1,
                    skip_runtime_bounds_check_because="visits() keeps them within the blocks")[1]
                rescale(k, p, blks[0])

                def between(g, place):
                    for at, there, part in softmax:
                        if left and (at, there) == (g, place):
                            part(k + 1, 1 - p, j)

                for g in range(G):
                    if not ph.dot and left == 2 and g == ph.expand_at - 2:
                        transposed_onehot(k + 2, p, j2)
                    if g:
                        lead(k, p, g + 2, left)
                    if left and ph.dot:
                        for i in ph.expands(g):
                            dot(k + 1, 1 - p, i, j)
                    between(g, 0)
                    add(k, p, g, blks[g])
                    between(g, 1)
                if left:
                    assert len(number) == PER_BATCH, number

            nc.vector.memset(m.acc[:, :], 0.0).then_inc(S["cleared"], 1)
            nc.vector.memset(m.fore_max[:, 0, 0:1], -BIG).then_inc(S["cleared"], 1)
            dve.wait_ge(S["cleared"], 2)
            steps(dve, chain, step)


class Space:

    def __init__(self, tensor, at=0):
        self.tensor, self.at = tensor, at

    def take(self, *shape):
        n = 1
        for s in shape:
            n *= s
        ap = self.tensor[:, self.at:self.at + n]
        self.at += n
        assert self.at <= self.tensor.shape[1], self.at
        if len(shape) == 2:
            ap = ap.rearrange("p (a b) -> p a b", a=shape[0])
        if len(shape) == 3:
            ap = ap.rearrange("p (a b c) -> p a b c", a=shape[0], b=shape[1])
        return ap


U = 4


def node_blocks(eng, *stages):
    last = max(lag for lag, _ in stages)
    start = last + U
    start += (NB - start) % U

    def turn(i, r):
        for lag, stage in stages:
            b = i - lag
            if not isinstance(b, int) or 0 <= b < NB:
                stage(b, (r - lag) % U)

    for i in range(start):
        turn(i, i)
    with eng.Fori(0, (NB - start) // U) as j:
        for r in range(start, start + U):
            turn(j * U + r, r)
    for i in range(NB, NB + last):
        turn(i, i)


def landed(eng, sem, b, p):
    eng.wait_ge(sem, (b - p) * (16 // U) + 16)


def vacated(eng, sem, b, p, buffers=U):
    if not (isinstance(b, int) and b < buffers):
        eng.wait_ge(sem, (b - p) * (16 // buffers))


def all_landed(eng, S, name):
    for p in range(U):
        eng.wait_ge(S[f"{name}{p}"], 16 * ((NB - p + U - 1) // U))


def use(eng, sem, b, ahead=0):
    if isinstance(b, int):
        if b - ahead >= 0:
            eng.wait_ge(sem, b - ahead + 1)
    else:
        eng.wait_ge(sem, b + (1 - ahead))


def as_row(v, n=P):
    return v.rearrange("(a n) -> a n", a=1).to_broadcast([n, v.shape[0]])


def rows_of(t, b, width=None):
    return t[bass.ds(b * P, P), 0:(width or t.shape[1])]


def head_mask_into(nc, m, chain, mask, C, heads):
    shift = {64: 6, 32: 5}[C]
    a = m.head_int[:, 0:2 * heads].rearrange("p (c h) -> p c h", c=2)
    chain.step(nc.vector.tensor_scalar(a, a, shift, None, ALU.arith_shift_right))
    chain.step(nc.vector.tensor_scalar(mask, a, 0, None, ALU.is_equal))


def split3(c, nc, part, value, rest):
    c.step(nc.vector.tensor_copy(part(0), value))
    c.step(nc.vector.tensor_tensor(rest, value, part(0), ALU.subtract))
    c.step(nc.vector.tensor_copy(part(1), rest))
    c.step(nc.vector.tensor_tensor(part(2), rest, part(1), ALU.subtract))


def prepare_gat(nc, m, args, sp_):
    w = sp_.take(2, W0)
    raw = sp_.take(2, D)
    turned = sp_.take(2, D)
    att = sp_.take(2, 2)
    mask = sp_.take(2, H0)
    att_m = sp_.take(2, 2 * H0)
    ps = m.psum
    with ExitStack() as ctx:
        S = Sems(nc, ctx, "pgat")
        block = ctx.enter_context(nc.Block())

        @block.sync
        def _(sp):
            sp.dma_start(raw, args.gat_W.rearrange("(c p) n -> p c n", p=P)).then_inc(S["load"], 16)
            for i, a in enumerate((args.att_src0, args.att_dst0)):
                sp.dma_start(att[:, :, i], a.rearrange("h k -> (h k)").rearrange("(c p) -> p c", p=P), allow_slow_non_contiguous=True).then_inc(S["load"], 16)
            sp.wait_ge(S["load"], 48)

        @block.gpsimd
        def _(pool):
            nc.gpsimd.iota(m.head_int[:, 0:2 * H0], [[P, 2], [-64, H0]], base=0, channel_multiplier=1).then_inc(S["iota"], 1)

        @block.tensor
        def _(pe):
            pe.wait_ge(S["load"], 48)
            for kc in range(2):
                for cc in range(2):
                    last = nc.tensor.transpose(ps[:, cc, kc * P:(kc + 1) * P], raw[:, kc, cc * P:(cc + 1) * P], m.ident[:, :])
            last.then_inc(S["turned"], 1)
            pe.wait_ge(S["masked"], 1)
            for kc in range(2):
                for cc in range(2):
                    last = nc.tensor.matmul(ps[:, 2, kc * 8:kc * 8 + 8], turned[:, cc, kc * P:(kc + 1) * P], att_m[:, cc, :], start=(cc == 0), stop=(cc == 1))
            last.then_inc(S["logit_w"], 1)

        @block.vector
        def _(dve):
            c = Chain(dve, S["dve"])
            dve.wait_ge(S["iota"], 1)
            head_mask_into(nc, m, c, mask, 64, H0)
            dve.wait_ge(S["load"], 48)
            dve.wait_ge(S["turned"], 1)
            nc.vector.tensor_copy(turned, ps[:, 0:2, 0:D])
            nc.vector.tensor_copy(w[:, :, 0:D], raw)
            for i in range(2):
                for cc in range(2):
                    last = nc.vector.tensor_scalar(att_m[:, cc, i * H0:(i + 1) * H0], mask[:, cc, :], att[:, cc, i:i + 1], None, ALU.mult)
            last.then_inc(S["masked"], 1)
            dve.wait_ge(S["logit_w"], 1)
            nc.vector.tensor_copy(w[:, :, D:W0], ps[:, 2, 0:16].rearrange("p (k j) -> p k j", k=2)).then_inc(S["done"], 1)
    return w


def layernorm_stats(nc, dve, S, x, st, b, idle, tag="ln"):
    nc.vector.bn_stats(st[:, 0:6], x).then_inc(S[tag + "_stats"], 1)
    wait_apart(dve, S[tag + "_stats"], b + 1, idle)
    nc.vector.bn_aggr(st[:, 6:8], st[:, 0:6]).then_inc(S[tag + "_aggr"], 1)
    use(dve, S[tag + "_aggr"], b)
    nc.vector.tensor_scalar(st[:, 8:9], st[:, 7:8], EPS, None, ALU.add).then_inc(S[tag + "_var"], 1)


def inverse_root(nc, pool, S, m, st, b, tag="ln"):
    use(pool, S[tag + "_var"], b)
    nc.gpsimd.tensor_tensor(st[:, 9:10], st[:, 8:9], m.half[:, :], ALU.pow).then_inc(S[tag + "_rstd"], 1)


def nodes_in(nc, m, args, dram, w, sp_):
    x, h, hT, row, st, rest = sp_.take(U, D), sp_.take(U, D), sp_.take(2, D), sp_.take(U, W0), sp_.take(U, 10), sp_.take(NB, H0)
    tab = m.tabs[:, 0:NB * 3 * H0].rearrange("p (b s k) -> p b s k", b=NB, s=3)
    ps = m.psum
    with ExitStack() as ctx:
        S = Sems(nc, ctx, "in")
        block = ctx.enter_context(nc.Block())

        @block.sync
        def _(sp):
            def load(b, p):
                use(sp, S["hn"], b, U)
                sp.dma_start(x[:, p, :], rows_of(args.x, b)).then_inc(S[f"x{p}"], 16)

            node_blocks(sp, (0, load))

        @block.scalar
        def _(act):
            def relu(b, p):
                use(act, S["turned"], b)
                use(act, S["mm"], b, 2)
                nc.scalar.activation(hT[:, p % 2, :], ps[:, p % 2, 0:D], ACT.Relu).then_inc(S["hT"], 1)

            def copy_row(b, p):
                use(act, S["mm"], b)
                vacated(act, S[f"stored{p}"], b, p)
                use(act, S["self"], b, U)
                nc.scalar.activation(row[:, p, :], ps[:, 2 + p % 2, 0:W0], ACT.Copy).then_inc(S["row"], 1)

            def store(b, p):
                use(act, S["row"], b)
                act.dma_start(rows_of(dram.t0, b), row[:, p, :]).then_inc(S[f"stored{p}"], 16)

            node_blocks(act, (2, store), (1, copy_row), (0, relu))
            all_landed(act, S, "stored")

        @block.gpsimd
        def _(pool):
            node_blocks(pool, (0, lambda b, p: inverse_root(nc, pool, S, m, st[:, p, :], b)))

        @block.tensor
        def _(pe):
            def turn(b, p):
                use(pe, S["hn"], b)
                use(pe, S["hT"], b, 2)
                for c in range(2):
                    last = nc.tensor.transpose(ps[:, p % 2, c * P:(c + 1) * P], h[:, p, c * P:(c + 1) * P], m.ident[:, :])
                last.then_inc(S["turned"], 1)

            def project(b, p):
                use(pe, S["hT"], b)
                use(pe, S["row"], b, 2)
                for c in range(2):
                    last = nc.tensor.matmul(ps[:, 2 + p % 2, 0:W0], hT[:, p % 2, c * P:(c + 1) * P], w[:, c, :], start=(c == 0), stop=(c == 1))
                last.then_inc(S["mm"], 1)

            node_blocks(pe, (1, project), (0, turn))

        @block.vector
        def _(dve):
            idle = dve.alloc_register("in_idle")

            def stats(b, p):
                landed(dve, S[f"x{p}"], b, p)
                layernorm_stats(nc, dve, S, x[:, p, :], st[:, p, :], b, idle)

            def normalize(b, p):
                use(dve, S["ln_rstd"], b)
                use(dve, S["turned"], b, U)
                nc.vector.tensor_scalar(h[:, p, :], x[:, p, :], st[:, p, 6:7], st[:, p, 9:10], ALU.subtract, ALU.mult).then_inc(S["hn"], 1)

            def own_logits(b, p):
                use(dve, S["row"], b)
                nc.vector.tensor_copy(m.self_logit[:, bass.ds(b, 1), 0:2 * H0], row[:, p, D:W0].unsqueeze(1)).then_inc(S["self"], 1)

            node_blocks(dve, (5, own_logits), (1, normalize), (0, stats))
            c = Chain(dve, S["dve"])
            dve.wait_ge(S["self"], NB)
            split3(c, nc, lambda s: tab[:, :, s, :], m.self_logit[:, :, H0:2 * H0], rest)


def acc_rows(m, b, at, n):
    return m.acc[:, bass.ds(b * WA + at, n)]


def by_heads(ap, H):
    return ap.rearrange("p (h c) -> p h c", h=H)


def one(ap):
    return ap.rearrange("p a k -> p (a k)")


def head_factors(nc, m, dram, H, src_at, dst_at, eps, sp_, name):
    keep, own = sp_.take(NB, H), sp_.take(NB, H)
    at = sp_.at
    t = [sp_.take(NB, H) for _ in range(5)]
    sp_.at = at
    acc = m.acc[:, :].rearrange("p (b w) -> p b w", b=NB)
    den, top = acc[:, :, D:D + H], acc[:, :, D + H:D + 2 * H]
    src, dst = m.self_logit[:, :, src_at:src_at + H], m.self_logit[:, :, dst_at:dst_at + H]
    with ExitStack() as ctx:
        S = Sems(nc, ctx, name)
        block = ctx.enter_context(nc.Block())

        @block.scalar
        def _(act):
            act.wait_ge(S["shifted"], 2)
            nc.scalar.activation(t[3], t[1], ACT.Exp).then_inc(S["exp"], 1)
            nc.scalar.activation(t[4], t[2], ACT.Exp).then_inc(S["exp"], 1)

        @block.vector
        def _(dve):
            c = Chain(dve, S["dve"])
            c.step(nc.vector.tensor_tensor(t[0], src, dst, ALU.add))
            c.step(nc.vector.scalar_tensor_tensor(t[0], t[0], 0.2, t[0], ALU.mult, ALU.max))
            c.step(nc.vector.tensor_scalar(t[1], den, 0.5, None, ALU.is_lt))
            c.step(nc.vector.scalar_tensor_tensor(t[1], t[1], -BIG, top, ALU.mult, ALU.add))
            c.step(nc.vector.tensor_tensor(t[2], t[0], t[1], ALU.max))
            nc.vector.tensor_tensor(t[1], t[1], t[2], ALU.subtract).then_inc(S["shifted"], 1)
            dve.wait_ge(S["shifted"], 1)
            nc.vector.tensor_tensor(t[2], t[0], t[2], ALU.subtract).then_inc(S["shifted"], 1)
            dve.wait_ge(S["exp"], 2)
            c.step(nc.vector.tensor_tensor(t[0], den, t[3], ALU.mult))
            c.step(nc.vector.tensor_tensor(t[0], t[0], t[4], ALU.add))
            c.step(nc.vector.tensor_scalar(t[0], t[0], eps, None, ALU.add))
            c.step(nc.vector.reciprocal(t[0], t[0]))
            nc.vector.tensor_tensor(keep, t[3], t[0], ALU.mult)
            c.step(nc.vector.tensor_tensor(own, t[4], t[0], ALU.mult))
    return keep, own


def prepare_attn(nc, m, args, sp_):
    w, wskip = sp_.take(2, WQ), sp_.take(2, D)
    qrow, gat_b, slope, skip_b = sp_.take(WQ), sp_.take(D), sp_.take(D), sp_.take(D)
    at = sp_.at
    wq, wk, wq_t, wk_t = sp_.take(2, D), sp_.take(2, D), sp_.take(2, D), sp_.take(2, WQ)
    bq, bqs = sp_.take(2), sp_.take(2, P)
    ps = m.psum
    with ExitStack() as ctx:
        S = Sems(nc, ctx, "pattn")
        block = ctx.enter_context(nc.Block())

        @block.sync
        def _(sp):
            for t, a in ((wq, args.Wq), (wk, args.Wk), (wskip, args.Wskip)):
                sp.dma_start(t, a.rearrange("(c p) n -> p c n", p=P)).then_inc(S["load"], 16)
            sp.dma_start(bq, args.bq.rearrange("(c p) -> p c", p=P), allow_slow_non_contiguous=True).then_inc(S["load"], 16)
            sp.dma_start(wk_t[:, :, D], args.bk.rearrange("(c p) -> p c", p=P), allow_slow_non_contiguous=True).then_inc(S["load"], 16)
            for t, a in ((gat_b, args.gat_bias), (slope, args.prelu1), (skip_b, args.bskip)):
                sp.dma_start(t, as_row(a)).then_inc(S["load"], 16)
            sp.wait_ge(S["load"], 128)

        @block.tensor
        def _(pe):
            pe.wait_ge(S["load"], 128)
            for i, t in enumerate((wq, wk)):
                for r in range(2):
                    for c in range(2):
                        last = nc.tensor.transpose(ps[:, 2 * i + c, r * P:(r + 1) * P], t[:, r, c * P:(c + 1) * P], m.ident[:, :])
            last.then_inc(S["turned"], 1)
            pe.wait_ge(S["copied"], 1)
            for r in range(2):
                for c in range(2):
                    nc.tensor.matmul(ps[:, 4 + r, 0:WQ], wq_t[:, c, r * P:(r + 1) * P], wk_t[:, c, :], start=(c == 0), stop=(c == 1))
            for c in range(2):
                last = nc.tensor.matmul(ps[:, 6, 0:WQ], bqs[:, c, :], wk_t[:, c, :], start=(c == 0), stop=(c == 1))
            last.then_inc(S["product"], 1)

        @block.vector
        def _(dve):
            nc.vector.memset(wk_t[:, :, D + 1], 0.0)
            dve.wait_ge(S["load"], 128)
            dve.wait_ge(S["turned"], 1)
            nc.vector.tensor_copy(wq_t, ps[:, 0:2, 0:D])
            nc.vector.tensor_copy(wk_t[:, :, 0:D], ps[:, 2:4, 0:D])
            nc.vector.tensor_copy(bqs, spread(bq, P)).then_inc(S["copied"], 1)
            dve.wait_ge(S["product"], 1)
            nc.vector.tensor_scalar(w, ps[:, 4:6, 0:WQ], float(D) ** -0.5, None, ALU.mult)
            nc.vector.tensor_scalar(qrow, ps[:, 6, 0:WQ], float(D) ** -0.5, None, ALU.mult).then_inc(S["done"], 1)
    sp_.at = at
    return w, wskip, qrow, gat_b, slope, skip_b


def prelu(nc, dve, S, b, x, low, slope, out, tag):
    nc.vector.scalar_tensor_tensor(low, x, 0.0, slope, ALU.min, ALU.mult).then_inc(S[tag + "_low"], 1)
    use(dve, S[tag + "_low"], b)
    return nc.vector.scalar_tensor_tensor(out, x, 0.0, low, ALU.max, ALU.add)


def nodes_mid(nc, m, dram, weights, keep, own, sp_):
    w, wskip, qrow, gat_b, slope, skip_b = weights
    h, t1, x1, skip = sp_.take(U, D), sp_.take(U, D), sp_.take(U, W1), sp_.take(U, D)
    t2, low, xT, q, rest = sp_.take(2, D), sp_.take(2, D), sp_.take(2, D), sp_.take(2, WQ), sp_.take(2, WQ)
    tab = m.tabs[:, 0:NB * 3 * WQ].rearrange("p (b s k) -> p b s k", b=NB, s=3)
    ps = m.psum
    with ExitStack() as ctx:
        S = Sems(nc, ctx, "mid")
        block = ctx.enter_context(nc.Block())

        def part(b, s):
            return one(tab[:, bass.ds(b, 1), s, :])

        @block.sync
        def _(sp):
            def load(b, p):
                use(sp, S["own"], b, U)
                sp.dma_start(h[:, p, :], rows_of(dram.t0, b, D)).then_inc(S[f"h{p}"], 16)

            node_blocks(sp, (0, load))

        @block.gpsimd
        def _(pool):
            def own_rows(b, p):
                landed(pool, S[f"h{p}"], b, p)
                use(pool, S["joined"], b, 2)
                nc.gpsimd.tensor_tensor(by_heads(t2[:, p % 2, :], H0), by_heads(h[:, p, :], H0), spread(one(own[:, bass.ds(b, 1), :]), D // H0), ALU.mult).then_inc(S["own"], 1)
                use(pool, S["own"], b)
                nc.gpsimd.tensor_tensor(t2[:, p % 2, :], t2[:, p % 2, :], gat_b, ALU.add).then_inc(S["own_bias"], 1)

            node_blocks(pool, (0, own_rows))

        @block.scalar
        def _(act):
            def turned(b, p):
                use(act, S["x1"], b)
                act.dma_start(rows_of(dram.t1, b), x1[:, p, :]).then_inc(S[f"x1_stored{p}"], 16)
                use(act, S["turned"], b)
                use(act, S["projected"], b, 2)
                nc.scalar.activation(xT[:, p % 2, :], ps[:, p % 2, 0:D], ACT.Copy).then_inc(S["xT"], 1)

            def high(b, p):
                use(act, S["skip"], b)
                act.dma_start(rows_of(dram.skip, b), skip[:, p, :]).then_inc(S[f"skip_stored{p}"], 16)
                use(act, S["q"], b)
                nc.scalar.activation(part(b, 0), q[:, p % 2, :], ACT.Copy).then_inc(S["hi"], 1)

            def middle(b, p):
                use(act, S["rest"], b)
                nc.scalar.activation(part(b, 1), rest[:, p % 2, :], ACT.Copy).then_inc(S["mid"], 1)

            node_blocks(act, (3, middle), (2, high), (0, turned))
            all_landed(act, S, "x1_stored")
            all_landed(act, S, "skip_stored")

        @block.tensor
        def _(pe):
            def turn(b, p):
                use(pe, S["x1"], b)
                use(pe, S["xT"], b, 2)
                for c in range(2):
                    last = nc.tensor.transpose(ps[:, p % 2, c * P:(c + 1) * P], x1[:, p, c * P:(c + 1) * P], m.ident[:, :])
                last.then_inc(S["turned"], 1)

            def project(b, p):
                use(pe, S["xT"], b)
                use(pe, S["q"], b, 2)
                use(pe, S["skip"], b, 2)
                for at, width, ww in ((2, WQ, w), (4, D, wskip)):
                    for c in range(2):
                        last = nc.tensor.matmul(ps[:, at + p % 2, 0:width], xT[:, p % 2, c * P:(c + 1) * P], ww[:, c, :], start=(c == 0), stop=(c == 1))
                last.then_inc(S["projected"], 1)

            node_blocks(pe, (1, project), (0, turn))

        @block.vector
        def _(dve):
            def output(b, p):
                use(dve, S["x1"], b, U)
                nc.vector.tensor_tensor(by_heads(t1[:, p, :], H0), by_heads(acc_rows(m, b, 0, D), H0), spread(one(keep[:, bass.ds(b, 1), :]), D // H0), ALU.mult).then_inc(S["kept"], 1)
                use(dve, S["kept"], b)
                use(dve, S["own_bias"], b)
                nc.vector.tensor_tensor(t1[:, p, :], t1[:, p, :], t2[:, p % 2, :], ALU.add).then_inc(S["joined"], 1)

            def activate(b, p):
                use(dve, S["joined"], b)
                vacated(dve, S[f"x1_stored{p}"], b, p)
                use(dve, S["turned"], b, U)
                use(dve, S["x1"], b, 1)
                prelu(nc, dve, S, b, t1[:, p, :], low[:, p % 2, :], slope, x1[:, p, 0:D], "p1").then_inc(S["x1"], 1)

            def biased(b, p):
                use(dve, S["projected"], b)
                use(dve, S["hi"], b, 2)
                use(dve, S["rest"], b, 2)
                nc.vector.tensor_tensor(q[:, p % 2, :], ps[:, 2 + p % 2, 0:WQ], qrow, ALU.add).then_inc(S["q"], 1)
                vacated(dve, S[f"skip_stored{p}"], b, p)
                nc.vector.tensor_tensor(skip[:, p, :], ps[:, 4 + p % 2, 0:D], skip_b, ALU.add).then_inc(S["skip"], 1)

            def less_high(b, p):
                use(dve, S["hi"], b)
                use(dve, S["mid"], b, 2)
                use(dve, S["lo"], b, 2)
                nc.vector.tensor_tensor(rest[:, p % 2, :], q[:, p % 2, :], part(b, 0), ALU.subtract).then_inc(S["rest"], 1)

            def low_part(b, p):
                use(dve, S["mid"], b)
                nc.vector.tensor_tensor(part(b, 2), rest[:, p % 2, :], part(b, 1), ALU.subtract).then_inc(S["lo"], 1)

            nc.vector.memset(x1[:, :, D:D + 1], 1.0)
            nc.vector.memset(x1[:, :, D + 1:W1], 0.0)
            node_blocks(dve, (5, low_part), (4, less_high), (3, biased), (1, activate), (0, output))


def prepare_typed(nc, m, args, dram, sp_):
    w, wv = sp_.take(2, W2), sp_.take(2, D)
    bv, slope = sp_.take(D), sp_.take(D)
    per_den, share = sp_.take(NB), sp_.take(NB)
    at = sp_.at
    ws, wd = sp_.take(2, D), sp_.take(2, D)
    att, mask, att_m = sp_.take(2, 4), sp_.take(2, H2), sp_.take(2, 4 * H2)
    acc = m.acc[:, :].rearrange("p (b w) -> p b w", b=NB)
    ps = m.psum
    with ExitStack() as ctx:
        S = Sems(nc, ctx, "ptyped")
        block = ctx.enter_context(nc.Block())

        @block.sync
        def _(sp):
            for t, a in ((ws, args.W_src), (wd, args.W_dst), (wv, args.Wv)):
                sp.dma_start(t, a.rearrange("(c p) n -> p c n", p=P)).then_inc(S["load"], 16)
            for i, a in enumerate((args.att_src1, args.att_dst1)):
                for ty in range(2):
                    sp.dma_start(att[:, :, 2 * i + ty], a[ty, :, :].rearrange("h k -> (h k)").rearrange("(c p) -> p c", p=P),
                                 allow_slow_non_contiguous=True).then_inc(S["load"], 16)
            for t, a in ((bv, args.bv), (slope, args.prelu2)):
                sp.dma_start(t, as_row(a)).then_inc(S["load"], 16)
            for i, t in enumerate((m.last_t, m.type_t, m.type0_t, m.weight_t)):
                sp.dma_start(t[:, :], dram.kept[:, i, :]).then_inc(S["load"], 16)
            sp.wait_ge(S["load"], 208)

        @block.gpsimd
        def _(pool):
            nc.gpsimd.iota(m.head_int[:, 0:2 * H2], [[P, 2], [-32, H2]], base=0, channel_multiplier=1).then_inc(S["iota"], 1)

        @block.tensor
        def _(pe):
            pe.wait_ge(S["load"], 208)
            for r in range(2):
                for c in range(2):
                    nc.tensor.transpose(ps[:, c, r * P:(r + 1) * P], ws[:, r, c * P:(c + 1) * P], m.ident[:, :])
            pe.wait_ge(S["masked"], 1)
            for r in range(2):
                for i, t in enumerate((ws, wd)):
                    for c in range(2):
                        last = nc.tensor.matmul(ps[:, 2 + r, 16 * i:16 * i + 16], t[:, c, r * P:(r + 1) * P], att_m[:, c, 16 * i:16 * i + 16],
                                                start=(c == 0), stop=(c == 1))
            last.then_inc(S["product"], 1)

        @block.vector
        def _(dve):
            c_ = Chain(dve, S["dve"])
            c_.step(nc.vector.tensor_scalar(share, acc[:, :, D], 1e-16, None, ALU.add))
            c_.step(nc.vector.reciprocal(per_den, share))
            c_.step(nc.vector.tensor_tensor(share, per_den, acc[:, :, D], ALU.mult))
            dve.wait_ge(S["iota"], 1)
            head_mask_into(nc, m, c_, mask, 32, H2)
            dve.wait_ge(S["load"], 208)
            for i in range(4):
                for c in range(2):
                    last = nc.vector.tensor_scalar(att_m[:, c, i * H2:(i + 1) * H2], mask[:, c, :], att[:, c, i:i + 1], None, ALU.mult)
            last.then_inc(S["masked"], 1)
            dve.wait_ge(S["product"], 1)
            nc.vector.tensor_copy(w[:, :, 0:D], ps[:, 0:2, 0:D])
            nc.vector.tensor_copy(w[:, :, D:W2], ps[:, 2:4, 0:4 * H2]).then_inc(S["done"], 1)
    sp_.at = at
    return w, wv, bv, slope, per_den, share


def nodes_between(nc, m, args, dram, weights, sp_):
    w, wv, bv, slope, per_den, share = weights
    y, x, x2, h = (sp_.take(U, D) for _ in range(4))
    agg, aggT, low, hn, hT = (sp_.take(2, D) for _ in range(5))
    row, st = sp_.take(2, W2), sp_.take(U, 10)
    rest = m.acc[:, 0:NB * 2 * H2].rearrange("p (b k) -> p b k", b=NB)
    tab = m.tabs[:, 0:NB * 3 * 2 * H2].rearrange("p (b s k) -> p b s k", b=NB, s=3)
    ps = m.psum
    with ExitStack() as ctx:
        S = Sems(nc, ctx, "between")
        block = ctx.enter_context(nc.Block())

        @block.sync
        def _(sp):
            def load(b, p):
                use(sp, S["y"], b, U)
                sp.dma_start(y[:, p, :], rows_of(dram.skip, b)).then_inc(S[f"skip_loaded{p}"], 16)
                use(sp, S["x2"], b, U)
                sp.dma_start(x[:, p, :], rows_of(args.x, b)).then_inc(S[f"x_loaded{p}"], 16)

            node_blocks(sp, (0, load))

        @block.gpsimd
        def _(pool):
            def rstd(b, p):
                use(pool, S["x2"], b)
                pool.dma_start(rows_of(dram.x2, b), x2[:, p, :]).then_inc(S[f"x2_stored{p}"], 16)
                inverse_root(nc, pool, S, m, st[:, p, :], b)

            node_blocks(pool, (0, rstd))
            all_landed(pool, S, "x2_stored")

        @block.scalar
        def _(act):
            def normalize_sum(b, p):
                use(act, S["agg_turned"], b, 2)
                nc.scalar.activation(agg[:, p % 2, :], acc_rows(m, b, 0, D), ACT.Copy, scale=per_den[:, bass.ds(b, 1)]).then_inc(S["agg"], 1)

            def turned_sum(b, p):
                use(act, S["agg_turned"], b)
                use(act, S["valued"], b, 2)
                nc.scalar.activation(aggT[:, p % 2, :], ps[:, p % 2, 0:D], ACT.Copy).then_inc(S["aggT"], 1)

            def relu(b, p):
                use(act, S["hn"], b)
                vacated(act, S[f"h_stored{p}"], b, p)
                nc.scalar.activation(h[:, p, :], hn[:, p % 2, :], ACT.Relu).then_inc(S["h"], 1)

            def turned(b, p):
                use(act, S["turned"], b)
                use(act, S["projected"], b, 2)
                nc.scalar.activation(hT[:, p % 2, :], ps[:, 4 + p % 2, 0:D], ACT.Relu).then_inc(S["hT"], 1)
                use(act, S["h"], b)
                act.dma_start(rows_of(dram.h1, b), h[:, p, :]).then_inc(S[f"h_stored{p}"], 16)

            def copy_row(b, p):
                use(act, S["projected"], b)
                vacated(act, S[f"row_stored{p % 2}"], b, p % 2, 2)
                use(act, S["self"], b, 2)
                nc.scalar.activation(row[:, p % 2, :], ps[:, 6 + p % 2, 0:W2], ACT.Copy).then_inc(S["row"], 1)

            def store(b, p):
                use(act, S["row"], b)
                act.dma_start(rows_of(dram.t2, b), row[:, p % 2, :]).then_inc(S[f"row_stored{p % 2}"], 16)

            node_blocks(act, (9, store), (8, copy_row), (7, turned), (6, relu), (1, turned_sum), (0, normalize_sum))
            all_landed(act, S, "h_stored")
            act.wait_ge(S["row_stored0"], 16 * (NB - NB // 2))
            act.wait_ge(S["row_stored1"], 16 * (NB // 2))

        @block.tensor
        def _(pe):
            def turn_sum(b, p):
                use(pe, S["agg"], b)
                use(pe, S["aggT"], b, 2)
                for c in range(2):
                    last = nc.tensor.transpose(ps[:, p % 2, c * P:(c + 1) * P], agg[:, p % 2, c * P:(c + 1) * P], m.ident[:, :])
                last.then_inc(S["agg_turned"], 1)

            def values(b, p):
                use(pe, S["aggT"], b)
                use(pe, S["y_sum"], b, 2)
                for c in range(2):
                    last = nc.tensor.matmul(ps[:, 2 + p % 2, 0:D], aggT[:, p % 2, c * P:(c + 1) * P], wv[:, c, :], start=(c == 0), stop=(c == 1))
                last.then_inc(S["valued"], 1)

            def turn(b, p):
                use(pe, S["hn"], b)
                use(pe, S["hT"], b, 2)
                for c in range(2):
                    last = nc.tensor.transpose(ps[:, 4 + p % 2, c * P:(c + 1) * P], hn[:, p % 2, c * P:(c + 1) * P], m.ident[:, :])
                last.then_inc(S["turned"], 1)

            def project(b, p):
                use(pe, S["hT"], b)
                use(pe, S["row"], b, 2)
                for c in range(2):
                    last = nc.tensor.matmul(ps[:, 6 + p % 2, 0:W2], hT[:, p % 2, c * P:(c + 1) * P], w[:, c, :], start=(c == 0), stop=(c == 1))
                last.then_inc(S["projected"], 1)

            node_blocks(pe, (7, project), (6, turn), (1, values), (0, turn_sum))

        @block.vector
        def _(dve):
            idle = dve.alloc_register("between_idle")

            def bias(b, p):
                landed(dve, S[f"skip_loaded{p}"], b, p)
                nc.vector.scalar_tensor_tensor(y[:, p, :], bv, share[:, bass.ds(b, 1)], y[:, p, :], ALU.mult, ALU.add).then_inc(S["y_bias"], 1)

            def sum_values(b, p):
                use(dve, S["y_bias"], b)
                use(dve, S["valued"], b)
                nc.vector.tensor_tensor(y[:, p, :], y[:, p, :], ps[:, 2 + p % 2, 0:D], ALU.add).then_inc(S["y_sum"], 1)
                use(dve, S["y_sum"], b)
                use(dve, S["x2"], b, 2)
                nc.vector.scalar_tensor_tensor(low[:, p % 2, :], y[:, p, :], 0.0, slope, ALU.min, ALU.mult).then_inc(S["low"], 1)

            def output(b, p):
                use(dve, S["low"], b)
                nc.vector.scalar_tensor_tensor(low[:, p % 2, :], y[:, p, :], 0.0, low[:, p % 2, :], ALU.max, ALU.add).then_inc(S["y"], 1)
                use(dve, S["y"], b)
                landed(dve, S[f"x_loaded{p}"], b, p)
                vacated(dve, S[f"x2_stored{p}"], b, p)
                use(dve, S["hn"], b, U)
                nc.vector.tensor_tensor(x2[:, p, :], x[:, p, :], low[:, p % 2, :], ALU.add).then_inc(S["x2"], 1)

            def stats(b, p):
                use(dve, S["x2"], b)
                layernorm_stats(nc, dve, S, x2[:, p, :], st[:, p, :], b, idle)

            def normalize(b, p):
                use(dve, S["ln_rstd"], b)
                use(dve, S["turned"], b, 2)
                use(dve, S["h"], b, 2)
                nc.vector.tensor_scalar(hn[:, p % 2, :], x2[:, p, :], st[:, p, 6:7], st[:, p, 9:10], ALU.subtract, ALU.mult).then_inc(S["hn"], 1)

            def own_logits(b, p):
                use(dve, S["row"], b)
                nc.vector.tensor_copy(m.self_logit[:, bass.ds(b, 1), :], row[:, p % 2, D:W2].unsqueeze(1)).then_inc(S["self"], 1)

            node_blocks(dve, (8, own_logits), (4, normalize), (3, stats), (2, output), (1, sum_values), (0, bias))
            c = Chain(dve, S["dve"])
            dve.wait_ge(S["self"], NB)
            split3(c, nc, lambda s: tab[:, :, s, :], m.self_logit[:, :, 2 * H2:4 * H2], rest)


def prepare_ffn(nc, m, args, sp_):
    ts = Space(m.tabs[:, :].bitcast(F32))
    w1_t, w2_t, raw1, raw2 = ts.take(2, FFN), ts.take(FFN // P, D), ts.take(FFN // P, D), ts.take(2, FFN)
    b1 = sp_.take(FFN // P)
    vectors = {"bias1": args.bias1, "ln1_g": args.ln1_g, "ln1_b": args.ln1_b, "ln2_g": args.ln2_g, "ln2_b": args.ln2_b, "b2": args.b2}
    rows = {n: sp_.take(D) for n in vectors}
    ps = m.psum
    FC = FFN // P
    with ExitStack() as ctx:
        S = Sems(nc, ctx, "pffn")
        block = ctx.enter_context(nc.Block())

        @block.sync
        def _(sp):
            sp.dma_start(raw1, args.W1.rearrange("(f p) n -> p f n", p=P)).then_inc(S["load"], 16)
            sp.dma_start(raw2, args.W2.rearrange("(c p) n -> p c n", p=P)).then_inc(S["load"], 16)
            sp.dma_start(b1, args.b1.rearrange("(f p) -> p f", p=P), allow_slow_non_contiguous=True).then_inc(S["load"], 16)
            for n, vector in vectors.items():
                sp.dma_start(rows[n], as_row(vector)).then_inc(S["load"], 16)
            sp.wait_ge(S["load"], 16 * (3 + len(vectors)))

        @block.tensor
        def _(pe):
            pe.wait_ge(S["load"], 16 * (3 + len(vectors)))
            for f in range(FC):
                for c in range(2):
                    nc.tensor.transpose(ps[:, 2 * c + f // 4, (f % 4) * P:(f % 4 + 1) * P], raw1[:, f, c * P:(c + 1) * P], m.ident[:, :])
                    last = nc.tensor.transpose(ps[:, 4 + f // 2, (f % 2) * D + c * P:(f % 2) * D + (c + 1) * P], raw2[:, c, f * P:(f + 1) * P], m.ident[:, :])
            last.then_inc(S["turned"], 1)

        @block.vector
        def _(dve):
            dve.wait_ge(S["turned"], 1)
            nc.vector.tensor_copy(w1_t.rearrange("p c (a n) -> p (c a) n", a=2), ps[:, 0:4, :])
            nc.vector.tensor_copy(w2_t.rearrange("p (a f) n -> p a (f n)", a=4), ps[:, 4:8, :]).then_inc(S["done"], 1)
    return w1_t, w2_t, b1, rows


def nodes_ffn(nc, m, args, dram, weights, keep, own, sp_):
    w1_t, w2_t, b1, rows = weights
    FC = FFN // P
    more = Space(m.tabs[:, :].bitcast(F32), 4 * 2 * FFN)
    xs, h1, x2, u, o = (more.take(U, D) for _ in range(5))
    t1, t2, z, uT, v = (more.take(2, D) for _ in range(5))
    g = more.take(2, FC, P)
    st, st2 = sp_.take(U, 10), sp_.take(U, 10)
    ps = m.psum
    with ExitStack() as ctx:
        S = Sems(nc, ctx, "ffn")
        block = ctx.enter_context(nc.Block())

        @block.sync
        def _(sp):
            def load(b, p):
                use(sp, S["own"], b, U)
                sp.dma_start(xs[:, p, :], rows_of(dram.t2, b, D)).then_inc(S[f"xs{p}"], 16)
                use(sp, S["own_sum"], b, U)
                sp.dma_start(h1[:, p, :], rows_of(dram.h1, b)).then_inc(S[f"h{p}"], 16)

            def load_x2(b, p):
                use(sp, S["out"], b, U)
                sp.dma_start(x2[:, p, :], rows_of(dram.x2, b)).then_inc(S[f"x2{p}"], 16)

            node_blocks(sp, (10, load_x2), (0, load))

        @block.gpsimd
        def _(pool):
            def own_rows(b, p):
                landed(pool, S[f"xs{p}"], b, p)
                use(pool, S["z"], b, 2)
                nc.gpsimd.tensor_tensor(by_heads(t2[:, p % 2, :], H2), by_heads(xs[:, p, :], H2), spread(one(own[:, bass.ds(b, 1), :]), D // H2), ALU.mult).then_inc(S["own"], 1)
                use(pool, S["own"], b)
                nc.gpsimd.tensor_tensor(t2[:, p % 2, :], t2[:, p % 2, :], rows["bias1"], ALU.add).then_inc(S["own_bias"], 1)
                use(pool, S["own_bias"], b)
                landed(pool, S[f"h{p}"], b, p)
                nc.gpsimd.tensor_tensor(t2[:, p % 2, :], t2[:, p % 2, :], h1[:, p, :], ALU.add).then_inc(S["own_sum"], 1)

            def root(b, p):
                inverse_root(nc, pool, S, m, st[:, p, :], b, "l1")

            def root2(b, p):
                inverse_root(nc, pool, S, m, st2[:, p, :], b, "l2")

            def finish(b, p):
                use(pool, S["vn"], b)
                nc.gpsimd.tensor_tensor(o[:, p, :], o[:, p, :], rows["ln2_g"], ALU.mult).then_inc(S["out_g"], 1)
                use(pool, S["out_g"], b)
                nc.gpsimd.tensor_tensor(o[:, p, :], o[:, p, :], rows["ln2_b"], ALU.add).then_inc(S["out_b"], 1)
                use(pool, S["out_b"], b)
                landed(pool, S[f"x2{p}"], b, p)
                nc.gpsimd.tensor_tensor(o[:, p, :], o[:, p, :], x2[:, p, :], ALU.add).then_inc(S["out"], 1)

            node_blocks(pool, (7, root2), (2, root), (9, finish), (0, own_rows))

        @block.scalar
        def _(act):
            def turned(b, p):
                use(act, S["turned"], b)
                use(act, S["up"], b, 2)
                nc.scalar.activation(uT[:, p % 2, :], ps[:, p % 2, 0:D], ACT.Copy).then_inc(S["uT"], 1)

            def gelu(b, p):
                use(act, S["up"], b)
                use(act, S["down"], b, 2)
                for f in range(FC):
                    last = nc.scalar.activation(g[:, p % 2, f, :], ps[:, 2 + 2 * (p % 2) + f // 4, (f % 4) * P:(f % 4 + 1) * P], ACT.Gelu, bias=b1[:, f:f + 1])
                last.then_inc(S["gelu"], 1)

            def store(b, p):
                use(act, S["out"], b)
                act.dma_start(rows_of(args.out, b), o[:, p, :]).then_inc(S[f"out_stored{p}"], 16)

            node_blocks(act, (7, store), (1, gelu), (0, turned))
            all_landed(act, S, "out_stored")

        @block.tensor
        def _(pe):
            def turn(b, p):
                use(pe, S["u"], b)
                use(pe, S["uT"], b, 2)
                for c in range(2):
                    last = nc.tensor.transpose(ps[:, p % 2, c * P:(c + 1) * P], u[:, p, c * P:(c + 1) * P], m.ident[:, :])
                last.then_inc(S["turned"], 1)

            def up(b, p):
                use(pe, S["uT"], b)
                use(pe, S["gelu"], b, 2)
                for f in range(FC):
                    for c in range(2):
                        last = nc.tensor.matmul(ps[:, 2 + 2 * (p % 2) + f // 4, (f % 4) * P:(f % 4 + 1) * P], w1_t[:, c, f * P:(f + 1) * P],
                                                uT[:, p % 2, c * P:(c + 1) * P], start=(c == 0), stop=(c == 1))
                last.then_inc(S["up"], 1)

            def down(b, p):
                use(pe, S["gelu"], b)
                use(pe, S["v"], b, 2)
                for f in range(FC):
                    last = nc.tensor.matmul(ps[:, 6 + p % 2, 0:D], g[:, p % 2, f, :], w2_t[:, f, :], start=(f == 0), stop=(f == FC - 1))
                last.then_inc(S["down"], 1)

            node_blocks(pe, (1, up), (0, turn), (2, down))

        @block.vector
        def _(dve):
            idle = dve.alloc_register("ffn_idle")

            def attention(b, p):
                use(dve, S["z"], b, 2)
                nc.vector.tensor_tensor(by_heads(t1[:, p % 2, :], H2), by_heads(acc_rows(m, b, 0, D), H2), spread(one(keep[:, bass.ds(b, 1), :]), D // H2), ALU.mult).then_inc(S["kept"], 1)
                use(dve, S["kept"], b)
                use(dve, S["own_sum"], b)
                use(dve, S["u"], b, 2)
                nc.vector.tensor_tensor(z[:, p % 2, :], t1[:, p % 2, :], t2[:, p % 2, :], ALU.add).then_inc(S["z"], 1)
                use(dve, S["z"], b)
                layernorm_stats(nc, dve, S, z[:, p % 2, :], st[:, p, :], b, idle, "l1")

            def normalize(b, p):
                use(dve, S["l1_rstd"], b)
                nc.vector.tensor_scalar(z[:, p % 2, :], z[:, p % 2, :], st[:, p, 6:7], st[:, p, 9:10], ALU.subtract, ALU.mult).then_inc(S["zn"], 1)
                use(dve, S["zn"], b)
                nc.vector.tensor_tensor(z[:, p % 2, :], z[:, p % 2, :], rows["ln1_g"], ALU.mult).then_inc(S["zg"], 1)
                use(dve, S["zg"], b)
                use(dve, S["turned"], b, U)
                use(dve, S["v_sum"], b, U)
                nc.vector.tensor_tensor(u[:, p, :], z[:, p % 2, :], rows["ln1_b"], ALU.add).then_inc(S["u"], 1)

            def residual(b, p):
                use(dve, S["down"], b)
                use(dve, S["vn"], b, 2)
                nc.vector.tensor_tensor(v[:, p % 2, :], ps[:, 6 + p % 2, 0:D], rows["b2"], ALU.add).then_inc(S["v"], 1)
                use(dve, S["v"], b)
                nc.vector.tensor_tensor(v[:, p % 2, :], v[:, p % 2, :], u[:, p, :], ALU.add).then_inc(S["v_sum"], 1)
                use(dve, S["v_sum"], b)
                layernorm_stats(nc, dve, S, v[:, p % 2, :], st2[:, p, :], b, idle, "l2")

            def output(b, p):
                use(dve, S["l2_rstd"], b)
                vacated(dve, S[f"out_stored{p}"], b, p)
                nc.vector.tensor_scalar(o[:, p, :], v[:, p % 2, :], st2[:, p, 6:7], st2[:, p, 9:10], ALU.subtract, ALU.mult).then_inc(S["vn"], 1)

            node_blocks(dve, (7, output), (5, residual), (2, normalize), (0, attention))


class Held:
    pass


def build_program(nc, x, edges, weights, gat_W, att_src0, att_dst0, gat_bias, prelu1, Wq, bq, Wk, bk, Wv, bv, Wskip, bskip, prelu2,
                  W_src, W_dst, att_src1, att_dst1, bias1, ln1_g, ln1_b, ln2_g, ln2_b, ffn1, b1, ffn2, b2, out):
    args = Held()
    (args.x, args.gat_W, args.att_src0, args.att_dst0, args.gat_bias, args.prelu1) = (x, gat_W, att_src0, att_dst0, gat_bias, prelu1)
    (args.Wq, args.bq, args.Wk, args.bk, args.Wv, args.bv, args.Wskip, args.bskip, args.prelu2) = (Wq, bq, Wk, bk, Wv, bv, Wskip, bskip, prelu2)
    (args.W_src, args.W_dst, args.att_src1, args.att_dst1, args.bias1) = (W_src, W_dst, att_src1, att_dst1, bias1)
    (args.ln1_g, args.ln1_b, args.ln2_g, args.ln2_b, args.W1, args.b1, args.W2, args.b2, args.out) = (ln1_g, ln1_b, ln2_g, ln2_b, ffn1, b1, ffn2, b2, out)
    m, dram = Held(), Held()
    dram.edges, dram.weights = edges, weights
    with ExitStack() as ctx:
        def sb(name, shape, dt=F32):
            return ctx.enter_context(nc.sbuf_tensor(name, shape, dt))

        def dr(name, shape, dt=F32):
            return nc.dram_tensor(name, shape, dt, kind="Internal").ap()

        dram.rel16 = dr("visit_positions", [NV * P], BF16)
        dram.scal = dr("visit_scalars", [4, NV])
        dram.dst_s = dr("visit_dst", [NV // G, HB, G, P])
        dram.rows = dr("batch_rows", [NV // G, 6, G])
        dram.t0 = dr("table_gat", [NP, W0])
        dram.t1 = dr("table_attn", [NP, W1])
        dram.t2 = dr("table_typed", [NP, W2])
        dram.skip = dr("skip_rows", [NP, D])
        dram.x2 = dr("x_after_layer0", [NP, D])
        dram.kept = dr("edge_tables", [P, 4, NV])
        dram.h1 = dr("h_layer1", [NP, D])
        m.arena = sb("arena", [P, 2 * G * W2])
        m.acc = sb("acc", [P, NB * WA])
        m.tabs = sb("tabs", [P, NB * 3 * WQ], BF16)
        m.src_t = sb("src_t", [P, NV], I32)
        m.rel_t, m.mask_t = sb("rel_t", [P, NV]), sb("mask_t", [P, NV])
        rest = Space(m.tabs[:, NB * 3 * 2 * H2:NB * 3 * WQ].bitcast(F32))
        m.last_t, m.type_t, m.type0_t, m.weight_t = (rest.take(NV) for _ in range(4))
        m.self_logit = rest.take(NB, 4 * H2)
        m.blocks = sb("blocks", [1, NV], I32)
        m.iota, m.pcol, m.ident = sb("iota", [P, P]), sb("pcol", [P, 1]), sb("ident", [P, P])
        m.half, m.ones = sb("half", [P, 1]), sb("ones", [P, 1])
        m.ints, m.ints2 = sb("ints", [P, G + HB], I32), sb("ints2", [P, G + HB], I32)
        m.ints_t, m.ints_t2 = sb("ints_t", [HB, P], I32), sb("ints_t2", [HB, P], I32)
        m.visit_col, m.head_rows, m.head_rows_t = sb("visit_col", [P, G]), sb("head_rows", [P, HB]), sb("head_rows_t", [HB, P])
        m.head_int = sb("head_int", [P, 2 * HB], I32)
        m.rel_row = sb("rel_row", [P, 2, G * P], BF16)
        m.onehot_t = sb("onehot_t", [P, G, P], BF16)
        m.onehot, m.dist = sb("onehot", [P, 4, P]), sb("dist", [P, 4, P])
        m.dst_s, m.rows = sb("dst_s", [P, 2, P]), sb("rows", [HB, 2, 6 * G])
        m.seg_bias, m.seg_max, m.seg_tmp = sb("seg_bias", [P, 1, P + 1]), sb("seg_max", [P, 3, P]), sb("seg_tmp", [P, 3, P])
        m.ends, m.end_max = sb("ends", [P, 2, G]), sb("end_max", [P, 2])
        m.fore_max, m.back_max = sb("fore_max", [HB, 2, G + 1]), sb("back_max", [HB, 1, G + 1])
        m.joined, m.join_tmp = sb("joined", [HB, 2, G]), sb("join_tmp", [HB, 3, G])
        m.first_hot, m.growth, m.shrink = sb("first_hot", [HB, P]), sb("growth", [HB, HB]), sb("shrink", [P, HB])
        m.raw, m.logit, m.shifted = sb("raw", [P, P]), sb("logit", [P, P]), sb("shifted", [P, P])
        m.both, m.edge_scale = sb("both", [P, G, 2 * HB]), sb("edge_scale", [P, G, HB])
        m.weight, m.neg_weight = sb("weight", [P, 2, G]), sb("neg_weight", [P, 2, G])
        m.junk = sb("junk", [P, 2, WQ])
        m.idx = sb("idx", [P, 2, G], I32)
        m.psum = ctx.enter_context(nc.psum_tensor("psum", [P, 8, 512], F32))

        constants(nc, m)
        visits(nc, m, dram)
        space = Space(m.arena)
        w = prepare_gat(nc, m, args, space)
        nodes_in(nc, m, args, dram, w, space)
        edge_pass(nc, m, dram, Phase(m, "gat", H0, dram.t0, W0, W0, H0, 5))
        space = Space(m.arena)
        keep, own = head_factors(nc, m, dram, H0, 0, H0, 1e-16, space, "fgat")
        w = prepare_attn(nc, m, args, space)
        nodes_mid(nc, m, dram, w, keep, own, space)
        edge_pass(nc, m, dram, Phase(m, "attn", 1, dram.t1, W1, WQ, WQ, 5))
        space = Space(m.arena)
        w = prepare_typed(nc, m, args, dram, space)
        nodes_between(nc, m, args, dram, w, space)
        edge_pass(nc, m, dram, Phase(m, "typed", H2, dram.t2, W2, WA, 2 * H2, 5))
        space = Space(m.arena)
        keep, own = head_factors(nc, m, dram, H2, 0, 2 * H2, 0.0, space, "ftyped")
        w = prepare_ffn(nc, m, args, space)
        nodes_ffn(nc, m, args, dram, w, keep, own, space)


_INS = ["x", "edges", "weights", "L0_gnn_gat_W", "L0_gnn_att_src", "L0_gnn_att_dst", "L0_gnn_gat_bias", "L0_gnn_prelu1_a",
        "L0_gnn_Wq", "L0_gnn_bq", "L0_gnn_Wk", "L0_gnn_bk", "L0_gnn_Wv", "L0_gnn_bv", "L0_gnn_Wskip", "L0_gnn_bskip",
        "L0_gnn_prelu2_a", "L1_gnn_W_src", "L1_gnn_W_dst", "L1_gnn_att_src", "L1_gnn_att_dst", "L1_gnn_bias", "L1_gnn_ln1_g",
        "L1_gnn_ln1_b", "L1_gnn_ln2_g", "L1_gnn_ln2_b", "L1_gnn_ffn_W1", "L1_gnn_ffn_b1", "L1_gnn_ffn_W2", "L1_gnn_ffn_b2"]


def kernel(**inputs):
    import numpy as _np
    import concourse.bacc as _bacc
    from concourse import mybir as _mybir
    from concourse.bass_utils import run_bass_kernel_spmd as _run

    def tiled(a, fill):
        return _np.concatenate([a, _np.full((NT + 1) * P - a.shape[0], fill, a.dtype)]).reshape(NT + 1, P)

    given = {k: _np.ascontiguousarray(v) for k, v in inputs.items()}
    dst = given["dst"]
    given["edges"] = _np.stack([tiled(given["src"], 0), tiled(dst, PAD_NODE), tiled(dst[1:], PAD_NODE),
                                tiled(given["edge_type_2"], 0)], axis=1).reshape(NT + 1, 4 * P)
    given["weights"] = tiled(given["edge_weight"], 0)
    given["x"] = _np.concatenate([given["x"], _np.zeros((NP - N, D), given["x"].dtype)])

    nc = _bacc.Bacc("TRN2", target_bir_lowering=False, num_devices=1)
    arrays, args = {}, []
    for name in _INS:
        a = _np.ascontiguousarray(given[name])
        arrays[f"in_{name}_dram"] = a
        args.append(nc.dram_tensor(f"in_{name}_dram", a.shape, _mybir.dt.from_np(a.dtype), kind="ExternalInput").ap())
    args.append(nc.dram_tensor("out_0_dram", (NP, D), _mybir.dt.float32, kind="ExternalOutput").ap())
    build_program(nc, *args)
    r = _run(nc, [arrays], core_ids=[0])
    return r.results[0]["out_0_dram"][:N]
```
